# Optimizing a Trainium2 kernel written in Bass

```python
import numpy as np
import jax
import jax.numpy as jnp

def _softmax(x, axis=-1):
    return jax.nn.softmax(x, axis=axis)

def _gelu(x):
    return jax.nn.gelu(x, approximate=True)

def _silu(x):
    return jax.nn.silu(x)

def _sigmoid(x):
    return jax.nn.sigmoid(x)

def _layernorm(x, axis=-1, eps=1e-05):
    m = jnp.mean(x, axis=axis, keepdims=True)
    v = jnp.var(x, axis=axis, keepdims=True)
    return (x - m) / jnp.sqrt(v + eps)

def _scatter_add(tgt, idx, src, axis=0):
    return tgt.at[idx].add(src)

def _segment_sum(src, seg, n):
    return jax.ops.segment_sum(src, seg, n)
kernel_name = 'mk_perceiver_d1_seqx_r4_7af662'

def setup_inputs(seed: int=0):
    np.random.seed(seed)
    _w = jnp.asarray

    def _rec_inputs():
        import jax
        import jax.numpy as jnp
        _rk = jax.random.key(seed)
        x = -0.0002928 + 1 * jax.random.normal(jax.random.fold_in(_rk, 1), (64, 32, 256), jnp.float32)
        _lenS = 32 - jax.random.randint(jax.random.fold_in(_rk, 7), (64,), 0, max(1, 32 // 4) + 1, jnp.int32)
        _lenS2 = 257 - jax.random.randint(jax.random.fold_in(_rk, 8), (64,), 0, max(1, 257 // 4) + 1, jnp.int32)
        _ctx_1024P = jax.random.normal(jax.random.fold_in(_rk, 11), (64, 16, 256), jnp.float32)
        _ctx_1024c = jax.random.dirichlet(jax.random.fold_in(_rk, 511), 0.3 * jnp.ones((16,), jnp.float32), (64, 257))
        _ctx_1024t = jnp.einsum('bsk,bkd->bsd', _ctx_1024c, _ctx_1024P)
        _ctx_1024t = _ctx_1024t * jax.lax.rsqrt(jnp.mean(jnp.square(_ctx_1024t)) + 1e-12) * 0.953939
        ctx_1024 = -1.39393e-06 + 0.999914 * (_ctx_1024t + 0.3 * jax.random.normal(jax.random.fold_in(_rk, 611), (64, 257, 256), jnp.float32))
        return (x, ctx_1024)
    x, ctx_1024 = _rec_inputs()

    def _L0_xattn_setup():
        import jax, jax.numpy as jnp
        import numpy as np
        DIM = 256
        NUM_HEADS = 16
        HEAD_DIM = DIM // NUM_HEADS
        key = jax.random.key(seed)
        ks = jax.random.split(key, 11)
        B, N, C = (2, 512, DIM)
        s = 1.0 / np.sqrt(C)
        inp = {'q': jax.random.normal(ks[0], (B, N, C), jnp.float32), 'k': jax.random.normal(ks[1], (B, N, C), jnp.float32), 'v': jax.random.normal(ks[2], (B, N, C), jnp.float32), 'Wq': jax.random.normal(ks[3], (C, C), jnp.float32) * s, 'bq': jnp.zeros((C,), jnp.float32), 'Wk': jax.random.normal(ks[4], (C, C), jnp.float32) * s, 'bk': jnp.zeros((C,), jnp.float32), 'Wv': jax.random.normal(ks[5], (C, C), jnp.float32) * s, 'bv': jnp.zeros((C,), jnp.float32), 'Wo': jax.random.normal(ks[6], (C, C), jnp.float32) * s, 'bo': jnp.zeros((C,), jnp.float32)}
        return inp
    _L0_xattn_all = _L0_xattn_setup()
    _L0_xattn_in = {k: v for k, v in _L0_xattn_all.items() if k in ('Wq', 'bq', 'Wk', 'bk', 'Wv', 'bv', 'Wo', 'bo')}
    del _L0_xattn_all

    def _L0_attn_setup():
        import jax, jax.numpy as jnp
        import numpy as np
        B, T, C, I = (4, 1024, 256, 1024)

        def rmsnorm(x, w, eps=1e-06):
            return x * jax.lax.rsqrt(jnp.mean(x * x, axis=-1, keepdims=True) + eps) * w

        def shift(h):
            return jnp.pad(h, ((0, 0), (1, 0), (0, 0)))[:, :-1]

        def wkv_scan(k, v, w, u):
            ew = jnp.exp(jnp.clip(w, -20.0, 20.0))

            def step(carry, kv):
                a, b = carry
                kt, vt = kv
                ekt = jnp.exp(jnp.clip(u + kt, -20.0, 20.0))
                out = (a + ekt * vt) / (b + ekt + 1e-08)
                ek = jnp.exp(jnp.clip(kt, -20.0, 20.0))
                return ((ew * a + ek * vt, ew * b + ek), out)
            init = (jnp.zeros((k.shape[0], k.shape[2]), jnp.float32), jnp.zeros((k.shape[0], k.shape[2]), jnp.float32))
            _, out = jax.lax.scan(step, init, (k.swapaxes(0, 1), v.swapaxes(0, 1)))
            return out.swapaxes(0, 1)
        key = jax.random.key(seed)
        ks = jax.random.split(key, 16)
        s = 1.0 / np.sqrt(C)
        si = 1.0 / np.sqrt(I)
        return {'x': jax.random.normal(ks[0], (B, T, C), jnp.float32), 'ln1_w': jnp.ones((C,), jnp.float32), 'ln2_w': jnp.ones((C,), jnp.float32), 'time_decay': jax.random.normal(ks[1], (C,), jnp.float32) * 0.1 - 5.0, 'time_first': jax.random.normal(ks[2], (C,), jnp.float32) * 0.01, 'time_mix_k': jnp.full((C,), 0.5, jnp.float32), 'time_mix_v': jnp.full((C,), 0.5, jnp.float32), 'time_mix_r': jnp.full((C,), 0.5, jnp.float32), 'W_key': jax.random.normal(ks[3], (C, C), jnp.float32) * s, 'W_value': jax.random.normal(ks[4], (C, C), jnp.float32) * s, 'W_recept': jax.random.normal(ks[5], (C, C), jnp.float32) * s, 'W_out': jax.random.normal(ks[6], (C, C), jnp.float32) * s, 'time_mix_k2': jnp.full((C,), 0.5, jnp.float32), 'time_mix_r2': jnp.full((C,), 0.5, jnp.float32), 'W_key2': jax.random.normal(ks[7], (C, I), jnp.float32) * s, 'W_value2': jax.random.normal(ks[8], (I, C), jnp.float32) * si, 'W_recept2': jax.random.normal(ks[9], (C, C), jnp.float32) * s}
    _L0_attn_all = _L0_attn_setup()
    _L0_attn_in = {k: v for k, v in _L0_attn_all.items() if k in ('ln1_w', 'ln2_w', 'time_decay', 'time_first', 'time_mix_k', 'time_mix_v', 'time_mix_r', 'W_key', 'W_value', 'W_recept', 'W_out', 'time_mix_k2', 'time_mix_r2', 'W_key2', 'W_value2', 'W_recept2')}
    del _L0_attn_all

    def _L0_ffn_setup():
        import jax, jax.numpy as jnp
        import numpy as np
        D_MODEL = 256
        N_EXPERTS = 8
        TOP_K = 2
        FFN_HIDDEN = 4 * D_MODEL
        key = jax.random.key(seed)
        ks = jax.random.split(key, 6)

        def xavier(k, shape):
            fan_in, fan_out = (shape[-2], shape[-1])
            lim = jnp.sqrt(6.0 / (fan_in + fan_out))
            return jax.random.uniform(k, shape, jnp.float32, -lim, lim)
        x = jax.random.normal(ks[0], (4, 512, D_MODEL), jnp.float32)
        w_gate = xavier(ks[1], (N_EXPERTS, D_MODEL))
        W1 = xavier(ks[2], (N_EXPERTS, D_MODEL, FFN_HIDDEN))
        b1 = jnp.zeros((N_EXPERTS, FFN_HIDDEN), jnp.float32)
        W2 = xavier(ks[3], (N_EXPERTS, FFN_HIDDEN, D_MODEL))
        b2 = jnp.zeros((N_EXPERTS, D_MODEL), jnp.float32)
        return {'x': x, 'w_gate': w_gate, 'W1': W1, 'b1': b1, 'W2': W2, 'b2': b2}
    _L0_ffn_all = _L0_ffn_setup()
    _L0_ffn_in = {k: v for k, v in _L0_ffn_all.items() if k in ('w_gate', 'W1', 'b1', 'W2', 'b2')}
    del _L0_ffn_all
    return {'x': x, 'ctx_1024': ctx_1024, 'L0_xattn_Wq': _L0_xattn_in['Wq'], 'L0_xattn_bq': _L0_xattn_in['bq'], 'L0_xattn_Wk': _L0_xattn_in['Wk'], 'L0_xattn_bk': _L0_xattn_in['bk'], 'L0_xattn_Wv': _L0_xattn_in['Wv'], 'L0_xattn_bv': _L0_xattn_in['bv'], 'L0_xattn_Wo': _L0_xattn_in['Wo'], 'L0_xattn_bo': _L0_xattn_in['bo'], 'L0_attn_ln1_w': _L0_attn_in['ln1_w'], 'L0_attn_ln2_w': _L0_attn_in['ln2_w'], 'L0_attn_time_decay': _L0_attn_in['time_decay'], 'L0_attn_time_first': _L0_attn_in['time_first'], 'L0_attn_time_mix_k': _L0_attn_in['time_mix_k'], 'L0_attn_time_mix_v': _L0_attn_in['time_mix_v'], 'L0_attn_time_mix_r': _L0_attn_in['time_mix_r'], 'L0_attn_W_key': _L0_attn_in['W_key'], 'L0_attn_W_value': _L0_attn_in['W_value'], 'L0_attn_W_recept': _L0_attn_in['W_recept'], 'L0_attn_W_out': _L0_attn_in['W_out'], 'L0_attn_time_mix_k2': _L0_attn_in['time_mix_k2'], 'L0_attn_time_mix_r2': _L0_attn_in['time_mix_r2'], 'L0_attn_W_key2': _L0_attn_in['W_key2'], 'L0_attn_W_value2': _L0_attn_in['W_value2'], 'L0_attn_W_recept2': _L0_attn_in['W_recept2'], 'L0_ffn_w_gate': _L0_ffn_in['w_gate'], 'L0_ffn_W1': _L0_ffn_in['W1'], 'L0_ffn_b1': _L0_ffn_in['b1'], 'L0_ffn_W2': _L0_ffn_in['W2'], 'L0_ffn_b2': _L0_ffn_in['b2']}

def reference(x, ctx_1024, L0_xattn_Wq, L0_xattn_bq, L0_xattn_Wk, L0_xattn_bk, L0_xattn_Wv, L0_xattn_bv, L0_xattn_Wo, L0_xattn_bo, L0_attn_ln1_w, L0_attn_ln2_w, L0_attn_time_decay, L0_attn_time_first, L0_attn_time_mix_k, L0_attn_time_mix_v, L0_attn_time_mix_r, L0_attn_W_key, L0_attn_W_value, L0_attn_W_recept, L0_attn_W_out, L0_attn_time_mix_k2, L0_attn_time_mix_r2, L0_attn_W_key2, L0_attn_W_value2, L0_attn_W_recept2, L0_ffn_w_gate, L0_ffn_W1, L0_ffn_b1, L0_ffn_W2, L0_ffn_b2):
    import jax
    import jax.numpy as jnp

    def _L0_xattn_ref(q, k, v, Wq, bq, Wk, bk, Wv, bv, Wo, bo):
        import jax, jax.numpy as jnp
        import numpy as np
        DIM = 256
        NUM_HEADS = 16
        HEAD_DIM = DIM // NUM_HEADS
        B, Nq, C = q.shape
        Nkv = k.shape[1]
        H, D = (NUM_HEADS, HEAD_DIM)
        qh = (q @ Wq.T + bq).reshape(B, Nq, H, D).transpose(0, 2, 1, 3)
        kh = (k @ Wk.T + bk).reshape(B, Nkv, H, D).transpose(0, 2, 1, 3)
        vh = (v @ Wv.T + bv).reshape(B, Nkv, H, D).transpose(0, 2, 1, 3)
        scale = D ** (-0.5)
        attn = jax.nn.softmax(jnp.einsum('bhqd,bhkd->bhqk', qh, kh) * scale, axis=-1)
        out = jnp.einsum('bhqk,bhkd->bhqd', attn, vh)
        out = out.transpose(0, 2, 1, 3).reshape(B, Nq, C)
        return out @ Wo.T + bo

    def _L0_attn_ref(x, ln1_w, ln2_w, time_decay, time_first, time_mix_k, time_mix_v, time_mix_r, W_key, W_value, W_recept, W_out, time_mix_k2, time_mix_r2, W_key2, W_value2, W_recept2):
        import jax, jax.numpy as jnp
        import numpy as np
        B, T, C, I = (4, 1024, 256, 1024)

        def rmsnorm(x, w, eps=1e-06):
            return x * jax.lax.rsqrt(jnp.mean(x * x, axis=-1, keepdims=True) + eps) * w

        def shift(h):
            return jnp.pad(h, ((0, 0), (1, 0), (0, 0)))[:, :-1]

        def wkv_scan(k, v, w, u):
            ew = jnp.exp(jnp.clip(w, -20.0, 20.0))

            def step(carry, kv):
                a, b = carry
                kt, vt = kv
                ekt = jnp.exp(jnp.clip(u + kt, -20.0, 20.0))
                out = (a + ekt * vt) / (b + ekt + 1e-08)
                ek = jnp.exp(jnp.clip(kt, -20.0, 20.0))
                return ((ew * a + ek * vt, ew * b + ek), out)
            init = (jnp.zeros((k.shape[0], k.shape[2]), jnp.float32), jnp.zeros((k.shape[0], k.shape[2]), jnp.float32))
            _, out = jax.lax.scan(step, init, (k.swapaxes(0, 1), v.swapaxes(0, 1)))
            return out.swapaxes(0, 1)
        h = rmsnorm(x, ln1_w)
        sh = shift(h)
        xk = h * time_mix_k + sh * (1 - time_mix_k)
        xv = h * time_mix_v + sh * (1 - time_mix_v)
        xr = h * time_mix_r + sh * (1 - time_mix_r)
        k = xk @ W_key
        v = xv @ W_value
        r = jax.nn.sigmoid(xr @ W_recept)
        w = -jnp.exp(time_decay)
        u = time_first
        wkv = wkv_scan(k.astype(jnp.float32), v.astype(jnp.float32), w, u).astype(x.dtype)
        x = x + r * wkv @ W_out
        h = rmsnorm(x, ln2_w)
        sh = shift(h)
        xk = h * time_mix_k2 + sh * (1 - time_mix_k2)
        xr = h * time_mix_r2 + sh * (1 - time_mix_r2)
        k2 = jnp.square(jax.nn.relu(xk @ W_key2))
        r2 = jax.nn.sigmoid(xr @ W_recept2)
        return x + r2 * (k2 @ W_value2)

    def _L0_ffn_ref(x, w_gate, W1, b1, W2, b2):
        import jax, jax.numpy as jnp
        import numpy as np
        D_MODEL = 256
        N_EXPERTS = 8
        TOP_K = 2
        FFN_HIDDEN = 4 * D_MODEL
        B, S, D = x.shape
        flat_x = x.reshape(-1, D)
        gate = jax.nn.softmax(flat_x @ w_gate.T, axis=-1)
        topk_scores, topk_idx = jax.lax.top_k(gate, TOP_K)
        cw = (jax.nn.one_hot(topk_idx, N_EXPERTS, dtype=flat_x.dtype) * topk_scores[..., None]).sum(axis=1)
        h = jax.nn.gelu(jnp.einsum('td,edh->teh', flat_x, W1) + b1, approximate=False)
        y = jnp.einsum('teh,ehd->ted', h, W2) + b2
        out = jnp.einsum('ted,te->td', y, cw)
        return out.reshape(B, S, D)
    x = x + _L0_xattn_ref(_layernorm(x, axis=-1), ctx_1024, ctx_1024, L0_xattn_Wq, L0_xattn_bq, L0_xattn_Wk, L0_xattn_bk, L0_xattn_Wv, L0_xattn_bv, L0_xattn_Wo, L0_xattn_bo)
    x = x + _L0_attn_ref(_layernorm(x, axis=-1), L0_attn_ln1_w, L0_attn_ln2_w, L0_attn_time_decay, L0_attn_time_first, L0_attn_time_mix_k, L0_attn_time_mix_v, L0_attn_time_mix_r, L0_attn_W_key, L0_attn_W_value, L0_attn_W_recept, L0_attn_W_out, L0_attn_time_mix_k2, L0_attn_time_mix_r2, L0_attn_W_key2, L0_attn_W_value2, L0_attn_W_recept2)
    x = x + _L0_ffn_ref(_layernorm(x, axis=-1), L0_ffn_w_gate, L0_ffn_W1, L0_ffn_b1, L0_ffn_W2, L0_ffn_b2)
    return x

_drawn_inputs = setup_inputs


def setup_inputs(seed=0):
    import zlib

    import numpy as np

    out = dict(_drawn_inputs(seed))
    spreads = {'L0_xattn_bq': (0.0, 0.354),
     'L0_xattn_bk': (0.0, 2.0),
     'L0_xattn_bv': (0.0, 0.1),
     'L0_xattn_bo': (0.0, 0.1),
     'L0_attn_ln1_w': (1.0, 0.2),
     'L0_attn_ln2_w': (1.0, 0.2),
     'L0_attn_time_mix_k': (0.5, 0.6),
     'L0_attn_time_mix_v': (0.5, 0.6),
     'L0_attn_time_mix_r': (0.5, 0.6),
     'L0_attn_time_mix_k2': (0.5, 0.2),
     'L0_attn_time_mix_r2': (0.5, 0.6),
     'L0_ffn_b1': (0.0, 0.403),
     'L0_ffn_b2': (0.0, 0.326)}
    factors = {'L0_attn_time_decay': 8.0, 'L0_attn_time_first': 200.0}
    for name, (base, spread) in spreads.items():
        noise = np.random.default_rng([zlib.crc32(name.encode()), seed]).standard_normal(out[name].shape)
        drawn = base * np.exp(spread * noise) if base else spread * noise
        out[name] = jnp.asarray(drawn.astype(out[name].dtype))
    for name, factor in factors.items():
        out[name] = (out[name] * factor).astype(out[name].dtype)
    return out
```

```python
import concourse.bass as bass
from concourse import mybir
from contextlib import ExitStack

F32 = mybir.dt.float32
F16 = mybir.dt.float16
ALU = mybir.AluOpType
ACT = mybir.ActivationFunctionType
AX = mybir.AxisListType

NB, SQ, SK, D = 64, 32, 257, 256
NH, HD = 16, 16
P = 128
TOK = NB * SQ
NT = TOK // P
BT = P // SQ
KC = D // P
FF, NE = 1024, 8
FC = FF // P
CT = 4
CN = CT * P
NC = NT // CT
CB = CN // SQ
HI, LO = 0, 1
PASSES = ((HI, HI), (HI, LO), (LO, HI))

WS = 64.0
PS_LN = 8.317766166719343
SM = HD ** -0.5 / (WS * WS)

WQ, WK, WV, WO, WTK, WTV, WTR, WTO, WR2, WK2, WG = (0, 256, 512, 768, 1024, 1280, 1536, 1792, 2048, 2304, 3328)
NW = WG + NE
NWA = WTK
BQ, BK, BV, LN1, LN2, TD, TF, MK, MV, MR, MK2, MR2 = range(12)
NV = 12


class Trail:

    def __init__(self, eng, sem, wait=None):
        self.eng, self.sem, self.base, self.k = eng, sem, 0, 0
        self.wait = wait or (lambda eng, sem, n: eng.wait_ge(sem, n))

    def mark(self, ins):
        ins.then_inc(self.sem, 1)
        self.k += 1
        return self.base + self.k

    def link(self, ins):
        self.wait(self.eng, self.sem, self.mark(ins))

    def enter(self, i, per):
        self.outer, self.per = self.base + self.k, per
        self.base, self.k = self.outer + i * per, 0

    def leave(self, times):
        assert self.k == self.per, f"{self.k} steps of {self.sem}, not {self.per}"
        self.base, self.k = self.outer + times * self.per, 0

ARENA = 212800 // 4
DVE_RWKV = 54


def need(eng, sem, n):
    if not (isinstance(n, int) and n <= 0):
        eng.wait_ge(sem, n)


def perceiver_layer(nc, x, ctx_t, ctx_last, w_all, w_value2, vecs, bo, w1, b1, w2, b2, out):
    stack = ExitStack()
    with stack:
        def sem(name):
            return stack.enter_context(nc.semaphore(name))

        arena = stack.enter_context(nc.sbuf_tensor("arena", [P, ARENA], F32))
        PS = stack.enter_context(nc.psum_tensor("PS", [P, 8, 512], F32))
        at = {}

        def place(name, off, shape, dt=F32):
            n = 1
            for s in shape:
                n *= s
            size = n * (4 if dt == F32 else 2)
            size = (size + 31) // 32 * 32
            assert off % 4 == 0 and off + size <= ARENA * 4, (name, off, size)
            flat = arena[:, off // 4:(off + size) // 4]
            if dt != F32:
                flat = flat.bitcast(dt)
            flat = flat[:, 0:n]
            at[name] = off + size
            if len(shape) == 1:
                return flat
            names = " ".join(f"d{i}" for i in range(len(shape)))
            return flat.rearrange(f"p ({names}) -> p {names}", **{f"d{i}": s for i, s in enumerate(shape)})

        W16 = place("W16", 0, [KC, 2, NW], F16)
        WV2 = place("WV2", at["W16"], [FC, 2, D], F16)
        x_all = place("x_all", at["WV2"], [NT, D])
        vec = place("vec", at["x_all"], [NV, KC])
        vec64 = place("vec64", at["vec"], [NV, KC])
        ident = place("ident", at["vec64"], [P])
        ident16 = place("ident16", at["ident"], [P], F16)
        neghalf = place("neghalf", at["ident16"], [NT])
        aoT = place("aoT", at["neghalf"], [KC, 2, TOK], F16)
        A0 = at["aoT"]
        qT = place("qT", A0, [KC, 2, TOK], F16)
        vlast = place("vlast", at["qT"], [NT, 2, D], F16)
        ctxf = place("ctxf", at["vlast"], [BT, KC, SK])
        ctx16 = place("ctx16", at["ctxf"], [2, KC, 2, SK + 1], F16)
        Kt = place("Kt", at["ctx16"], [2, 2, 2, SK + 1], F16)
        Vt = place("Vt", at["Kt"], [BT, 2, 2, D], F16)
        Pr = place("Pr", at["Vt"], [2, 2, SK])
        PT = place("PT", at["Pr"], [2, 4 * P], F16)
        PTl = place("PTl", at["PT"], [2, P], F16)
        plast = place("plast", at["PTl"], [2, BT, 2, BT])
        Qbd = place("Qbd", at["plast"], [2, 4, 2, 8 * SQ], F16)
        vlc = place("vlc", at["Qbd"], [2, 2, D], F16)
        Om = place("Om", at["vlc"], [2, P])
        Om16 = place("Om16", at["Om"], [4, 2, P], F16)
        aoF = place("aoF", at["Om16"], [KC, P])
        nm = place("nm", at["aoF"], [2, 2])
        nb = place("nb", at["nm"], [2, 2])
        den = place("den", at["nb"], [2, 2])
        rec = place("rec", at["den"], [2, 2])
        mask8 = place("mask8", at["rec"], [8])
        maskO = place("maskO", at["mask8"], [4, HD])
        maskV = place("maskV", at["maskO"], [2, 2, 64])
        sel16 = place("sel16", at["maskV"], [SQ], F16)
        S0 = at["sel16"]
        stage = place("stage", S0, [KC, NW])
        stage2 = place("stage2", at["stage"], [FC, D])
        xn = place("xn", at["stage2"], [2, CT, D])
        xT = place("xT", at["xn"], [2, KC, 2, CN], F16)
        clf = place("clf", at["xT"], [KC, NT, 8])
        cl16 = place("cl16", at["clf"], [KC, 2, NT, 8], F16)
        vlf = place("vlf", at["cl16"], [2, 2, D])
        bo_bc = place("bo_bc", at["vlf"], [D])
        st0 = place("st0", at["bo_bc"], [NT, 6])
        mv0 = place("mv0", at["st0"], [NT, 2])
        ve0 = place("ve0", at["mv0"], [NT])
        rs0 = place("rs0", at["ve0"], [NT])

        vecs_in, wa_in, wb_in, bo_in, cl_in = sem("vecs_in"), sem("wa_in"), sem("wb_in"), sem("bo_in"), sem("cl_in")
        x_in = [sem(f"x_in{c}") for c in range(NC)]
        ctx_in = [sem(f"ctx_in{b}") for b in range(BT)]
        consts, wa_ready, wb_ready = sem("consts"), sem("wa_ready"), sem("wb_ready")
        var_ready, rstd_ready, xn_ready = sem("var_ready"), sem("rstd_ready"), sem("xn_ready")
        xt_ps, xt_hi, xt_split = sem("xt_ps"), sem("xt_hi"), sem("xt_split")
        q_ps, q_hi, q_split = sem("q_ps"), sem("q_hi"), sem("q_split")
        cl_split, vl_ps, vl_evac, vl_split = sem("cl_split"), sem("vl_ps"), sem("vl_evac"), sem("vl_split")
        ctx_split = sem("ctx_split")
        k_ps, k_hi, k_split = sem("k_ps"), sem("k_hi"), sem("k_split")
        v_ps, v_hi, v_split = sem("v_ps"), sem("v_hi"), sem("v_split")
        qbd, vl_now, scores, negmax, probs, p_last = sem("qbd"), sem("vl_now"), sem("scores"), sem("negmax"), sem("probs"), sem("p_last")
        pt_ps, pt_hi, pt_split, pv = sem("pt_ps"), sem("pt_hi"), sem("pt_split"), sem("pv")
        o_masked, o_split, selected, ao_evac, ao_split = sem("o_masked"), sem("o_split"), sem("selected"), sem("ao_evac"), sem("ao_split")
        xbo_ready = sem("xbo_ready")
        dve_step, act_step, pool_step = sem("dve_step"), sem("act_step"), sem("pool_step")

        wait_value = {}

        def wait_apart(eng, sem, n):
            if not isinstance(n, int):
                if eng not in wait_value:
                    wait_value[eng] = eng.alloc_register("wait_value")
                eng.reg_mov(wait_value[eng], n)
                n = wait_value[eng]
                eng.wait_ge(consts, 1)
            eng.wait_ge(sem, n)


        hT = place("hT", A0, [KC, CB, SQ + 1])
        h2T = place("h2T", at["hT"], [KC, CB, SQ + 1])
        dT = place("dT", at["h2T"], [KC, CN])
        d2T = place("d2T", at["dT"], [KC, CN])
        xl = place("xl", at["d2T"], [CT, D])
        hN = place("hN", at["xl"], [CT, D])
        h2N = place("h2N", at["hN"], [CT, D])
        mixf = place("mixf", at["h2N"], [2, CN])
        mix2f = place("mix2f", at["mixf"], [2, CN])
        mix16 = place("mix16", at["mix2f"], [3, KC, 2, CN], F16)
        mix216 = place("mix216", at["mix16"], [2, KC, 2, CN], F16)
        ek = place("ek", at["mix216"], [KC, CN])
        eu = place("eu", at["ek"], [KC, CN])
        vS = place("vS", at["eu"], [KC, CN])
        rS = place("rS", at["vS"], [KC, CN])
        ekp = place("ekp", at["rS"], [KC, CB, SQ + 1])
        ekvp = place("ekvp", at["ekp"], [KC, CB, SQ + 1])
        num = place("num", at["ekvp"], [2, CB, SQ + 1])
        dnm = place("dnm", at["num"], [2, CB, SQ + 1])
        euv = place("euv", at["dnm"], [2, CN])
        top = place("top", at["euv"], [2, CN])
        bot = place("bot", at["top"], [2, CN])
        rw16 = place("rw16", at["bot"], [KC, 2, CN], F16)
        yN = hN
        r2N = place("r2N", at["rw16"], [CT, D])
        reluf = place("reluf", at["r2N"], [2, CN])
        sqf = place("sqf", at["reluf"], [2, CN])
        k216 = place("k216", at["sqf"], [FC, 2, CN], F16)
        zN = d2T.rearrange("p k n -> p (k n)").rearrange("p (t n) -> p t n", t=CT)
        decay = place("decay", at["k216"], [KC, CB, SQ + 1])
        ew = place("ew", at["decay"], [2, KC])
        st1 = place("st1", at["ew"], [CT, 6])
        mv1 = place("mv1", at["st1"], [CT, 2])
        ve1 = place("ve1", at["mv1"], [2, CT])
        rs1 = place("rs1", at["ve1"], [2, CT])
        nmc = place("nmc", at["rs1"], [CT])
        st2 = place("st2", at["nmc"], [CT, 6])
        mv2 = place("mv2", at["st2"], [CT, 2])
        ve2 = place("ve2", at["mv2"], [CT])
        rs2 = place("rs2", at["ve2"], [CT])
        st3 = place("st3", at["rs2"], [CT, 6])
        mv3 = place("mv3", at["st3"], [CT, 2])
        ve3 = place("ve3", at["mv3"], [CT])
        rs3 = place("rs3", at["ve3"], [CT])
        logits = place("logits", at["rs3"], [NT, NE])
        xn3 = hN2 = zN
        x3T = aoT

        (c_ew, wo_ps, tm_x, tm_var, tm_rs, tm_norm, h_ps, h_t, d_t, mixed, mix_hi, mix_lo, kvr_ps, kvr_out, eu_v, rwf, rw_hi, rw_lo,
         wout_ps, y_var, y_rs, y_done, h2_n, h2_ps, h2_t, d2_t, mixed2, mix2_hi, mix2_lo, key_ps, relu_out, sq_out, k2_hi, k2_lo, r2_ps, r2_out,
         val_ps, z_out, x2_var, x2_rs, xn3_done, x3_ps, x3_hi, x3_lo, lg_ps, lg_out) = [sem(n) for n in (
            "c_ew wo_ps tm_x tm_var tm_rs tm_norm h_ps h_t d_t mixed mix_hi mix_lo kvr_ps kvr_out eu_v rwf rw_hi rw_lo "
            "wout_ps y_var y_rs y_done h2_n h2_ps h2_t d2_t mixed2 mix2_hi mix2_lo key_ps relu_out sq_out k2_hi k2_lo r2_ps r2_out "
            "val_ps z_out x2_var x2_rs xn3_done x3_ps x3_hi x3_lo lg_ps lg_out").split()]

        def chunk_steps(eng, step, trail=None, per=0):
            step(0, True, False)
            with eng.Fori(1, NC) as s:
                if trail:
                    trail.enter(s - 1, per)
                step(s, True, True)
            if trail:
                trail.leave(NC - 1)
            step(NC, False, True)

        def tiles_of(s, i, n):
            return x_all[:, bass.ds(s * CT + i, n)]

        def rwkv_pool(pool, own):
            g = nc.gpsimd

            def times(out, a, b, op=ALU.mult):
                return g.tensor_tensor(out, a, b, op)

            def step(s, tm, cm):
                if tm:
                    pool.wait_ge(tm_var, s + 1)
                    g.tensor_tensor(rs1, ve1, neghalf[:, 0:2 * CT].rearrange("p (a b) -> p a b", a=2), ALU.pow).then_inc(tm_rs, 1)
                    pool.wait_ge(h_t, s + 1)
                    for k in range(KC):
                        ins = times(dT[:, k].rearrange("p (b q) -> p b q", q=SQ), hT[:, k, :, 1:], hT[:, k, :, 0:SQ], ALU.subtract)
                    ins.then_inc(d_t, 1)
                if cm:
                    pool.wait_ge(h2_t, s)
                    for k in range(KC):
                        ins = times(d2T[:, k].rearrange("p (b q) -> p b q", q=SQ), h2T[:, k, :, 1:], h2T[:, k, :, 0:SQ], ALU.subtract)
                    ins.then_inc(d2_t, 1)
                if cm:
                    for m in range(2):
                        for k in range(KC):
                            pool.wait_ge(mix2_hi, s * 4 + (2 * m + k + 1 - 4))
                            times(mix216[:, m, k, LO], mix2f[:, k], mix216[:, m, k, HI], ALU.subtract).then_inc(mix2_lo, 1)
                if tm:
                    for m in range(3):
                        for k in range(KC):
                            pool.wait_ge(mix_hi, s * 6 + (2 * m + k + 1))
                            times(mix16[:, m, k, LO], mixf[:, k], mix16[:, m, k, HI], ALU.subtract).then_inc(mix_lo, 1)
                if cm:
                    for f in range(0, FC):
                        pool.wait_ge(k2_hi, s * 8 + (f + 1 - 8))
                        times(k216[:, f, LO], sqf[:, f % 2], k216[:, f, HI], ALU.subtract).then_inc(k2_lo, 1)
                if tm:
                    for o in range(KC):
                        pool.wait_ge(eu_v, s * 2 + (o + 1))
                        times(euv[:, o], eu[:, o], vS[:, o]).then_inc(rwf, 1)
                if tm:
                    for o in range(KC):
                        pool.wait_ge(rw_hi, s * 2 + (o + 1))
                        times(rw16[:, o, LO], top[:, o], rw16[:, o, HI], ALU.subtract).then_inc(rw_lo, 1)
                if cm:
                    pool.wait_ge(x2_var, s)
                    g.tensor_tensor(rs3, ve3, neghalf[:, 0:CT], ALU.pow).then_inc(x2_rs, 1)
                if tm:
                    pool.wait_ge(y_var, s + 1)
                    g.tensor_tensor(rs2, ve2, neghalf[:, 0:CT], ALU.pow).then_inc(y_rs, 1)

            chunk_steps(pool, step)

        def rwkv_scalar(act):
            a = nc.scalar
            pad = lambda t, k: t[:, k, :, 1:]
            fold = lambda ap: ap.rearrange("p (b q) -> p b q", q=SQ)
            a.activation(ew[:, 0], vec[:, TD], ACT.Exp).then_inc(c_ew, 1)
            act.wait_ge(c_ew, 2)
            a.activation(ew[:, 1], ew[:, 0], ACT.Exp).then_inc(c_ew, 1)

            def step(s, tm, cm):
                if tm:
                    act.wait_ge(tm_norm, s + 1)
                    need(act, h2_n, s)
                    for i in range(CT):
                        ins = a.activation(hN[:, i], tiles_of(s, i, 1).squeeze(1), ACT.Identity, bias=nmc[:, i:i + 1], scale=rs1[:, 1, i:i + 1])
                    ins.then_inc(hn_done, 1)
                    act.wait_ge(h_ps, s + 1)
                    for k in range(KC):
                        ins = a.activation(pad(hT, k), fold(PS[:, 2 + k]), ACT.Copy, scale=vec[:, LN1, k:k + 1])
                    ins.then_inc(h_t, 1)
                if cm:
                    act.wait_ge(h2_ps, s)
                    for k in range(KC):
                        ins = a.activation(pad(h2T, k), fold(PS[:, 4 + k]), ACT.Copy, scale=vec[:, LN2, k:k + 1])
                    ins.then_inc(h2_t, 1)
                if cm:
                    for m in range(2):
                        for k in range(KC):
                            act.wait_ge(mixed2, s * 4 + (2 * m + k + 1 - 4))
                            a.activation(mix216[:, m, k, HI], mix2f[:, k], ACT.Copy).then_inc(mix2_hi, 1)
                if tm:
                    for m in range(3):
                        for k in range(KC):
                            act.wait_ge(mixed, s * 6 + (2 * m + k + 1))
                            a.activation(mix16[:, m, k, HI], mixf[:, k], ACT.Copy).then_inc(mix_hi, 1)
                if tm:
                    for o in range(KC):
                        act.wait_ge(kvr_ps, s * 6 + (o + 1))
                        a.activation(ek[:, o], PS[:, o], ACT.Exp, scale=1 / WS)
                        a.activation(eu[:, o], PS[:, o], ACT.Exp, scale=1 / WS, bias=vec[:, TF, o:o + 1]).then_inc(kvr_out, 1)
                    for o in range(KC):
                        act.wait_ge(kvr_ps, s * 6 + (o + 3))
                        a.activation(vS[:, o], PS[:, 2 + o], ACT.Copy, scale=1 / WS).then_inc(kvr_out, 1)
                    for o in range(KC):
                        act.wait_ge(kvr_ps, s * 6 + (o + 5))
                        a.activation(rS[:, o], PS[:, o], ACT.Tanh, scale=0.5 / WS).then_inc(kvr_out, 1)
                if cm:
                    for p in range(2):
                        act.wait_ge(r2_ps, s * 2 + (p + 1 - 2))
                        a.activation(r2N[:, 2 * p:2 * p + 2], PS[:, 6 + p].rearrange("p (a n) -> p a n", a=2), ACT.Tanh,
                                     scale=0.5 / WS).then_inc(r2_out, 1)

                    def relu(f):
                        act.wait_ge(key_ps, s * 8 + (f + 1 - 8))
                        if f >= 2:
                            act.wait_ge(sq_out, s * 8 + (f - 1 - 8))
                        a.activation(reluf[:, f % 2], PS[:, 4 + f % 4], ACT.Relu, scale=1 / WS).then_inc(relu_out, 1)

                    def square_hi(f):
                        act.wait_ge(sq_out, s * 8 + (f + 1 - 8))
                        a.activation(k216[:, f, HI], sqf[:, f % 2], ACT.Copy).then_inc(k2_hi, 1)

                    relu(0)
                    for f in range(1, FC):
                        relu(f)
                        square_hi(f - 1)
                    square_hi(FC - 1)
                if tm:
                    for o in range(KC):
                        act.wait_ge(top_ready, s * 2 + (o + 1))
                        a.activation(rw16[:, o, HI], top[:, o], ACT.Copy).then_inc(rw_hi, 1)
                    act.wait_ge(y_rs, s + 1)
                    for i in range(CT):
                        ins = a.activation(h2N[:, i], yN[:, i], ACT.Copy, scale=rs2[:, i:i + 1])
                    ins.then_inc(h2_n, 1)
                if cm:
                    act.wait_ge(x3_ps, s)
                    cols = bass.ds(s * CN - CN, CN)
                    for k in range(KC):
                        ins = a.activation(x3T[:, k, HI, cols], PS[:, 6 + k], ACT.Copy)
                    ins.then_inc(x3_hi, 1)
                    act.wait_ge(lg_ps, s)
                    a.activation(logits[:, bass.ds(s * CT - CT, CT)], PS[:, 4, 0:CT * NE].rearrange("p (t e) -> p t e", e=NE),
                                 ACT.Copy, scale=1 / WS).then_inc(lg_out, 1)

            chunk_steps(act, step)

        top_ready, hn_done = sem("top_ready"), sem("hn_done")
        E20, EM20 = 485165195.4097903, 2.061153622438558e-09

        def rwkv_vector(dve, own):
            v = nc.vector
            fold = lambda ap: ap.rearrange("p (b q) -> p b q", q=SQ)
            for t in (hT, h2T, ekp, ekvp):
                v.memset(t[:, :, :, 0:1], 0.0)
            own.link(v.memset(decay, 0.0))
            dve.wait_ge(c_ew, 1)
            v.tensor_scalar(ew[:, 0], ew[:, 0], -1.0, -20.0, ALU.mult, ALU.max).then_inc(c_ew, 1)
            dve.wait_ge(c_ew, 3)
            own.link(v.tensor_copy(decay[:, :, :, 1:], ew[:, 1].unsqueeze(2).unsqueeze(3).to_broadcast([P, KC, CB, SQ])))

            def stats(st, mv, src):
                for i in range(CT):
                    n = own.mark(v.bn_stats(st[:, i], src(i)))
                wait_apart(dve, dve_step, n)
                for i in range(CT):
                    n = own.mark(v.bn_aggr(mv[:, i], st[:, i]))
                dve.wait_ge(dve_step, n)

            def step(s, tm, cm):
                if tm:
                    for p in range(2):
                        dve.wait_ge(wo_ps, s * 2 + (p + 1))
                        rows = tiles_of(s, 2 * p, 2)
                        n = own.mark(v.scalar_tensor_tensor(rows, PS[:, p].rearrange("p (a n) -> p a n", a=2), 1 / WS, rows, ALU.mult, ALU.add))
                    wait_apart(dve, dve_step, n)
                    stats(st1, mv1, lambda i: tiles_of(s, i, 1).squeeze(1))
                    own.mark(v.tensor_scalar(ve1[:, 0], mv1[:, :, 1], 1e-5, None, ALU.add))
                    v.tensor_scalar(ve1[:, 1], mv1[:, :, 1], 1.0 + 1e-6, 1e-11, ALU.mult, ALU.add).then_inc(tm_var, 1)
                    dve.wait_ge(tm_rs, s + 1)
                    v.scalar_tensor_tensor(nmc, mv1[:, :, 0], -1.0, rs1[:, 1], ALU.mult, ALU.mult).then_inc(tm_norm, 1)
                    for i in range(CT):
                        n = own.mark(v.tensor_scalar(xl[:, i], tiles_of(s, i, 1).squeeze(1), mv1[:, i, 0:1], rs1[:, 0, i:i + 1], ALU.subtract, ALU.mult))
                if cm:
                    dve.wait_ge(d2_t, s)
                    for m, mix in ((0, MK2), (1, MR2)):
                        for k in range(KC):
                            if m:
                                dve.wait_ge(mix2_lo, s * 4 + (2 * m + k - 1 - 4))
                            v.scalar_tensor_tensor(fold(mix2f[:, k]), fold(d2T[:, k]), vec[:, mix, k:k + 1], h2T[:, k, :, 0:SQ],
                                                   ALU.mult, ALU.add).then_inc(mixed2, 1)
                if tm:
                    dve.wait_ge(d_t, s + 1)
                    for m, mix in ((0, MK), (1, MV), (2, MR)):
                        for k in range(KC):
                            if m:
                                dve.wait_ge(mix_lo, s * 6 + (2 * m + k - 1))
                            v.scalar_tensor_tensor(fold(mixf[:, k]), fold(dT[:, k]), vec[:, mix, k:k + 1], hT[:, k, :, 0:SQ],
                                                   ALU.mult, ALU.add).then_inc(mixed, 1)
                if cm:
                    for f in range(FC):
                        dve.wait_ge(relu_out, s * 8 + (f + 1 - 8))
                        if f >= 2:
                            dve.wait_ge(k2_lo, s * 8 + (f - 1 - 8))
                        v.tensor_tensor(sqf[:, f % 2], reluf[:, f % 2], reluf[:, f % 2], ALU.mult).then_inc(sq_out, 1)
                if tm:
                    for o in range(KC):
                        dve.wait_ge(kvr_out, s * 6 + (o + 1))
                        own.mark(v.tensor_scalar(ekp[:, o, :, 1:], fold(ek[:, o]), EM20, E20, ALU.max, ALU.min))
                        own.link(v.tensor_scalar(eu[:, o], eu[:, o], EM20, E20, ALU.max, ALU.min))
                        dve.wait_ge(kvr_out, s * 6 + (o + 3))
                        own.mark(v.tensor_tensor(ekvp[:, o, :, 1:], ekp[:, o, :, 1:], fold(vS[:, o]), ALU.mult))
                        v.tensor_tensor_scan(dnm[:, o].rearrange("p b q -> p (b q)"), decay[:, o].rearrange("p b q -> p (b q)"),
                                             ekp[:, o].rearrange("p b q -> p (b q)"), 0.0, ALU.mult, ALU.add).then_inc(eu_v, 1)
                        dve.wait_ge(eu_v, s * 2 + (o + 1))
                        own.mark(v.scalar_tensor_tensor(fold(bot[:, o]), dnm[:, o, :, 0:SQ], 1e-8, fold(eu[:, o]), ALU.add, ALU.add))
                        own.link(v.tensor_tensor_scan(num[:, o].rearrange("p b q -> p (b q)"), decay[:, o].rearrange("p b q -> p (b q)"),
                                                      ekvp[:, o].rearrange("p b q -> p (b q)"), 0.0, ALU.mult, ALU.add))
                        own.mark(v.reciprocal(bot[:, o], bot[:, o]))
                        dve.wait_ge(rwf, s * 2 + (o + 1))
                        own.link(v.tensor_tensor(fold(top[:, o]), num[:, o, :, 0:SQ], fold(euv[:, o]), ALU.add))
                        own.link(v.tensor_tensor(top[:, o], top[:, o], bot[:, o], ALU.mult))
                        dve.wait_ge(kvr_out, s * 6 + (o + 5))
                        v.scalar_tensor_tensor(top[:, o], rS[:, o], 1.0, top[:, o], ALU.add, ALU.mult).then_inc(top_ready, 1)
                if cm:
                    dve.wait_ge(r2_out, s * 2)
                    for p in range(2):
                        dve.wait_ge(val_ps, s * 2 + (p + 1 - 2))
                        n = own.mark(v.scalar_tensor_tensor(zN[:, 2 * p:2 * p + 2], r2N[:, 2 * p:2 * p + 2], 1.0,
                                                            PS[:, 4 + p].rearrange("p (a n) -> p a n", a=2), ALU.add, ALU.mult))
                    dve.wait_ge(dve_step, n)
                    rows = tiles_of(s, -CT, CT)
                    n = own.mark(v.scalar_tensor_tensor(rows, zN, 0.5 / WS, rows, ALU.mult, ALU.add))
                    wait_apart(dve, dve_step, n)
                    stats(st3, mv3, lambda i: tiles_of(s, i - CT, 1).squeeze(1))
                    v.tensor_scalar(ve3, mv3[:, :, 1], 1e-5, None, ALU.add).then_inc(x2_var, 1)
                if tm:
                    for p in range(2):
                        dve.wait_ge(wout_ps, s * 2 + (p + 1))
                        pair = slice(2 * p, 2 * p + 2)
                        n = own.mark(v.scalar_tensor_tensor(yN[:, pair], PS[:, 2 + p].rearrange("p (a n) -> p a n", a=2), 0.5 / WS, xl[:, pair],
                                                            ALU.mult, ALU.add))
                    wait_apart(dve, dve_step, n)
                    stats(st2, mv2, lambda i: yN[:, i])
                    own.link(v.tensor_tensor(ve2, mv2[:, :, 0], mv2[:, :, 0], ALU.mult))
                    v.scalar_tensor_tensor(ve2, ve2, 1e-6, mv2[:, :, 1], ALU.add, ALU.add).then_inc(y_var, 1)
                    rows = tiles_of(s, 0, CT)
                    own.mark(v.tensor_tensor(rows, rows, yN, ALU.add))
                if cm:
                    dve.wait_ge(x2_rs, s)
                    for i in range(CT):
                        ins = v.tensor_scalar(xn3[:, i], tiles_of(s, i - CT, 1).squeeze(1), mv3[:, i, 0:1], rs3[:, i:i + 1], ALU.subtract, ALU.mult)
                    ins.then_inc(xn3_done, 1)
                    dve.wait_ge(x3_hi, s)
                    cols = bass.ds(s * CN - CN, CN)
                    for k in range(KC):
                        ins = v.tensor_tensor(x3T[:, k, LO, cols], PS[:, 6 + k], x3T[:, k, HI, cols], ALU.subtract)
                    ins.then_inc(x3_lo, 1)

            chunk_steps(dve, step, own, DVE_RWKV)

        def rwkv_tensor(pe):
            te = nc.tensor

            def product(out, pairs):
                n, last = 0, 3 * len(pairs) - 1
                for lhs, rhs in pairs:
                    for a, b in PASSES:
                        ins = te.matmul(out, lhs(a), rhs(b), start=n == 0, stop=n == last)
                        n += 1
                return ins

            def w(k, col, n=P):
                return lambda part: W16[:, k, part, col:col + n]

            def step(s, tm, cm):
                if tm:
                    pe.wait_ge(ao_split, s * CT + CT)
                    need(pe, kvr_out, s * 6)
                    for i in range(CT):
                        ins = product(PS[:, i // 2, D * (i % 2):D * (i % 2 + 1)],
                                      [((lambda part, k=k: aoT[:, k, part, bass.ds(s * CN + i * P, P)]), w(k, WO, D)) for k in range(KC)])
                        if i % 2:
                            ins.then_inc(wo_ps, 1)
                if cm:
                    pe.wait_ge(h2_n, s)
                    if tm:
                        pe.wait_ge(hn_done, s + 1)
                    else:
                        pe.wait_ge(lg_out, s - 1)
                    for k in range(KC):
                        for i in range(CT):
                            ins = te.transpose(PS[:, 4 + k, P * i:P * (i + 1)], h2N[:, i, P * k:P * (k + 1)], ident)
                    ins.then_inc(h2_ps, 1)
                if tm:
                    pe.wait_ge(hn_done, s + 1)
                    need(pe, y_var, s)
                    for k in range(KC):
                        for i in range(CT):
                            ins = te.transpose(PS[:, 2 + k, P * i:P * (i + 1)], hN[:, i, P * k:P * (k + 1)], ident)
                    ins.then_inc(h_ps, 1)
                if tm:
                    pe.wait_ge(tm_var, s + 1)
                    for m, col in ((0, WTK), (1, WTV), (2, WTR)):
                        pe.wait_ge(mix_lo, s * 6 + (2 * m + 2))
                        for o in range(KC):
                            if m == 2:
                                pe.wait_ge(kvr_out, s * 6 + (o + 1))
                            product(PS[:, (2 * m + o) % 4], [(w(k, col + P * o), lambda part, k=k: mix16[:, m, k, part]) for k in range(KC)]
                                    ).then_inc(kvr_ps, 1)
                if cm:
                    pe.wait_ge(mix2_lo, s * 4)
                    for i in range(CT):
                        ins = product(PS[:, 6 + i // 2, D * (i % 2):D * (i % 2 + 1)],
                                      [(lambda part, k=k: mix216[:, 1, k, part, P * i:P * (i + 1)], w(k, WR2, D)) for k in range(KC)])
                        if i % 2:
                            ins.then_inc(r2_ps, 1)
                    for f in range(FC):
                        if f == 2:
                            pe.wait_ge(r2_out, s * 2)
                        if f >= 4:
                            pe.wait_ge(relu_out, s * 8 + (f - 3 - 8))
                        product(PS[:, 4 + f % 4], [(w(k, WK2 + P * f), lambda part, k=k: mix216[:, 0, k, part]) for k in range(KC)]
                                ).then_inc(key_ps, 1)
                if tm:
                    pe.wait_ge(rw_lo, s * 2 + 2)
                    pe.wait_ge(kvr_out, s * 6 + 4)
                    for i in range(CT):
                        ins = product(PS[:, 2 + i // 2, D * (i % 2):D * (i % 2 + 1)],
                                      [(lambda part, k=k: rw16[:, k, part, P * i:P * (i + 1)], w(k, WTO, D)) for k in range(KC)])
                        if i % 2:
                            ins.then_inc(wout_ps, 1)
                if cm:
                    pe.wait_ge(k2_lo, s * 8)
                    for i in range(CT):
                        ins = product(PS[:, 4 + i // 2, D * (i % 2):D * (i % 2 + 1)],
                                      [(lambda part, f=f: k216[:, f, part, P * i:P * (i + 1)], lambda part, f=f: WV2[:, f, part]) for f in range(FC)])
                        if i % 2:
                            ins.then_inc(val_ps, 1)
                    pe.wait_ge(xn3_done, s)
                    for k in range(KC):
                        for i in range(CT):
                            ins = te.transpose(PS[:, 6 + k, P * i:P * (i + 1)], xn3[:, i, P * k:P * (k + 1)], ident)
                    ins.then_inc(x3_ps, 1)
                    pe.wait_ge(x3_lo, s)
                    for i in range(CT):
                        ins = product(PS[:, 4, NE * i:NE * (i + 1)],
                                      [(lambda part, k=k: x3T[:, k, part, bass.ds(s * CN + (i - CT) * P, P)], w(k, WG, NE)) for k in range(KC)])
                    ins.then_inc(lg_ps, 1)

            pe.wait_ge(wb_ready, 8)
            chunk_steps(pe, step)

        w1f = place("w1f", A0, [KC, FF])
        w2f = place("w2f", at["w1f"], [FC, D])
        w1h = place("w1h", at["w2f"], [2, KC, 2, FF], F16)
        w2h = place("w2h", at["w1h"], [2, FC, 2, D], F16)
        hid16 = place("hid16", at["w2h"], [2, FC, 2, CN], F16)
        gel = place("gel", at["hid16"], [2, CN])
        b1s = place("b1s", at["gel"], [NE, FC])
        b2s = place("b2s", at["b1s"], [D])
        cwT = place("cwT", at["b2s"], [NT, P])
        mx = place("mx", at["cwT"], [NT])
        gate = place("gate", at["mx"], [NT, NE])
        ge = place("ge", at["gate"], [NT, NE])
        cmp1 = place("cmp1", at["ge"], [NT, NE, NE])
        cmp2 = place("cmp2", at["cmp1"], [NT, NE, NE])
        tri = place("tri", at["cmp2"], [NE, NE])
        rank = place("rank", at["tri"], [NT, NE])
        cw = place("cw", at["rank"], [NT, NE])
        cwe = place("cwe", at["cw"], [2, NT])
        b1e = place("b1e", at["cwe"], [2, FC])
        (tri_ready, sm_in, sm_exp, cw_ready, cwt_ps, cwt_out, cb_ps, cb_out, b_in, w1_in, w2_in, w1_split, w2_split, hid_ps, gel_out, g_hi, g_lo,
         y_ps, acc_out, hid_used) = [sem(n) for n in (
            "tri_ready sm_in sm_exp cw_ready cwt_ps cwt_out cb_ps cb_out b_in w1_in w2_in w1_split w2_split hid_ps gel_out g_hi g_lo "
            "y_ps acc_out hid_used").split()]
        b1_in = [sem("b1_in0"), sem("b1_in1")]
        stored = sem("stored")
        NQ = TOK // CN

        def moe_sync(sp):
            sp.wait_ge(lg_out, NC)
            sp.dma_start(b2s[:NE], b2).then_inc(b_in, 16)
            with sp.Fori(0, NE // 2) as i:
                for par in range(2):
                    e = i * 2 + par
                    if par:
                        sp.wait_ge(w1_split, i * 2 + 1)
                        sp.wait_ge(w2_split, i * 2 + 1)
                    sp.dma_start(w1f, w1[bass.ds(e, 1)].rearrange("e (k p) f -> p (e k) f", p=P)).then_inc(w1_in, 16)
                    sp.dma_start(w2f, w2[bass.ds(e, 1)].rearrange("e (k p) d -> p (e k) d", p=P)).then_inc(w2_in, 16)
                    sp.dma_start(b1e[:, par], b1[bass.ds(e, 1)].rearrange("e p f -> p (e f)")).then_inc(b1_in[par], 16)
                wait_apart(sp, y_ps, i * (2 * NQ * 2) + 2 * NQ * 2)
            sp.wait_ge(acc_out, NE * NQ * 2)
            sp.dma_start(out.rearrange("(t p) d -> p t d", p=P), x_all).then_inc(stored, 16)
            sp.wait_ge(stored, 16)

        def moe_pool(pool, own):
            g = nc.gpsimd
            pool.wait_ge(lg_out, NC)
            own.link(g.memset(tri, 1.0))
            g.affine_select(out=tri, in_=tri, compare_op=ALU.is_gt, fill=0.0, base=0, channel_multiplier=0, pattern=[[1, NE], [-1, NE]]).then_inc(tri_ready, 1)
            with pool.Fori(0, NE // 2) as i:
                own.enter(i, 8)
                for par in range(2):
                    for f32, f16, arrived, done in ((w1f, w1h, w1_in, w1_split), (w2f, w2h, w2_in, w2_split)):
                        wait_apart(pool, arrived, i * 32 + 16 * (par + 1))
                        own.link(g.tensor_scalar(f32, f32, WS, 0.0, ALU.mult, ALU.add))
                        own.link(g.tensor_scalar(f16[:, par, :, HI], f32, 1.0, 0.0, ALU.mult, ALU.add))
                        g.tensor_tensor(f16[:, par, :, LO], f32, f16[:, par, :, HI], ALU.subtract).then_inc(done, 1)
            own.leave(NE // 2)

        def moe_scalar(act):
            a = nc.scalar
            act.wait_ge(sm_in, 1)
            a.activation(ge, ge, ACT.Exp).then_inc(sm_exp, 1)
            for c in range(NC):
                act.wait_ge(cwt_ps, c + 1)
                a.activation(cwT[:NE, CT * c:CT * (c + 1)], PS[:NE, c].rearrange("p (t n) -> p t n", t=CT), ACT.Copy).then_inc(cwt_out, 1)
            with act.Fori(0, NE // 2) as i:
                for par in range(2):
                    act.wait_ge(b1_in[par], i * 16 + 16)
                    for q in range(NQ):
                        base = (par * NQ + q) * FC

                        def hi(f):
                            act.wait_ge(gel_out, i * (2 * NQ * FC) + (base + f + 1))
                            a.activation(hid16[:, q % 2, f, HI], gel[:, f % 2], ACT.Copy).then_inc(g_hi, 1)

                        for f in range(FC):
                            act.wait_ge(hid_ps, i * (2 * NQ * FC) + (base + f + 1))
                            if base + f >= 2:
                                act.wait_ge(g_lo, i * (2 * NQ * FC) + (base + f - 1))
                            a.activation(gel[:, f % 2], PS[:, f % 4], ACT.Gelu, bias=b1e[:, par, f:f + 1], scale=1 / WS).then_inc(gel_out, 1)
                            if f:
                                hi(f - 1)
                        hi(FC - 1)
                act.wait_ge(g_lo, i * (2 * NQ * FC) + 2 * NQ * FC)

        def moe_vector(dve, own):
            v = nc.vector
            bc_e = lambda t: t.unsqueeze(2).to_broadcast([P, NT, NE])
            dve.wait_ge(lg_out, NC)
            own.link(v.tensor_reduce(mx, logits, AX.X, ALU.max))
            v.tensor_tensor(ge, logits, bc_e(mx), ALU.subtract).then_inc(sm_in, 1)
            dve.wait_ge(sm_exp, 1)
            own.link(v.tensor_reduce(mx, ge, AX.X, ALU.add))
            own.link(v.reciprocal(mx, mx))
            own.link(v.tensor_tensor(gate, ge, bc_e(mx), ALU.mult))
            full = [P, NT, NE, NE]
            of_j, of_e = gate.unsqueeze(2).to_broadcast(full), gate.unsqueeze(3).to_broadcast(full)
            own.mark(v.tensor_tensor(cmp1, of_j, of_e, ALU.is_gt))
            own.link(v.tensor_tensor(cmp2, of_j, of_e, ALU.is_equal))
            dve.wait_ge(tri_ready, 1)
            own.link(v.tensor_tensor(cmp2, cmp2, tri.unsqueeze(1).to_broadcast(full), ALU.mult))
            own.link(v.tensor_tensor(cmp1, cmp1, cmp2, ALU.add))
            own.link(v.tensor_reduce(rank, cmp1, AX.X, ALU.add))
            v.scalar_tensor_tensor(cw, rank, 2.0, gate, ALU.is_lt, ALU.mult).then_inc(cw_ready, 1)
            for c in range(NC):
                for p in range(2):
                    dve.wait_ge(cb_ps, 2 * c + p + 1)
                    rows = x_all[:, CT * c + 2 * p:CT * c + 2 * p + 2]
                    v.tensor_tensor(rows, rows, PS[:, 4 + p].rearrange("p (a n) -> p a n", a=2), ALU.add).then_inc(cb_out, 1)
            dve.wait_ge(cw_ready, 1)
            with dve.Fori(0, NE // 2) as i:
                own.enter(i, 2)
                for par in range(2):
                    own.link(v.tensor_scalar(cwe[:, par], cw[:, :, bass.ds(i * 2 + par, 1)].squeeze(2), 1 / WS, None, ALU.mult))
                    for q in range(NQ + 1):
                        if q < NQ:
                            base = (par * NQ + q) * FC
                            for f in range(FC):
                                dve.wait_ge(g_hi, i * (2 * NQ * FC) + (base + f + 1))
                                v.tensor_tensor(hid16[:, q % 2, f, LO], gel[:, f % 2], hid16[:, q % 2, f, HI], ALU.subtract).then_inc(g_lo, 1)
                        if q:
                            for p in range(2):
                                dve.wait_ge(y_ps, i * (4 * NQ) + (par * 2 * NQ + 2 * (q - 1) + p + 1))
                                for u in range(2):
                                    t = CT * (q - 1) + 2 * p + u
                                    ins = v.scalar_tensor_tensor(x_all[:, t], PS[:, 4 + 2 * (q % 2) + p, D * u:D * (u + 1)], cwe[:, par, t:t + 1], x_all[:, t],
                                                                 ALU.mult, ALU.add)
                                ins.then_inc(acc_out, 1)
            own.leave(NE // 2)

        def moe_tensor(pe):
            te = nc.tensor
            pe.wait_ge(cw_ready, 1)
            pe.wait_ge(b_in, 16)
            for c in range(NC):
                for i in range(CT):
                    ins = te.transpose(PS[:NE, c, P * i:P * (i + 1)], cw[:, CT * c + i], ident)
                ins.then_inc(cwt_ps, 1)
            for c in range(NC):
                pe.wait_ge(cwt_out, c + 1)
                for i in range(CT):
                    if i % 2 == 0:
                        need(pe, cb_out, 2 * c + i // 2 - 1)
                    ins = te.matmul(PS[:, 4 + i // 2, D * (i % 2):D * (i % 2 + 1)], cwT[:NE, CT * c + i], b2s[:NE], start=True, stop=True)
                    if i % 2:
                        ins.then_inc(cb_ps, 1)
            pe.wait_ge(cb_out, 2 * NC)
            with pe.Fori(0, NE // 2) as i:
                for par in range(2):
                    pe.wait_ge(w1_split, i * 2 + (par + 1))
                    for q in range(NQ + 1):
                        if q < NQ:
                            base = (par * NQ + q) * FC
                            for f in range(FC):
                                n = base + f
                                if n >= 4:
                                    pe.wait_ge(gel_out, i * (2 * NQ * FC) + (n - 3))
                                for m in range(6):
                                    k, (a, b) = m // 3, PASSES[m % 3]
                                    ins = te.matmul(PS[:, f % 4], w1h[:, par, k, a, P * f:P * (f + 1)], x3T[:, k, b, CN * q:CN * (q + 1)],
                                                    start=m == 0, stop=m == 5)
                                ins.then_inc(hid_ps, 1)
                        if q == 1:
                            pe.wait_ge(w2_split, i * 2 + (par + 1))
                        if q:
                            pe.wait_ge(g_lo, i * (2 * NQ * FC) + ((par * NQ + q) * FC))
                            for u in range(CT):
                                n = (par * NQ + q - 1) * 2 + u // 2
                                if u % 2 == 0 and n >= 4:
                                    pe.wait_ge(acc_out, i * (4 * NQ) + (n - 3))
                                for m in range(3 * FC):
                                    f, (a, b) = m // 3, PASSES[m % 3]
                                    ins = te.matmul(PS[:, 4 + 2 * (q % 2) + u // 2, D * (u % 2):D * (u % 2 + 1)], hid16[:, (q - 1) % 2, f, a, P * u:P * (u + 1)],
                                                    w2h[:, par, f, b], start=m == 0, stop=m == 3 * FC - 1)
                                if u % 2:
                                    ins.then_inc(y_ps, 1)

        def after_attention_sync(sp):
            moe_sync(sp)

        def after_attention_pool(pool, own):
            rwkv_pool(pool, own)
            moe_pool(pool, own)

        def after_attention_scalar(act):
            rwkv_scalar(act)
            moe_scalar(act)

        def after_attention_vector(dve, own):
            dve.wait_ge(xbo_ready, 8)
            dve.wait_ge(ao_split, NT)
            rwkv_vector(dve, own)
            moe_vector(dve, own)

        def after_attention_tensor(pe):
            rwkv_tensor(pe)
            moe_tensor(pe)

        block = stack.enter_context(nc.Block())

        def attention_tiles(eng, step, trail=None, per=0):
            step(0, True, False)
            with eng.Fori(1, NT - 1) as t:
                if trail:
                    trail.enter(t - 1, per)
                step(t, False, False)
            if trail:
                trail.leave(NT - 2)
            step(NT - 1, False, True)

        UNITS = [(b, j) for b in range(BT) for j in range(2)]

        @block.sync
        def _(sp):
            x_v = x.rearrange("(t p) d -> p t d", p=P)
            ctx_v = ctx_t.rearrange("(k p) n -> p k n", p=P)
            w_v = w_all.rearrange("(k p) n -> p k n", p=P)
            sp.dma_start(vec, vecs).then_inc(vecs_in, 16)
            sp.dma_start(stage[:, :, 0:NWA], w_v[:, :, 0:NWA]).then_inc(wa_in, 16)
            for c in range(NC):
                sp.dma_start(x_all[:, CT * c:CT * (c + 1), :], x_v[:, CT * c:CT * (c + 1), :]).then_inc(x_in[c], 16)
                if c == 0:
                    sp.dma_start(clf, ctx_last).then_inc(cl_in, 16)
            for b in range(BT):
                sp.dma_start(ctxf[:, b], ctx_v[:, :, SK * b:SK * (b + 1)]).then_inc(ctx_in[b], 16)
            sp.dma_start(bo_bc, bo.partition_broadcast(P)).then_inc(bo_in, 16)
            sp.dma_start(stage[:, :, NWA:NW], w_v[:, :, NWA:NW]).then_inc(wb_in, 16)
            sp.dma_start(stage2, w_value2.rearrange("(k p) n -> p k n", p=P)).then_inc(wb_in, 16)
            with sp.Fori(1, NT) as t:
                for b in range(BT):
                    sp.wait_ge(ctx_split, t * BT + (b - BT + 1))
                    sp.dma_start(ctxf[:, b], ctx_v[:, :, bass.ds(t * (BT * SK) + SK * b, SK)]).then_inc(ctx_in[b], 16)
            after_attention_sync(sp)

        @block.gpsimd
        def _(pool):
            g = nc.gpsimd
            own = Trail(pool, pool_step, wait_apart)

            def keep(m, base, cm, pattern, op=ALU.is_ge, fill=0.0):
                own.link(g.affine_select(out=m, in_=m, compare_op=op, fill=fill, base=base, channel_multiplier=cm, pattern=pattern))

            g.memset(neghalf, -0.5).then_inc(consts, 1)
            own.mark(g.memset(ident, 0.0))
            own.mark(g.memset(mask8, 1.0))
            own.mark(g.memset(maskO, 1.0))
            own.mark(g.memset(maskV, 1.0))
            own.mark(g.memset(sel16, 0.0))
            own.link(g.memset(plast, 0.0))
            keep(ident, 0, 1, [[-1, P]], ALU.not_equal, 1.0)
            keep(mask8, 0, 1, [[-HD, 8]])
            keep(mask8, HD - 1, -1, [[HD, 8]])
            keep(maskO, 0, 1, [[-SQ, 4], [0, HD]])
            keep(maskO, SQ - 1, -1, [[SQ, 4], [0, HD]])
            keep(maskV, 0, 1, [[0, 2], [-4, 2], [0, 64]])
            keep(maskV, 3, -1, [[0, 2], [4, 2], [0, 64]])
            for h in range(4):
                keep(sel16, -SQ * h, 1, [[-1, SQ]], ALU.not_equal, 1.0)
            g.tensor_copy(ident16, ident).then_inc(consts, 1)

            pool.wait_ge(cl_in, 16)
            for k in range(KC):
                own.link(g.tensor_scalar(cl16[:, k, HI], clf[:, k], 1.0, 0.0, ALU.mult, ALU.add))
                g.tensor_tensor(cl16[:, k, LO], clf[:, k], cl16[:, k, HI], ALU.subtract).then_inc(cl_split, 1)

            def split_ctx_hi(slot, par, arrivals):
                wait_apart(pool, ctx_in[slot], arrivals * 16)
                own.link(g.tensor_scalar(ctx16[:, par, :, HI, 0:SK], ctxf[:, slot], 1.0, 0.0, ALU.mult, ALU.add))

            def split_ctx_lo(slot, par):
                g.tensor_tensor(ctx16[:, par, :, LO, 0:SK], ctxf[:, slot], ctx16[:, par, :, HI, 0:SK], ALU.subtract).then_inc(ctx_split, 1)

            split_ctx_hi(0, 0, 1)
            split_ctx_lo(0, 0)
            pool.wait_ge(var_ready, 1)
            g.tensor_tensor(rs0, ve0, neghalf, ALU.pow).then_inc(rstd_ready, 1)
            split_ctx_hi(1, 1, 1)
            split_ctx_lo(1, 1)
            for i in range(NT // 2):
                pool.wait_ge(vl_evac, i + 1)
                own.link(g.tensor_scalar(vlast[:8, 2 * i:2 * i + 2, HI], vlf[:8, i % 2], 1.0, 0.0, ALU.mult, ALU.add))
                g.tensor_tensor(vlast[:8, 2 * i:2 * i + 2, LO], vlf[:8, i % 2], vlast[:8, 2 * i:2 * i + 2, HI], ALU.subtract).then_inc(vl_split, 1)

            def plast_of(U, b, j):
                wait_apart(pool, probs, U + 1)
                g.tensor_copy(plast[:, j, b, :, b], Pr[:, j, :, SK - 1]).then_inc(p_last, 1)

            def split_o(Up, b, j):
                wait_apart(pool, o_masked, Up + 1)
                s = (2 * b + j) % 4
                own.link(g.tensor_scalar(Om16[:, s, HI], Om[:, j], 1.0, 0.0, ALU.mult, ALU.add))
                g.tensor_tensor(Om16[:, s, LO], Om[:, j], Om16[:, s, HI], ALU.subtract).then_inc(o_split, 1)

            def step(t, first, last):
                for n, (b, j) in enumerate(UNITS):
                    U = t * 8 + n
                    ahead = b + 2
                    load = j == 0 and not (last and ahead >= BT)
                    if load:
                        wait_apart(pool, v_ps, t * 8 + (2 * b + 2))
                        split_ctx_hi(ahead % BT, b % 2, t + (1 + ahead // BT))
                    plast_of(U, b, j)
                    if load:
                        split_ctx_lo(ahead % BT, b % 2)
                    if not (first and n == 0):
                        split_o(t * 8 + (n - 1), *UNITS[n - 1])
                    if first:
                        rest_of_weights(n)

            def rest_of_weights(n):
                if n == 0:
                    pool.wait_ge(wb_in, 32)
                    pool.wait_ge(bo_in, 16)
                    pool.wait_ge(xn_ready, NC)
                cols = slice(NWA + (NW - NWA) // 8 * n, NWA + (NW - NWA) // 8 * (n + 1))
                own.mark(g.tensor_scalar(stage[:, :, cols], stage[:, :, cols], WS, 0.0, ALU.mult, ALU.add))
                own.link(g.tensor_scalar(stage2[:, n], stage2[:, n], WS, 0.0, ALU.mult, ALU.add))
                own.mark(g.tensor_scalar(W16[:, :, HI, cols], stage[:, :, cols], 1.0, 0.0, ALU.mult, ALU.add))
                own.link(g.tensor_scalar(WV2[:, n, HI], stage2[:, n], 1.0, 0.0, ALU.mult, ALU.add))
                g.tensor_tensor(W16[:, :, LO, cols], stage[:, :, cols], W16[:, :, HI, cols], ALU.subtract)
                g.tensor_tensor(WV2[:, n, LO], stage2[:, n], WV2[:, n, HI], ALU.subtract).then_inc(wb_ready, 1)
                rows = x_all[:, 2 * n:2 * n + 2]
                g.tensor_tensor(rows, rows, bo_bc.unsqueeze(1).to_broadcast([P, 2, D]), ALU.add).then_inc(xbo_ready, 1)

            attention_tiles(pool, step, own, 4 + 8)
            split_o(8 * NT - 1, BT - 1, 1)
            after_attention_pool(pool, own)

        @block.scalar
        def _(act):
            s = nc.scalar

            def x_hi(c):
                act.wait_ge(xt_ps, c + 1)
                for k in range(KC):
                    ins = s.activation(xT[:, c % 2, k, HI], PS[:, 2 * (c % 2) + k], ACT.Copy)
                ins.then_inc(xt_hi, 1)

            def q_parts(c):
                act.wait_ge(q_ps, c + 1)
                for j in range(KC):
                    ins = s.activation(qT[:, j, HI, CN * c:CN * (c + 1)], PS[:, 4 + 2 * (c % 2) + j], ACT.Identity,
                                       bias=vec64[:, BQ, j:j + 1])
                ins.then_inc(q_hi, 1)

            for c in range(NC + 1):
                if c < NC:
                    x_hi(c)
                if c > 0:
                    q_parts(c - 1)

            def kv_hi(n, bpar, b4, j):
                act.wait_ge(k_ps, n + 1)
                s.activation(Kt[:, bpar, j, HI, 0:SK], PS[:, 4, 0:SK], ACT.Identity, bias=vec64[:, BK, j:j + 1]).then_inc(k_hi, 1)
                act.wait_ge(v_ps, n + 1)
                s.activation(Vt[:, b4, j, HI], PS[:, 5, 0:D], ACT.Copy).then_inc(v_hi, 1)

            def pt_high(Up):
                act.wait_ge(pt_ps, Up + 1)
                s.activation(PT[:, HI], PS[:, 6], ACT.Copy)
                s.activation(PTl[:8, HI], PS[:8, 7, P:2 * P], ACT.Copy).then_inc(pt_hi, 1)

            def tile_out(t):
                act.wait_ge(selected, t * 8)
                s.activation(aoF, PS[:, 5, D:2 * D].rearrange("p (k n) -> p k n", k=KC), ACT.Copy, scale=1 / WS).then_inc(ao_evac, 1)

            for j in range(2):
                kv_hi(j, 0, 0, j)

            def step(t, first, last):
                for n, (b, j) in enumerate(UNITS):
                    U = t * 8 + n
                    if not (first and n == 0):
                        pt_high(U - 1)
                    if n == 1 and not first:
                        tile_out(t)
                    act.wait_ge(negmax, U + 1)
                    for h in range(2):
                        ins = s.activation(Pr[:, j, h], PS[:, 2 * j + h, 0:SK], ACT.Exp, bias=nb[:, j, h:h + 1], scale=SM,
                                           accum_out=den[:, j, h:h + 1])
                    ins.then_inc(probs, 1)
                    if not (last and b == BT - 1):
                        kv_hi(U + 2, (b + 1) % 2, (b + 1) % BT, j)

            attention_tiles(act, step)
            pt_high(8 * NT - 1)
            tile_out(NT)
            after_attention_scalar(act)

        @block.vector
        def _(dve):
            v = nc.vector
            own = Trail(dve, dve_step)
            dve.wait_ge(vecs_in, 16)
            own.mark(v.tensor_scalar(vec64, vec, WS, None, ALU.mult))
            dve.wait_ge(wa_in, 16)
            own.link(v.tensor_scalar(W16[:, :, HI, 0:NWA], stage[:, :, 0:NWA], WS, None, ALU.mult))
            v.scalar_tensor_tensor(W16[:, :, LO, 0:NWA], stage[:, :, 0:NWA], WS, W16[:, :, HI, 0:NWA],
                                   ALU.mult, ALU.subtract).then_inc(wa_ready, 1)
            for t in range(NT):
                if t % CT == 0:
                    dve.wait_ge(x_in[t // CT], 16)
                n = own.mark(v.bn_stats(st0[:, t], x_all[:, t]))
            dve.wait_ge(dve_step, n)
            for t in range(NT):
                n = own.mark(v.bn_aggr(mv0[:, t], st0[:, t]))
            dve.wait_ge(dve_step, n)
            v.tensor_scalar(ve0, mv0[:, :, 1], 1e-5, None, ALU.add).then_inc(var_ready, 1)

            def last_values(i):
                dve.wait_ge(vl_ps, i + 1)
                need(dve, vl_split, i - 1)
                v.tensor_tensor(vlf[:8, i % 2], PS[:8, i].rearrange("p (t n) -> p t n", t=2),
                                maskV8, ALU.mult).then_inc(vl_evac, 1)

            dve.wait_ge(rstd_ready, 1)
            maskV8 = maskV[:8].rearrange("p a b n -> p (a b n)").unsqueeze(1).to_broadcast([8, 2, D])
            for c in range(NC + 2):
                if c < NC:
                    need(dve, xt_ps, c - 1)
                    for i in range(CT):
                        t = CT * c + i
                        ins = v.tensor_scalar(xn[:, c % 2, i], x_all[:, t], mv0[:, t, 0:1], rs0[:, t:t + 1], ALU.subtract, ALU.mult)
                    ins.then_inc(xn_ready, 1)
                if c == 0:
                    for i in range(NT // 2):
                        last_values(i)
                if 0 < c <= NC:
                    dve.wait_ge(xt_hi, c)
                    for k in range(KC):
                        ins = v.tensor_tensor(xT[:, (c - 1) % 2, k, LO], PS[:, 2 * ((c - 1) % 2) + k], xT[:, (c - 1) % 2, k, HI], ALU.subtract)
                    ins.then_inc(xt_split, 1)
                if c > 1:
                    dve.wait_ge(q_hi, c - 1)
                    for j in range(KC):
                        cols = slice(CN * (c - 2), CN * (c - 1))
                        ins = v.scalar_tensor_tensor(qT[:, j, LO, cols], PS[:, 4 + 2 * (c % 2) + j], vec64[:, BQ, j:j + 1],
                                                     qT[:, j, HI, cols], ALU.add, ALU.subtract)
                    ins.then_inc(q_split, 1)

            def kv_lo(n, bpar, b4, j):
                dve.wait_ge(k_hi, n + 1)
                v.scalar_tensor_tensor(Kt[:, bpar, j, LO, 0:SK], PS[:, 4, 0:SK], vec64[:, BK, j:j + 1], Kt[:, bpar, j, HI, 0:SK],
                                       ALU.add, ALU.subtract).then_inc(k_split, 1)
                dve.wait_ge(v_hi, n + 1)
                v.tensor_tensor(Vt[:, b4, j, LO], PS[:, 5, 0:D], Vt[:, b4, j, HI], ALU.subtract).then_inc(v_split, 1)

            qT4 = qT.rearrange("p j c n -> p (j c) n")

            def spread_queries(pair, half, heads):
                src = qT4[:, :, bass.ds(pair * (2 * SQ), 2 * SQ)].rearrange("p c (b q) -> p c b q", b=2)
                for h in heads:
                    ins = v.tensor_scalar(Qbd[:, half, :, :, SQ * h:SQ * (h + 1)], src, mask8[:, h:h + 1], None, ALU.mult)
                if heads[-1] == 7:
                    ins.then_inc(qbd, 1)

            def last_values_now(tile, half):
                v.tensor_copy(vlc[:8, half].rearrange("p c n -> p (c n)"),
                              vlast[:8].rearrange("p t c n -> p t (c n)")[:, bass.ds(tile, 1)].squeeze(1) if not isinstance(tile, int)
                              else vlast[:8, tile].rearrange("p c n -> p (c n)")).then_inc(vl_now, 1)

            dve.wait_ge(q_split, NC)
            dve.wait_ge(vl_split, NT // 2)
            spread_queries(0, 0, range(8))
            last_values_now(0, 0)
            for j in range(2):
                kv_lo(j, 0, 0, j)

            def pt_low(Up):
                dve.wait_ge(pt_hi, Up + 1)
                v.tensor_tensor(PT[:, LO], PS[:, 6], PT[:, HI], ALU.subtract)
                v.tensor_tensor(PTl[:8, LO], PS[:8, 7, P:2 * P], PTl[:8, HI], ALU.subtract).then_inc(pt_split, 1)

            def mask_out(Up, j):
                dve.wait_ge(pv, Up + 1)
                own.link(v.reciprocal(rec[:, j], den[:, j]))
                for h in range(2):
                    ins = v.scalar_tensor_tensor(Om[:, j, 64 * h:64 * (h + 1)], PS[:, 7, 64 * h:64 * (h + 1)], rec[:, j, h:h + 1],
                                                 maskO.rearrange("p a b -> p (a b)"), ALU.mult, ALU.mult)
                ins.then_inc(o_masked, 1)

            def split_tile_out(t):
                dve.wait_ge(ao_evac, t)
                cols = bass.ds(t * P - P, P)
                for k in range(KC):
                    own.link(v.tensor_scalar(aoT[:, k, HI, cols], aoF[:, k], vec[:, BV, k:k + 1], None, ALU.add))
                    ins = v.scalar_tensor_tensor(aoT[:, k, LO, cols], aoF[:, k], vec[:, BV, k:k + 1], aoT[:, k, HI, cols],
                                                 ALU.add, ALU.subtract)
                ins.then_inc(ao_split, 1)

            def step(t, first, last):
                for n, (b, j) in enumerate(UNITS):
                    U = t * 8 + n
                    half = b // 2
                    dve.wait_ge(scores, U + 1)
                    own.link(v.tensor_reduce(nm[:, j], PS[:, 2 * j:2 * j + 2, 0:SK], AX.X, ALU.max, negate=True))
                    v.tensor_scalar(nb[:, j], nm[:, j], SM, PS_LN, ALU.mult, ALU.add).then_inc(negmax, 1)
                    if not (first and n == 0):
                        pt_low(U - 1)
                    if not (last and b == BT - 1):
                        kv_lo(U + 2, (b + 1) % 2, (b + 1) % BT, j)
                    if not (last and half == 1):
                        if n % 4 < 3:
                            spread_queries(t * 2 + (half + 1), 1 - half, (range(0, 3), range(3, 6), range(6, 8))[n % 4])
                        if n % 4 == 1:
                            need(dve, pv, t * 8 + 4 * half)
                            last_values_now(t + half, 1 - half)
                    if n == 2 and not first:
                        split_tile_out(t)
                    if not (first and n == 0):
                        mask_out(U - 1, UNITS[n - 1][1])

            attention_tiles(dve, step, own, 8 * 2 + 2)
            pt_low(8 * NT - 1)
            mask_out(8 * NT - 1, 1)
            split_tile_out(NT)
            after_attention_vector(dve, own)

        @block.tensor
        def _(pe):
            te = nc.tensor
            pe.wait_ge(cl_split, KC)
            pe.wait_ge(wa_ready, 1)
            for t in range(NT):
                n = 0
                for k in range(KC):
                    for a, b in PASSES:
                        ins = te.matmul(PS[:8, t // 2, D * (t % 2):D * (t % 2 + 1)], cl16[:, k, a, t], W16[:, k, b, WV:WV + D],
                                        start=n == 0, stop=n == 2 * len(PASSES) - 1)
                        n += 1
                if t % 2:
                    ins.then_inc(vl_ps, 1)
            pe.wait_ge(consts, 2)
            pe.wait_ge(vl_evac, NT // 2)
            for c in range(NC + 1):
                if c < NC:
                    pe.wait_ge(xn_ready, c + 1)
                    need(pe, xt_split, c - 1)
                    for k in range(KC):
                        for i in range(CT):
                            ins = te.transpose(PS[:, 2 * (c % 2) + k, P * i:P * (i + 1)], xn[:, c % 2, i, P * k:P * (k + 1)], ident)
                    ins.then_inc(xt_ps, 1)
                if c > 0:
                    pe.wait_ge(xt_split, c)
                    need(pe, q_split, c - 2)
                    for j in range(KC):
                        n = 0
                        for k in range(KC):
                            for a, b in PASSES:
                                ins = te.matmul(PS[:, 4 + 2 * ((c - 1) % 2) + j], W16[:, k, a, WQ + P * j:WQ + P * (j + 1)],
                                                xT[:, (c - 1) % 2, k, b], start=n == 0, stop=n == 5)
                                n += 1
                    ins.then_inc(q_ps, 1)

            def project_keys(n, par, j):
                need(pe, k_split, n)
                m = 0
                for k in range(KC):
                    for a, b in PASSES:
                        ins = te.matmul(PS[:, 4, 0:SK], W16[:, k, a, WK + P * j:WK + P * (j + 1)], ctx16[:, par, k, b, 0:SK],
                                        start=m == 0, stop=m == 5)
                        m += 1
                ins.then_inc(k_ps, 1)

            def project_values(n, par, j):
                need(pe, v_split, n)
                m = 0
                for k in range(KC):
                    for a, b in PASSES:
                        ins = te.matmul(PS[:, 5, 0:D], ctx16[:, par, k, a, P * j:P * (j + 1)], W16[:, k, b, WV:WV + D],
                                        start=m == 0, stop=m == 5)
                        m += 1
                ins.then_inc(v_ps, 1)

            pe.wait_ge(q_split, NC)
            pe.wait_ge(ctx_split, 1)
            for j in range(2):
                project_keys(j, 0, j)
                project_values(j, 0, j)

            def select_heads(Up, b, j):
                pe.wait_ge(o_split, Up + 1)
                for m, a in enumerate((HI, LO)):
                    ins = te.matmul(PS[:, 5, D + P * j + SQ * b:D + P * j + SQ * (b + 1)], Om16[:, (2 * b + j) % 4, a], sel16,
                                    start=m == 0, stop=m == 1)
                ins.then_inc(selected, 1)

            def transpose_probs(Up, b, j):
                pe.wait_ge(probs, Up + 1)
                pe.wait_ge(p_last, Up + 1)
                need(pe, o_masked, Up)
                for h in range(2):
                    for k in range(2):
                        te.transpose(PS[:, 6, P * (2 * h + k):P * (2 * h + k + 1)], Pr[:, j, h, P * k:P * (k + 1)], ident)
                te.transpose(PS[:8, 7, P:2 * P], plast[:, j, b].rearrange("p g c -> p (g c)"), ident).then_inc(pt_ps, 1)

            def outputs(Up, b, j):
                pe.wait_ge(pt_split, Up + 1)
                half = b // 2
                for h in range(2):
                    cols = slice(P * j + 64 * h, P * j + 64 * (h + 1))
                    terms = [(PT[:, a, P * (2 * h + k):P * (2 * h + k + 1)], Vt[:, b, k, c, cols]) for k in range(2) for a, c in PASSES]
                    terms += [(PTl[:8, a], vlc[:8, half, c, cols]) for a, c in PASSES]
                    for m, (lhs, rhs) in enumerate(terms):
                        ins = te.matmul(PS[:, 7, 64 * h:64 * (h + 1)], lhs, rhs, start=m == 0, stop=m == len(terms) - 1)
                ins.then_inc(pv, 1)

            def step(t, first, last):
                for n, (b, j) in enumerate(UNITS):
                    U = t * 8 + n
                    half = b // 2
                    if n % 4 == 0:
                        pe.wait_ge(qbd, t * 2 + (half + 1))
                        pe.wait_ge(vl_now, t * 2 + (half + 1))
                    pe.wait_ge(k_split, U + 1)
                    need(pe, probs, U - 1)
                    for h in range(2):
                        for m, (a, c) in enumerate(PASSES):
                            ins = te.matmul(PS[:, 2 * j + h, 0:SK], Qbd[:, half, 2 * j + a, b % 2, P * h:P * (h + 1)],
                                            Kt[:, b % 2, j, c, 0:SK], start=m == 0, stop=m == 2)
                    ins.then_inc(scores, 1)
                    if not (first and n == 0):
                        transpose_probs(U - 1, *UNITS[n - 1])
                    more = not (last and b == BT - 1)
                    if n == 1 and not first:
                        pe.wait_ge(v_split, U + 2)
                        select_heads(U - 2, *UNITS[n - 2])
                    if more:
                        if n % 2 == 0:
                            pe.wait_ge(ctx_split, t * 4 + (b + 2))
                        project_keys(U + 2, (b + 1) % 2, j)
                    if n == 1 and not first:
                        pe.wait_ge(ao_evac, t)
                    elif not (first and n < 2):
                        if more:
                            pe.wait_ge(v_split, U + 2)
                        select_heads(U - 2, *UNITS[n - 2])
                    if more:
                        project_values(U + 2, (b + 1) % 2, j)
                    if not (first and n == 0):
                        pe.wait_ge(v_split, (t * 8 + (n - 1) // 2 * 2 + 2) if n else t * 8)
                        outputs(U - 1, *UNITS[n - 1])

            attention_tiles(pe, step)
            U = 8 * NT
            transpose_probs(U - 1, BT - 1, 1)
            select_heads(U - 2, BT - 1, 0)
            outputs(U - 1, BT - 1, 1)
            select_heads(U - 1, BT - 1, 1)
            after_attention_tensor(pe)


def kernel(**inputs):
    import numpy as np
    import concourse.bacc as bacc
    from concourse.bass_utils import run_bass_kernel_spmd

    def a(name):
        return np.asarray(inputs[name])

    def layer(name):
        return a("L0_" + name)

    ctx = a("ctx_1024")
    last = ctx[:, SK - 1, :].reshape(NT, BT, KC, P).transpose(3, 2, 0, 1)
    w_all = np.concatenate(
        [layer("xattn_" + n).T for n in ("Wq", "Wk", "Wv", "Wo")]
        + [layer("attn_" + n) for n in ("W_key", "W_value", "W_recept", "W_out", "W_recept2", "W_key2")]
        + [layer("ffn_w_gate").T], axis=1)
    vecs = np.stack([layer(n) for n in (
        "xattn_bq", "xattn_bk", "xattn_bv", "attn_ln1_w", "attn_ln2_w", "attn_time_decay", "attn_time_first",
        "attn_time_mix_k", "attn_time_mix_v", "attn_time_mix_r", "attn_time_mix_k2", "attn_time_mix_r2")])
    host = {
        "x": a("x").reshape(TOK, D),
        "ctx_t": ctx.reshape(NB * SK, D).T,
        "ctx_last": np.concatenate([last, last], axis=3),
        "w_all": w_all,
        "w_value2": layer("attn_W_value2"),
        "vecs": vecs.reshape(NV, KC, P).transpose(2, 0, 1),
        "bo": layer("xattn_bo"),
        "w1": layer("ffn_W1"),
        "b1": layer("ffn_b1").reshape(NE, FC, P).transpose(0, 2, 1),
        "w2": layer("ffn_W2"),
        "b2": layer("ffn_b2"),
    }
    nc = bacc.Bacc("TRN2", target_bir_lowering=False, num_devices=1)
    arrays, args = {}, []
    for name, value in host.items():
        value = np.ascontiguousarray(value)
        arrays[f"in_{name}"] = value
        args.append(nc.dram_tensor(f"in_{name}", value.shape, mybir.dt.from_np(value.dtype), kind="ExternalInput").ap())
    args.append(nc.dram_tensor("out", (TOK, D), F32, kind="ExternalOutput").ap())
    perceiver_layer(nc, *args)
    r = run_bass_kernel_spmd(nc, [arrays], core_ids=[0])
    return r.results[0]["out"].reshape(NB, SQ, D)
```

```python
import concourse.bass as bass
from concourse import mybir
from contextlib import ExitStack

F32 = mybir.dt.float32
F16 = mybir.dt.float16
U32, I32 = mybir.dt.uint32, mybir.dt.int32
ALU = mybir.AluOpType
ACT = mybir.ActivationFunctionType
AX = mybir.AxisListType

NB, SQ, SK, D = 64, 32, 257, 256
NH, HD = 16, 16
P = 128
TOK = NB * SQ
NT = TOK // P
BT = P // SQ
KC = D // P
FF, NE = 1024, 8
FC = FF // P
CT = 4
CN = CT * P
NC = NT // CT
CB = CN // SQ
HI, LO = 0, 1
PASSES = ((HI, HI), (HI, LO), (LO, HI))

WS = 64.0
PS_LN = 8.317766166719343
SM = HD ** -0.5 / (WS * WS)

WQ, WK, WV, WO, WTK, WTV, WTR, WTO, WR2, WK2, WG = (0, 256, 512, 768, 1024, 1280, 1536, 1792, 2048, 2304, 3328)
NW = WG + NE
NWA = WTK
BQ, BK, BV, LN1, LN2, TD, TF, MK, MV, MR, MK2, MR2 = range(12)
NV = 12
RT = 2 * P
REG = TOK + RT
TPE = TOK // RT
NTILE = (2 * TOK + NE * (RT - 1)) // RT
R_BASE, R_TILE, R_AFTER, R_J = 0, NE, NE + TPE, NE + TPE + NE * NE
NRC = R_J + NTILE


class Trail:

    def __init__(self, eng, sem, wait=None):
        self.eng, self.sem, self.base, self.k = eng, sem, 0, 0
        self.wait = wait or (lambda eng, sem, n: eng.wait_ge(sem, n))

    def mark(self, ins):
        ins.then_inc(self.sem, 1)
        self.k += 1
        return self.base + self.k

    def link(self, ins):
        self.wait(self.eng, self.sem, self.mark(ins))

    def enter(self, i, per):
        self.outer, self.per = self.base + self.k, per
        self.base, self.k = self.outer + i * per, 0

    def leave(self, times):
        assert self.k == self.per, f"{self.k} steps of {self.sem}, not {self.per}"
        self.base, self.k = self.outer + times * self.per, 0

ARENA = 212800 // 4
DVE_RWKV = 71


def need(eng, sem, n):
    if not (isinstance(n, int) and n <= 0):
        eng.wait_ge(sem, n)


def perceiver_layer(nc, x, ctx_t, ctx_last, w_all, w_value2, vecs, bo, route_consts, w1, b1, w2, b2, out):
    stack = ExitStack()
    with stack:
        def sem(name):
            return stack.enter_context(nc.semaphore(name))

        routed = nc.dram_tensor("routed", (NE * REG, D), F32).ap()
        returned = nc.dram_tensor("returned", (NTILE * RT, D), F32).ap()

        arena = stack.enter_context(nc.sbuf_tensor("arena", [P, ARENA], F32))
        PS = stack.enter_context(nc.psum_tensor("PS", [P, 8, 512], F32))
        at = {}

        def place(name, off, shape, dt=F32):
            n = 1
            for s in shape:
                n *= s
            size = n * (2 if dt == F16 else 4)
            size = (size + 31) // 32 * 32
            assert off % 4 == 0 and off + size <= ARENA * 4, (name, off, size)
            flat = arena[:, off // 4:(off + size) // 4]
            if dt != F32:
                flat = flat.bitcast(dt)
            flat = flat[:, 0:n]
            at[name] = off + size
            if len(shape) == 1:
                return flat
            names = " ".join(f"d{i}" for i in range(len(shape)))
            return flat.rearrange(f"p ({names}) -> p {names}", **{f"d{i}": s for i, s in enumerate(shape)})

        W16 = place("W16", 0, [KC, 2, NW], F16)
        WV2 = place("WV2", at["W16"], [FC, 2, D], F16)
        x_all = place("x_all", at["WV2"], [NT, D])
        vec = place("vec", at["x_all"], [NV, KC])
        vec64 = place("vec64", at["vec"], [NV, KC])
        ident = place("ident", at["vec64"], [P])
        ident16 = place("ident16", at["ident"], [P], F16)
        neghalf = place("neghalf", at["ident16"], [NT])
        logits = place("logits", at["neghalf"], [NT, NE])
        gate = place("gate", at["logits"], [NT, NE])
        rank = place("rank", at["gate"], [NT, NE])
        row_of = place("row_of", at["rank"], [NT, NE])
        taken = place("taken", at["row_of"], [NT, NE], F16)
        before = place("before", at["taken"], [NT + 1, NE], F16)
        picked = place("picked", at["before"], [2, CT, NE])
        rows_f = place("rows_f", at["picked"], [2, CT])
        rows_u = place("rows_u", at["rows_f"], [2, CT], U32)
        mx = place("mx", at["rows_u"], [CT])
        rc = place("rc", at["mx"], [NRC])
        earlier = place("earlier", at["rc"], [P], F16)
        ones16 = place("ones16", at["earlier"], [P], F16)
        aoT = place("aoT", at["ones16"], [KC, 2, TOK], F16)
        A0 = at["aoT"]
        qT = place("qT", A0, [KC, 2, TOK], F16)
        vlast = place("vlast", at["qT"], [NT, 2, D], F16)
        ctxf = place("ctxf", at["vlast"], [BT, KC, SK])
        ctx16 = place("ctx16", at["ctxf"], [2, KC, 2, SK + 1], F16)
        Kt = place("Kt", at["ctx16"], [2, 2, 2, SK + 1], F16)
        Vt = place("Vt", at["Kt"], [BT, 2, 2, D], F16)
        Pr = place("Pr", at["Vt"], [2, 2, SK])
        PT = place("PT", at["Pr"], [2, 4 * P], F16)
        PTl = place("PTl", at["PT"], [2, P], F16)
        plast = place("plast", at["PTl"], [2, BT, 2, BT])
        Qbd = place("Qbd", at["plast"], [2, 4, 2, 8 * SQ], F16)
        vlc = place("vlc", at["Qbd"], [2, 2, D], F16)
        Om = place("Om", at["vlc"], [2, P])
        Om16 = place("Om16", at["Om"], [4, 2, P], F16)
        aoF = place("aoF", at["Om16"], [KC, P])
        nm = place("nm", at["aoF"], [2, 2])
        nb = place("nb", at["nm"], [2, 2])
        den = place("den", at["nb"], [2, 2])
        rec = place("rec", at["den"], [2, 2])
        mask8 = place("mask8", at["rec"], [8])
        maskO = place("maskO", at["mask8"], [4, HD])
        maskV = place("maskV", at["maskO"], [2, 2, 64])
        sel16 = place("sel16", at["maskV"], [SQ], F16)
        S0 = at["sel16"]
        stage = place("stage", S0, [KC, NW])
        stage2 = place("stage2", at["stage"], [FC, D])
        xn = place("xn", at["stage2"], [2, CT, D])
        xT = place("xT", at["xn"], [2, KC, 2, CN], F16)
        clf = place("clf", at["xT"], [KC, NT, 8])
        cl16 = place("cl16", at["clf"], [KC, 2, NT, 8], F16)
        vlf = place("vlf", at["cl16"], [2, 2, D])
        bo_bc = place("bo_bc", at["vlf"], [D])
        st0 = place("st0", at["bo_bc"], [NT, 6])
        mv0 = place("mv0", at["st0"], [NT, 2])
        ve0 = place("ve0", at["mv0"], [NT])
        rs0 = place("rs0", at["ve0"], [NT])

        vecs_in, wa_in, wb_in, bo_in, rc_in, cl_in = sem("vecs_in"), sem("wa_in"), sem("wb_in"), sem("bo_in"), sem("rc_in"), sem("cl_in")
        x_in = [sem(f"x_in{c}") for c in range(NC)]
        ctx_in = [sem(f"ctx_in{b}") for b in range(BT)]
        consts, wa_ready, wb_ready = sem("consts"), sem("wa_ready"), sem("wb_ready")
        var_ready, rstd_ready, xn_ready = sem("var_ready"), sem("rstd_ready"), sem("xn_ready")
        xt_ps, xt_hi, xt_split = sem("xt_ps"), sem("xt_hi"), sem("xt_split")
        q_ps, q_hi, q_split = sem("q_ps"), sem("q_hi"), sem("q_split")
        cl_split, vl_ps, vl_evac, vl_split = sem("cl_split"), sem("vl_ps"), sem("vl_evac"), sem("vl_split")
        ctx_split = sem("ctx_split")
        k_ps, k_hi, k_split = sem("k_ps"), sem("k_hi"), sem("k_split")
        v_ps, v_hi, v_split = sem("v_ps"), sem("v_hi"), sem("v_split")
        qbd, vl_now, scores, negmax, probs, p_last = sem("qbd"), sem("vl_now"), sem("scores"), sem("negmax"), sem("probs"), sem("p_last")
        pt_ps, pt_hi, pt_split, pv = sem("pt_ps"), sem("pt_hi"), sem("pt_split"), sem("pv")
        o_masked, o_split, selected, ao_evac, ao_split = sem("o_masked"), sem("o_split"), sem("selected"), sem("ao_evac"), sem("ao_split")
        xbo_ready = sem("xbo_ready")
        dve_step, act_step, pool_step = sem("dve_step"), sem("act_step"), sem("pool_step")

        wait_value = {}

        def wait_apart(eng, sem, n):
            if not isinstance(n, int):
                if eng not in wait_value:
                    wait_value[eng] = eng.alloc_register("wait_value")
                eng.reg_mov(wait_value[eng], n)
                n = wait_value[eng]
                eng.wait_ge(consts, 1)
            eng.wait_ge(sem, n)


        h2T = place("h2T", A0, [KC, CB, SQ + 1])
        d2T = place("d2T", at["h2T"], [KC, CN])
        h2N = place("h2N", at["d2T"], [CT, D])
        mix2f = place("mix2f", at["h2N"], [2, CN])
        mix216 = place("mix216", at["mix2f"], [2, KC, 2, CN], F16)
        r2N = place("r2N", at["mix216"], [CT, D])
        reluf = place("reluf", at["r2N"], [2, CN])
        sqf = place("sqf", at["reluf"], [2, CN])
        k216 = place("k216", at["sqf"], [FC, 2, CN], F16)
        st3 = place("st3", at["k216"], [CT, 6])
        mv3 = place("mv3", at["st3"], [CT, 2])
        ve3 = place("ve3", at["mv3"], [CT])
        rs3 = place("rs3", at["ve3"], [CT])
        ew = place("ew", at["rs3"], [2, KC])
        st1 = place("st1", at["ew"], [CT, 6])
        mv1 = place("mv1", at["st1"], [CT, 2])
        ve1 = place("ve1", at["mv1"], [2, CT])
        rs1 = place("rs1", at["ve1"], [2, CT])
        shift1 = place("shift1", at["rs1"], [CT])
        st2 = place("st2", at["shift1"], [CT, 6])
        mv2 = place("mv2", at["st2"], [CT, 2])
        ve2 = place("ve2", at["mv2"], [CT])
        rs2 = place("rs2", at["ve2"], [CT])
        xl = place("xl", at["rs2"], [CT, D])
        hN = place("hN", at["xl"], [CT, D])
        hT = place("hT", at["hN"], [KC, CB, SQ + 1])
        dT = place("dT", at["hT"], [KC, CN])
        mixf = place("mixf", at["dT"], [2, CN])
        mix16 = place("mix16", at["mixf"], [3, KC, 2, CN], F16)
        ek = place("ek", at["mix16"], [KC, CN])
        eu = place("eu", at["ek"], [KC, CN])
        vS = place("vS", at["eu"], [KC, CN])
        rS = place("rS", at["vS"], [KC, CN])
        ekp = place("ekp", at["rS"], [KC, CB, SQ + 1])
        ekvp = place("ekvp", at["ekp"], [KC, CB, SQ + 1])
        num = place("num", at["ekvp"], [2, CB, SQ + 1])
        dnm = place("dnm", at["num"], [2, CB, SQ + 1])
        top = place("top", at["dnm"], [2, CN])
        bot = place("bot", at["top"], [2, CN])
        rw16 = place("rw16", at["bot"], [KC, 2, CN], F16)
        decay = place("decay", at["rw16"], [KC, CB, SQ + 1])
        cmp1 = reluf.rearrange("p a n -> p (a n)")[:, :CT * NE * NE].rearrange("p (t e j) -> p t e j", e=NE, j=NE)
        cmp2 = sqf.rearrange("p a n -> p (a n)")[:, :CT * NE * NE].rearrange("p (t e j) -> p t e j", e=NE, j=NE)
        euv = dT
        yN = hN
        zN = d2T.rearrange("p k n -> p (k n)").rearrange("p (t n) -> p t n", t=CT)
        xn3 = zN
        x3T = mix2f.rearrange("p a n -> p (a n)").bitcast(F16).rearrange("p (k a n) -> p k a n", k=KC, a=2)

        W2_AT = KC * 2 * FF
        experts = place("experts", ARENA * 4 - NE * 2 * W2_AT * 2, [NE, 2 * W2_AT], F16)
        w1f = place("w1f", at["ones16"], [KC, FF])
        w2f = place("w2f", at["w1f"], [FC, D])

        (sm_in, sm_exp, before_ready, count_ps, total_ps, rows_ready, routed_sent, w1_in, w2_in, w1_ready, w2_ready) = [sem(n) for n in (
            "sm_in sm_exp before_ready count_ps total_ps rows_ready routed_sent w1_in w2_in w1_ready w2_ready").split()]
        (c_ew, wo_ps, tm_x, tm_var, tm_rs, tm_norm, h_ps, h_t, d_t, mixed, mix_hi, mix_lo, kvr_ps, kvr_out, eu_v, rwf, rw_hi, rw_lo,
         wout_ps, y_var, y_rs, y_done, h2_n, h2_ps, h2_t, d2_t, mixed2, mix2_hi, mix2_lo, key_ps, relu_out, sq_out, k2_hi, k2_lo, r2_ps, r2_out,
         val_ps, z_out, x2_var, x2_rs, xn3_done, x3_ps, x3_hi, x3_lo, lg_ps, lg_out) = [sem(n) for n in (
            "c_ew wo_ps tm_x tm_var tm_rs tm_norm h_ps h_t d_t mixed mix_hi mix_lo kvr_ps kvr_out eu_v rwf rw_hi rw_lo "
            "wout_ps y_var y_rs y_done h2_n h2_ps h2_t d2_t mixed2 mix2_hi mix2_lo key_ps relu_out sq_out k2_hi k2_lo r2_ps r2_out "
            "val_ps z_out x2_var x2_rs xn3_done x3_ps x3_hi x3_lo lg_ps lg_out").split()]

        def chunk_steps(eng, step, trail=None, per=0):
            step(0, True, False)
            with eng.Fori(1, NC) as s:
                if trail:
                    trail.enter(s - 1, per)
                step(s, True, True)
            if trail:
                trail.leave(NC - 1)
            step(NC, False, True)

        def tiles_of(s, i, n):
            return x_all[:, bass.ds(s * CT + i, n)]

        def rwkv_pool(pool, own):
            g = nc.gpsimd

            def times(out, a, b, op=ALU.mult):
                return g.tensor_tensor(out, a, b, op)

            def load_w1(e):
                g.dma_start(w1f, w1[e].rearrange("(k p) f -> p k f", p=P)).then_inc(w1_in, 16)

            def load_w2(e):
                g.dma_start(w2f, w2[e].rearrange("(f p) d -> p f d", p=P)).then_inc(w2_in, 16)

            def split(f32, hi, lo, ready):
                own.link(g.tensor_scalar(f32, f32, WS, 0.0, ALU.mult, ALU.add))
                own.link(g.tensor_scalar(hi, f32, 1.0, 0.0, ALU.mult, ALU.add))
                g.tensor_tensor(lo, f32, hi, ALU.subtract).then_inc(ready, 1)

            def split_w1(e):
                pool.wait_ge(w1_in, 16 * (NE - e))
                w = experts[:, e, 0:W2_AT].rearrange("p (k a f) -> p k a f", k=KC, a=2)
                split(w1f, w[:, :, HI], w[:, :, LO], w1_ready)
                if e:
                    pool.wait_ge(w1_ready, NE - e)
                    load_w1(e - 1)

            def split_w2(e):
                pool.wait_ge(w2_in, 16 * (NE - e))
                w = experts[:, e, W2_AT:].rearrange("p (f a d) -> p f a d", f=FC, a=2)
                split(w2f, w[:, :, HI], w[:, :, LO], w2_ready)
                if e:
                    pool.wait_ge(w2_ready, NE - e)
                    load_w2(e - 1)

            def step(s, tm, cm):
                if not tm:
                    pool.wait_ge(wo_ps, 2 * NC)
                    load_w1(NE - 1)
                    load_w2(NE - 1)
                if tm:
                    pool.wait_ge(tm_var, s + 1)
                    g.tensor_tensor(rs1, ve1, neghalf[:, 0:2 * CT].rearrange("p (a b) -> p a b", a=2), ALU.pow).then_inc(tm_rs, 1)
                    pool.wait_ge(h_t, s + 1)
                    for k in range(KC):
                        ins = times(dT[:, k].rearrange("p (b q) -> p b q", q=SQ), hT[:, k, :, 1:], hT[:, k, :, 0:SQ], ALU.subtract)
                    ins.then_inc(d_t, 1)
                if cm:
                    pool.wait_ge(h2_t, s)
                    for k in range(KC):
                        ins = times(d2T[:, k].rearrange("p (b q) -> p b q", q=SQ), h2T[:, k, :, 1:], h2T[:, k, :, 0:SQ], ALU.subtract)
                    ins.then_inc(d2_t, 1)
                if cm:
                    for m in range(2):
                        for k in range(KC):
                            pool.wait_ge(mix2_hi, s * 4 + (2 * m + k + 1 - 4))
                            times(mix216[:, m, k, LO], mix2f[:, k], mix216[:, m, k, HI], ALU.subtract).then_inc(mix2_lo, 1)
                if tm:
                    for m in range(3):
                        for k in range(KC):
                            pool.wait_ge(mix_hi, s * 6 + (2 * m + k + 1))
                            times(mix16[:, m, k, LO], mixf[:, k], mix16[:, m, k, HI], ALU.subtract).then_inc(mix_lo, 1)
                if cm:
                    for f in range(0, FC):
                        pool.wait_ge(k2_hi, s * 8 + (f + 1 - 8))
                        times(k216[:, f, LO], sqf[:, f % 2], k216[:, f, HI], ALU.subtract).then_inc(k2_lo, 1)
                if tm:
                    for o in range(KC):
                        pool.wait_ge(eu_v, s * 2 + (o + 1))
                        times(euv[:, o], eu[:, o], vS[:, o]).then_inc(rwf, 1)
                if tm:
                    for o in range(KC):
                        pool.wait_ge(rw_hi, s * 2 + (o + 1))
                        times(rw16[:, o, LO], top[:, o], rw16[:, o, HI], ALU.subtract).then_inc(rw_lo, 1)
                if cm and not tm:
                    split_w1(NE - 1)
                if cm:
                    pool.wait_ge(x2_var, s)
                    g.tensor_tensor(rs3, ve3, neghalf[:, 0:CT], ALU.pow).then_inc(x2_rs, 1)
                if tm:
                    pool.wait_ge(y_var, s + 1)
                    g.tensor_tensor(rs2, ve2, neghalf[:, 0:CT], ALU.pow).then_inc(y_rs, 1)
                if cm and not tm:
                    split_w2(NE - 1)
                if cm:
                    wait_apart(pool, rows_ready, s)
                    if not tm:
                        g.memset(zeros, 0.0).then_inc(zeros_ready, 1)
                    for c in range(2):
                        for i in range(CT):
                            g.indirect_dma_start(routed, bass.IndirectOffsetOnAxis(ap=rows_u[:, c, i:i + 1], axis=0), xn3[:, i], None
                                                 ).then_inc(routed_sent, 16)
                    wait_apart(pool, routed_sent, s * (2 * CT * 16))

            chunk_steps(pool, step)
            return split_w1, split_w2

        def rwkv_scalar(act):
            a = nc.scalar
            pad = lambda t, k: t[:, k, :, 1:]
            fold = lambda ap: ap.rearrange("p (b q) -> p b q", q=SQ)
            a.activation(ew[:, 0], vec[:, TD], ACT.Exp).then_inc(c_ew, 1)
            act.wait_ge(c_ew, 2)
            a.activation(ew[:, 1], ew[:, 0], ACT.Exp).then_inc(c_ew, 1)

            def step(s, tm, cm):
                if tm:
                    act.wait_ge(tm_norm, s + 1)
                    need(act, h2_n, s)
                    for i in range(CT):
                        ins = a.activation(hN[:, i], tiles_of(s, i, 1).squeeze(1), ACT.Identity, bias=shift1[:, i:i + 1], scale=rs1[:, 1, i:i + 1])
                    ins.then_inc(hn_done, 1)
                    act.wait_ge(h_ps, s + 1)
                    for k in range(KC):
                        ins = a.activation(pad(hT, k), fold(PS[:, 2 + k]), ACT.Copy, scale=vec[:, LN1, k:k + 1])
                    ins.then_inc(h_t, 1)
                if cm:
                    act.wait_ge(h2_ps, s)
                    for k in range(KC):
                        ins = a.activation(pad(h2T, k), fold(PS[:, 4 + k]), ACT.Copy, scale=vec[:, LN2, k:k + 1])
                    ins.then_inc(h2_t, 1)
                if cm:
                    for m in range(2):
                        for k in range(KC):
                            act.wait_ge(mixed2, s * 4 + (2 * m + k + 1 - 4))
                            a.activation(mix216[:, m, k, HI], mix2f[:, k], ACT.Copy).then_inc(mix2_hi, 1)
                if tm:
                    for m in range(3):
                        for k in range(KC):
                            act.wait_ge(mixed, s * 6 + (2 * m + k + 1))
                            a.activation(mix16[:, m, k, HI], mixf[:, k], ACT.Copy).then_inc(mix_hi, 1)
                if tm:
                    for o in range(KC):
                        act.wait_ge(kvr_ps, s * 6 + (o + 1))
                        a.activation(ek[:, o], PS[:, o], ACT.Exp, scale=1 / WS)
                        a.activation(eu[:, o], PS[:, o], ACT.Exp, scale=1 / WS, bias=vec[:, TF, o:o + 1]).then_inc(kvr_out, 1)
                    for o in range(KC):
                        act.wait_ge(kvr_ps, s * 6 + (o + 3))
                        a.activation(vS[:, o], PS[:, 2 + o], ACT.Copy, scale=1 / WS).then_inc(kvr_out, 1)
                    for o in range(KC):
                        act.wait_ge(kvr_ps, s * 6 + (o + 5))
                        a.activation(rS[:, o], PS[:, o], ACT.Tanh, scale=0.5 / WS).then_inc(kvr_out, 1)
                if cm:
                    for p in range(2):
                        act.wait_ge(r2_ps, s * 2 + (p + 1 - 2))
                        a.activation(r2N[:, 2 * p:2 * p + 2], PS[:, 6 + p].rearrange("p (a n) -> p a n", a=2), ACT.Tanh,
                                     scale=0.5 / WS).then_inc(r2_out, 1)

                    def relu(f):
                        act.wait_ge(key_ps, s * 8 + (f + 1 - 8))
                        if f >= 2:
                            act.wait_ge(sq_out, s * 8 + (f - 1 - 8))
                        a.activation(reluf[:, f % 2], PS[:, 4 + f % 4], ACT.Relu, scale=1 / WS).then_inc(relu_out, 1)

                    def square_hi(f):
                        act.wait_ge(sq_out, s * 8 + (f + 1 - 8))
                        a.activation(k216[:, f, HI], sqf[:, f % 2], ACT.Copy).then_inc(k2_hi, 1)

                    relu(0)
                    for f in range(1, FC):
                        relu(f)
                        square_hi(f - 1)
                    square_hi(FC - 1)
                if tm:
                    for o in range(KC):
                        act.wait_ge(top_ready, s * 2 + (o + 1))
                        a.activation(rw16[:, o, HI], top[:, o], ACT.Copy).then_inc(rw_hi, 1)
                    act.wait_ge(y_rs, s + 1)
                    for i in range(CT):
                        ins = a.activation(h2N[:, i], yN[:, i], ACT.Copy, scale=rs2[:, i:i + 1])
                    ins.then_inc(h2_n, 1)
                if cm:
                    act.wait_ge(x3_ps, s)
                    for k in range(KC):
                        ins = a.activation(x3T[:, k, HI], PS[:, 6 + k], ACT.Copy)
                    ins.then_inc(x3_hi, 1)
                    act.wait_ge(lg_ps, s)
                    a.activation(logits[:, bass.ds(s * CT - CT, CT)], PS[:, 4, 0:CT * NE].rearrange("p (t e) -> p t e", e=NE),
                                 ACT.Copy, scale=1 / WS).then_inc(lg_out, 1)
                    act.wait_ge(sm_in, s)
                    chunk = gate[:, bass.ds(s * CT - CT, CT)]
                    a.activation(chunk, chunk, ACT.Exp).then_inc(sm_exp, 1)

            chunk_steps(act, step)

        top_ready, hn_done = sem("top_ready"), sem("hn_done")
        E20, EM20 = 485165195.4097903, 2.061153622438558e-09

        def rwkv_vector(dve, own):
            v = nc.vector
            fold = lambda ap: ap.rearrange("p (b q) -> p b q", q=SQ)
            for t in (hT, h2T, ekp, ekvp):
                v.memset(t[:, :, :, 0:1], 0.0)
            own.link(v.memset(decay, 0.0))
            dve.wait_ge(c_ew, 1)
            v.tensor_scalar(ew[:, 0], ew[:, 0], -1.0, -20.0, ALU.mult, ALU.max).then_inc(c_ew, 1)
            dve.wait_ge(c_ew, 3)
            own.link(v.tensor_copy(decay[:, :, :, 1:], ew[:, 1].unsqueeze(2).unsqueeze(3).to_broadcast([P, KC, CB, SQ])))

            def stats(st, mv, src):
                for i in range(CT):
                    n = own.mark(v.bn_stats(st[:, i], src(i)))
                wait_apart(dve, dve_step, n)
                for i in range(CT):
                    n = own.mark(v.bn_aggr(mv[:, i], st[:, i]))
                dve.wait_ge(dve_step, n)

            def route(s):
                tiles = bass.ds(s * CT - CT, CT)
                bc_e = lambda t: t.unsqueeze(2).to_broadcast([P, CT, NE])
                full = [P, CT, NE, NE]
                wait_apart(dve, lg_out, s)
                own.link(v.tensor_reduce(mx, logits[:, tiles], AX.X, ALU.max))
                v.tensor_tensor(gate[:, tiles], logits[:, tiles], bc_e(mx), ALU.subtract).then_inc(sm_in, 1)
                wait_apart(dve, sm_exp, s)
                own.link(v.tensor_reduce(mx, gate[:, tiles], AX.X, ALU.add))
                own.link(v.reciprocal(mx, mx))
                own.link(v.tensor_tensor(gate[:, tiles], gate[:, tiles], bc_e(mx), ALU.mult))
                of_j, of_e = gate[:, tiles].unsqueeze(2).to_broadcast(full), gate[:, tiles].unsqueeze(3).to_broadcast(full)
                own.mark(v.tensor_tensor(cmp1, of_j, of_e, ALU.is_gt))
                own.link(v.tensor_tensor(cmp2, of_j, of_e, ALU.is_equal))
                own.link(v.tensor_tensor(cmp2, cmp2, lower.unsqueeze(1).to_broadcast(full), ALU.mult))
                wait_apart(dve, dve_step, own.mark(v.tensor_tensor(cmp1, cmp1, cmp2, ALU.add)))
                own.link(v.tensor_reduce(rank[:, tiles], cmp1, AX.X, ALU.add))
                n = own.mark(v.tensor_scalar(taken[:, tiles], rank[:, tiles], 2.0, None, ALU.is_lt))
                wait_apart(dve, dve_step, n)
                for i in range(CT):
                    ins = v.tensor_tensor(before[:, bass.ds(s * CT + (i + 1 - CT), 1)], before[:, bass.ds(s * CT + (i - CT), 1)],
                                          taken[:, bass.ds(s * CT + (i - CT), 1)], ALU.add)
                    if i < CT - 1:
                        own.link(ins)
                ins.then_inc(before_ready, 1)
                dve.wait_ge(count_ps, s)
                counts = PS[:, 4, 64:64 + CT * NE].rearrange("p (t e) -> p t e", e=NE)
                own.link(v.tensor_tensor(row_of[:, tiles], counts, rc[:, R_BASE:R_BASE + NE].unsqueeze(1).to_broadcast([P, CT, NE]), ALU.add))
                own.mark(v.scalar_tensor_tensor(picked[:, 0], rank[:, tiles], 0.0, row_of[:, tiles], ALU.is_equal, ALU.mult))
                own.link(v.scalar_tensor_tensor(picked[:, 1], rank[:, tiles], 1.0, row_of[:, tiles], ALU.is_equal, ALU.mult))
                own.link(v.tensor_reduce(rows_f, picked, AX.X, ALU.add))
                v.tensor_copy(rows_u, rows_f).then_inc(rows_ready, 1)

            lower = rc[:, R_AFTER:R_AFTER + NE * NE].rearrange("p (e j) -> p e j", j=NE)
            own.link(v.memset(before[:, 0:1], 0.0))

            def step(s, tm, cm):
                if tm:
                    for p in range(2):
                        dve.wait_ge(wo_ps, s * 2 + (p + 1))
                        rows = tiles_of(s, 2 * p, 2)
                        n = own.mark(v.scalar_tensor_tensor(rows, PS[:, p].rearrange("p (a n) -> p a n", a=2), 1 / WS, rows, ALU.mult, ALU.add))
                    wait_apart(dve, dve_step, n)
                    stats(st1, mv1, lambda i: tiles_of(s, i, 1).squeeze(1))
                    own.mark(v.tensor_scalar(ve1[:, 0], mv1[:, :, 1], 1e-5, None, ALU.add))
                    v.tensor_scalar(ve1[:, 1], mv1[:, :, 1], 1.0 + 1e-6, 1e-11, ALU.mult, ALU.add).then_inc(tm_var, 1)
                    dve.wait_ge(tm_rs, s + 1)
                    v.scalar_tensor_tensor(shift1, mv1[:, :, 0], -1.0, rs1[:, 1], ALU.mult, ALU.mult).then_inc(tm_norm, 1)
                    for i in range(CT):
                        n = own.mark(v.tensor_scalar(xl[:, i], tiles_of(s, i, 1).squeeze(1), mv1[:, i, 0:1], rs1[:, 0, i:i + 1], ALU.subtract, ALU.mult))
                if cm:
                    dve.wait_ge(d2_t, s)
                    for m, mix in ((0, MK2), (1, MR2)):
                        for k in range(KC):
                            if m:
                                dve.wait_ge(mix2_lo, s * 4 + (2 * m + k - 1 - 4))
                            v.scalar_tensor_tensor(fold(mix2f[:, k]), fold(d2T[:, k]), vec[:, mix, k:k + 1], h2T[:, k, :, 0:SQ],
                                                   ALU.mult, ALU.add).then_inc(mixed2, 1)
                if tm:
                    dve.wait_ge(d_t, s + 1)
                    for m, mix in ((0, MK), (1, MV), (2, MR)):
                        for k in range(KC):
                            if m:
                                dve.wait_ge(mix_lo, s * 6 + (2 * m + k - 1))
                            v.scalar_tensor_tensor(fold(mixf[:, k]), fold(dT[:, k]), vec[:, mix, k:k + 1], hT[:, k, :, 0:SQ],
                                                   ALU.mult, ALU.add).then_inc(mixed, 1)
                if cm:
                    for f in range(FC):
                        dve.wait_ge(relu_out, s * 8 + (f + 1 - 8))
                        if f >= 2:
                            dve.wait_ge(k2_lo, s * 8 + (f - 1 - 8))
                        v.tensor_tensor(sqf[:, f % 2], reluf[:, f % 2], reluf[:, f % 2], ALU.mult).then_inc(sq_out, 1)
                if tm:
                    for o in range(KC):
                        dve.wait_ge(kvr_out, s * 6 + (o + 1))
                        own.mark(v.tensor_scalar(ekp[:, o, :, 1:], fold(ek[:, o]), EM20, E20, ALU.max, ALU.min))
                        own.link(v.tensor_scalar(eu[:, o], eu[:, o], EM20, E20, ALU.max, ALU.min))
                        dve.wait_ge(kvr_out, s * 6 + (o + 3))
                        own.mark(v.tensor_tensor(ekvp[:, o, :, 1:], ekp[:, o, :, 1:], fold(vS[:, o]), ALU.mult))
                        v.tensor_tensor_scan(dnm[:, o].rearrange("p b q -> p (b q)"), decay[:, o].rearrange("p b q -> p (b q)"),
                                             ekp[:, o].rearrange("p b q -> p (b q)"), 0.0, ALU.mult, ALU.add).then_inc(eu_v, 1)
                        dve.wait_ge(eu_v, s * 2 + (o + 1))
                        own.mark(v.scalar_tensor_tensor(fold(bot[:, o]), dnm[:, o, :, 0:SQ], 1e-8, fold(eu[:, o]), ALU.add, ALU.add))
                        own.link(v.tensor_tensor_scan(num[:, o].rearrange("p b q -> p (b q)"), decay[:, o].rearrange("p b q -> p (b q)"),
                                                      ekvp[:, o].rearrange("p b q -> p (b q)"), 0.0, ALU.mult, ALU.add))
                        own.mark(v.reciprocal(bot[:, o], bot[:, o]))
                        dve.wait_ge(rwf, s * 2 + (o + 1))
                        own.link(v.tensor_tensor(fold(top[:, o]), num[:, o, :, 0:SQ], fold(euv[:, o]), ALU.add))
                        own.link(v.tensor_tensor(top[:, o], top[:, o], bot[:, o], ALU.mult))
                        dve.wait_ge(kvr_out, s * 6 + (o + 5))
                        v.scalar_tensor_tensor(top[:, o], rS[:, o], 1.0, top[:, o], ALU.add, ALU.mult).then_inc(top_ready, 1)
                if cm:
                    dve.wait_ge(r2_out, s * 2)
                    for p in range(2):
                        dve.wait_ge(val_ps, s * 2 + (p + 1 - 2))
                        n = own.mark(v.scalar_tensor_tensor(zN[:, 2 * p:2 * p + 2], r2N[:, 2 * p:2 * p + 2], 1.0,
                                                            PS[:, 4 + p].rearrange("p (a n) -> p a n", a=2), ALU.add, ALU.mult))
                    dve.wait_ge(dve_step, n)
                    rows = tiles_of(s, -CT, CT)
                    n = own.mark(v.scalar_tensor_tensor(rows, zN, 0.5 / WS, rows, ALU.mult, ALU.add))
                    wait_apart(dve, dve_step, n)
                    stats(st3, mv3, lambda i: tiles_of(s, i - CT, 1).squeeze(1))
                    v.tensor_scalar(ve3, mv3[:, :, 1], 1e-5, None, ALU.add).then_inc(x2_var, 1)
                if tm:
                    for p in range(2):
                        dve.wait_ge(wout_ps, s * 2 + (p + 1))
                        pair = slice(2 * p, 2 * p + 2)
                        n = own.mark(v.scalar_tensor_tensor(yN[:, pair], PS[:, 2 + p].rearrange("p (a n) -> p a n", a=2), 0.5 / WS, xl[:, pair],
                                                            ALU.mult, ALU.add))
                    wait_apart(dve, dve_step, n)
                    stats(st2, mv2, lambda i: yN[:, i])
                    own.link(v.tensor_tensor(ve2, mv2[:, :, 0], mv2[:, :, 0], ALU.mult))
                    v.scalar_tensor_tensor(ve2, ve2, 1e-6, mv2[:, :, 1], ALU.add, ALU.add).then_inc(y_var, 1)
                    rows = tiles_of(s, 0, CT)
                    own.mark(v.tensor_tensor(rows, rows, yN, ALU.add))
                if cm:
                    dve.wait_ge(x2_rs, s)
                    for i in range(CT):
                        ins = v.tensor_scalar(xn3[:, i], tiles_of(s, i - CT, 1).squeeze(1), mv3[:, i, 0:1], rs3[:, i:i + 1], ALU.subtract, ALU.mult)
                    ins.then_inc(xn3_done, 1)
                    dve.wait_ge(x3_hi, s)
                    for k in range(KC):
                        ins = v.tensor_tensor(x3T[:, k, LO], PS[:, 6 + k], x3T[:, k, HI], ALU.subtract)
                    ins.then_inc(x3_lo, 1)
                    route(s)

            chunk_steps(dve, step, own, DVE_RWKV)

        def rwkv_tensor(pe):
            te = nc.tensor

            def product(out, pairs):
                n, last = 0, 3 * len(pairs) - 1
                for lhs, rhs in pairs:
                    for a, b in PASSES:
                        ins = te.matmul(out, lhs(a), rhs(b), start=n == 0, stop=n == last)
                        n += 1
                return ins

            def w(k, col, n=P):
                return lambda part: W16[:, k, part, col:col + n]

            def step(s, tm, cm):
                if tm:
                    pe.wait_ge(ao_split, s * CT + CT)
                    need(pe, kvr_out, s * 6)
                    for i in range(CT):
                        ins = product(PS[:, i // 2, D * (i % 2):D * (i % 2 + 1)],
                                      [((lambda part, k=k: aoT[:, k, part, bass.ds(s * CN + i * P, P)]), w(k, WO, D)) for k in range(KC)])
                        if i % 2:
                            ins.then_inc(wo_ps, 1)
                if cm:
                    pe.wait_ge(h2_n, s)
                    if tm:
                        pe.wait_ge(hn_done, s + 1)
                    else:
                        pe.wait_ge(rows_ready, s - 1)
                    for k in range(KC):
                        for i in range(CT):
                            ins = te.transpose(PS[:, 4 + k, P * i:P * (i + 1)], h2N[:, i, P * k:P * (k + 1)], ident)
                    ins.then_inc(h2_ps, 1)
                if tm:
                    pe.wait_ge(hn_done, s + 1)
                    need(pe, y_var, s)
                    for k in range(KC):
                        for i in range(CT):
                            ins = te.transpose(PS[:, 2 + k, P * i:P * (i + 1)], hN[:, i, P * k:P * (k + 1)], ident)
                    ins.then_inc(h_ps, 1)
                if tm:
                    pe.wait_ge(tm_var, s + 1)
                    for m, col in ((0, WTK), (1, WTV), (2, WTR)):
                        pe.wait_ge(mix_lo, s * 6 + (2 * m + 2))
                        for o in range(KC):
                            if m == 2:
                                pe.wait_ge(kvr_out, s * 6 + (o + 1))
                            product(PS[:, (2 * m + o) % 4], [(w(k, col + P * o), lambda part, k=k: mix16[:, m, k, part]) for k in range(KC)]
                                    ).then_inc(kvr_ps, 1)
                if cm:
                    pe.wait_ge(mix2_lo, s * 4)
                    for i in range(CT):
                        ins = product(PS[:, 6 + i // 2, D * (i % 2):D * (i % 2 + 1)],
                                      [(lambda part, k=k: mix216[:, 1, k, part, P * i:P * (i + 1)], w(k, WR2, D)) for k in range(KC)])
                        if i % 2:
                            ins.then_inc(r2_ps, 1)
                    for f in range(FC):
                        if f == 2:
                            pe.wait_ge(r2_out, s * 2)
                        if f >= 4:
                            pe.wait_ge(relu_out, s * 8 + (f - 3 - 8))
                        product(PS[:, 4 + f % 4], [(w(k, WK2 + P * f), lambda part, k=k: mix216[:, 0, k, part]) for k in range(KC)]
                                ).then_inc(key_ps, 1)
                if tm:
                    pe.wait_ge(rw_lo, s * 2 + 2)
                    pe.wait_ge(kvr_out, s * 6 + 4)
                    for i in range(CT):
                        ins = product(PS[:, 2 + i // 2, D * (i % 2):D * (i % 2 + 1)],
                                      [(lambda part, k=k: rw16[:, k, part, P * i:P * (i + 1)], w(k, WTO, D)) for k in range(KC)])
                        if i % 2:
                            ins.then_inc(wout_ps, 1)
                if cm:
                    pe.wait_ge(k2_lo, s * 8)
                    for i in range(CT):
                        ins = product(PS[:, 4 + i // 2, D * (i % 2):D * (i % 2 + 1)],
                                      [(lambda part, f=f: k216[:, f, part, P * i:P * (i + 1)], lambda part, f=f: WV2[:, f, part]) for f in range(FC)])
                        if i % 2:
                            ins.then_inc(val_ps, 1)
                    pe.wait_ge(xn3_done, s)
                    for k in range(KC):
                        for i in range(CT):
                            ins = te.transpose(PS[:, 6 + k, P * i:P * (i + 1)], xn3[:, i, P * k:P * (k + 1)], ident)
                    ins.then_inc(x3_ps, 1)
                    pe.wait_ge(x3_lo, s)
                    for i in range(CT):
                        ins = product(PS[:, 4, NE * i:NE * (i + 1)],
                                      [(lambda part, k=k: x3T[:, k, part, P * i:P * (i + 1)], w(k, WG, NE)) for k in range(KC)])
                    ins.then_inc(lg_ps, 1)
                    pe.wait_ge(before_ready, s)
                    for i in range(CT):
                        te.matmul(PS[:, 4, 64 + NE * i:64 + NE * (i + 1)], earlier, taken[:, bass.ds(s * CT + (i - CT), 1)].squeeze(1),
                                  start=True, stop=False)
                        ins = te.matmul(PS[:, 4, 64 + NE * i:64 + NE * (i + 1)], ones16, before[:, bass.ds(s * CT + (i - CT), 1)].squeeze(1),
                                        start=False, stop=True)
                    ins.then_inc(count_ps, 1)
                    if not tm:
                        te.matmul(PS[:, 7, 0:NE], ones16, before[:, NT], start=True, stop=True).then_inc(total_ps, 1)

            pe.wait_ge(wb_ready, 8)
            chunk_steps(pe, step)

        xg = place("xg", 0, [2, 2, D])
        x16 = place("x16", at["xg"], [2, KC, 2, RT], F16)
        gel = place("gel", at["x16"], [FC, RT])
        hid16 = place("hid16", at["gel"], [2, FC, 2, RT], F16)
        zeros = place("zeros", at["hid16"], [D])
        both = place("both", at["zeros"], [2, NT, NE])
        assert at["both"] <= at["WV2"], "over RWKV's weights"
        b1s = place("b1s", A0, [NE, FC])
        tiles_of_e = place("tiles_of_e", at["b1s"], [NE])
        ends = place("ends", at["tiles_of_e"], [NE])
        starts = place("starts", at["ends"], [NE])
        more = place("more", at["starts"], [NE, NE])
        past = place("past", at["more"], [NTILE, NE])
        expert_f = place("expert_f", at["past"], [NTILE])
        used = place("used", at["expert_f"], [NTILE])
        first_f = place("first_f", at["used"], [NTILE])
        table = place("table", at["first_f"], [3, NTILE], I32)
        pad_at = place("pad_at", at["table"], [NE], I32)
        weight = place("weight", at["pad_at"], [2, NT])
        back_f = place("back_f", at["weight"], [2, NT])
        back_u = place("back_u", at["back_f"], [2, NT], U32)
        b2t = place("b2t", at["back_u"], [2, D])
        yS = place("yS", at["b2t"], [2, 2, D])
        gathered = place("gathered", ARENA * 4 - NE * 2 * W2_AT * 2, [2, NT, D])
        assert at["yS"] <= ARENA * 4 - NE * 2 * W2_AT * 2

        (table_ready, pad_sent, zeros_ready, b1_in, t_ps, x_hi_out, x_lo_out, hid_ps, gel_out, g_hi, g_lo, y_ps, y_out, back_ready, added, stored) = [
            sem(n) for n in ("table_ready pad_sent zeros_ready b1_in t_ps x_hi_out x_lo_out hid_ps gel_out g_hi g_lo y_ps y_out "
                             "back_ready added stored").split()]
        xg_in = [sem("xg_in0"), sem("xg_in1")]
        b2_in = [sem("b2_in0"), sem("b2_in1")]
        y_sent = [sem("y_sent0"), sem("y_sent1")]
        gather_in = [sem(f"gather_in{c}") for c in range(NC)]
        returned_v = returned.rearrange("(j u p) d -> p j u d", p=P, u=2)

        later = rc[:, R_AFTER:R_AFTER + NE * NE].rearrange("p (e j) -> p j e", j=NE)

        def expert_tiles(eng, step, trail=None, per=0):
            step(0, 0, 0)
            step(1, 0, 1)
            with eng.Fori(1, NTILE // 2) as i:
                if trail:
                    trail.enter(i - 1, per)
                for par in range(2):
                    step(i * 2 + par, i, par)
            if trail:
                trail.leave(NTILE // 2 - 1)
            step(NTILE - 1, NTILE // 2, 0)

        def last_tile(j):
            return isinstance(j, int) and j == NTILE - 1

        def moe_sync(sp):
            sp.wait_ge(zeros_ready, 1)
            sp.wait_ge(table_ready, 1)
            for e in range(NE):
                at_row = sp.value_load(pad_at[0:1, e:e + 1], min_val=e * REG, max_val=e * REG + TOK)
                sp.dma_start(routed[bass.ds(at_row, RT)].rearrange("(u p) d -> p u d", p=P), zeros.unsqueeze(1).to_broadcast([P, 2, D])).then_inc(pad_sent, 16)
            sp.wait_ge(routed_sent, NC * 2 * CT * 16)
            sp.wait_ge(pad_sent, NE * 16)

            def load(j, i, par):
                row = sp.value_load(table[0:1, 1, bass.ds(j, 1)], min_val=0, max_val=NE * REG - RT)
                sp.dma_start(xg[:, par], routed[bass.ds(row, RT)].rearrange("(u p) d -> p u d", p=P)).then_inc(xg_in[par], 16)

            def store(j, par):
                sp.wait_ge(y_out, j + 1)
                sp.dma_start(returned_v[:, bass.ds(j, 1)].squeeze(1), yS[:, par]).then_inc(y_sent[par], 16)

            def load_b2(j, par):
                e = sp.value_load(table[0:1, 0, bass.ds(j, 1)], min_val=0, max_val=NE - 1)
                sp.dma_start(b2t[:, par], b2[bass.ds(e, 1)].rearrange("e d -> (e d)").partition_broadcast(P)).then_inc(b2_in[par], 16)

            def step(j, i, par):
                if not (isinstance(j, int) and j + 2 >= NTILE):
                    sp.wait_ge(t_ps, j + 1)
                    load(j + 2, i + 1, par)
                if not (isinstance(j, int) and j == 0):
                    store(j - 1, 1 - par)
                if not last_tile(j):
                    load_b2(j + 1, 1 - par)

            load(0, 0, 0)
            load(1, 0, 1)
            load_b2(0, 0)
            step(0, 0, 0)
            step(1, 0, 1)
            with sp.Fori(1, NTILE // 2 - 1) as i:
                for par in range(2):
                    step(i * 2 + par, i, par)
            for j in range(NTILE - 3, NTILE):
                step(j, j // 2, j % 2)
            store(NTILE - 1, (NTILE - 1) % 2)
            for c in range(NC):
                sp.wait_ge(added, c + 1)
                sp.dma_start(out.rearrange("(t p) d -> p t d", p=P)[:, CT * c:CT * (c + 1)], x_all[:, CT * c:CT * (c + 1)]).then_inc(stored, 16)
            sp.wait_ge(stored, 16 * NC)

        def moe_pool(pool, own, split_w1, split_w2):
            g = nc.gpsimd
            for e in range(NE - 2, -1, -1):
                split_w1(e)
                split_w2(e)
            pool.wait_ge(back_ready, 1)
            for par in range(2):
                pool.wait_ge(y_sent[par], 16 * ((NTILE + 1 - par) // 2))
            for c in range(NC):
                for t in range(CT * c, CT * (c + 1)):
                    for n in range(2):
                        g.indirect_dma_start(gathered[:, n, t], None, returned, bass.IndirectOffsetOnAxis(ap=back_u[:, n, t:t + 1], axis=0)
                                             ).then_inc(gather_in[c], 16)

        def moe_scalar(act):
            a = nc.scalar
            act.wait_ge(table_ready, 1)
            act.wait_ge(b1_in, 16)

            def x_hi(j, par):
                act.wait_ge(t_ps, j + 1)
                if not (isinstance(j, int) and j < 2):
                    act.wait_ge(hid_ps, (j - 1) * FC)
                a.activation(x16[:, par, :, HI], PS[:, 7 * par].rearrange("p (k n) -> p k n", k=KC), ACT.Copy).then_inc(x_hi_out, 1)

            def step(j, i, par):
                if not last_tile(j):
                    x_hi(j + 1, 1 - par)
                e = act.value_load(table[0:1, 0, bass.ds(j, 1)], min_val=0, max_val=NE - 1)

                def hi(half):
                    f = slice(FC // 2 * half, FC // 2 * (half + 1))
                    act.wait_ge(gel_out, j * FC + FC // 2 * (half + 1))
                    if not (isinstance(j, int) and j < 2):
                        act.wait_ge(y_ps, j - 1)
                    a.activation(hid16[:, par, f, HI], gel[:, f], ACT.Copy).then_inc(g_hi, 1)

                for f in range(FC):
                    if f % 2 == 0:
                        act.wait_ge(hid_ps, j * FC + (f + 2))
                    if f % (FC // 2) == 0 and not (isinstance(j, int) and j == 0):
                        act.wait_ge(g_lo, j * 2 + (f // (FC // 2) - 1))
                    a.activation(gel[:, f], PS[:, 1 + f // 2, RT * (f % 2):RT * (f % 2 + 1)], ACT.Gelu,
                                 bias=b1s[:, bass.ds(e, 1), f:f + 1].squeeze(1), scale=1 / WS).then_inc(gel_out, 1)
                    if f == FC // 2:
                        hi(0)
                hi(1)

            x_hi(0, 0)
            expert_tiles(act, step)

        def moe_vector(dve, own):
            v = nc.vector
            dve.wait_ge(total_ps, 1)
            dve.wait_ge(rows_ready, NC)
            total = PS[:, 7, 0:NE]
            own.mark(v.tensor_tensor(ends, total, rc[:, R_BASE:R_BASE + NE], ALU.add))
            bc8 = [P, NE, TPE]
            own.link(v.tensor_tensor(more, total.unsqueeze(2).to_broadcast(bc8), rc[:, R_TILE:R_TILE + TPE].unsqueeze(1).to_broadcast(bc8), ALU.is_gt))
            own.mark(v.tensor_copy(pad_at, ends))
            own.link(v.tensor_reduce(tiles_of_e, more, AX.X, ALU.add))
            own.link(v.tensor_tensor(more, tiles_of_e.unsqueeze(1).to_broadcast([P, NE, NE]), later, ALU.mult))
            own.link(v.tensor_reduce(starts, more, AX.X, ALU.add))
            own.link(v.tensor_tensor(ends, starts, tiles_of_e, ALU.add))
            full = [P, NTILE, NE]
            j_f = rc[:, R_J:R_J + NTILE]
            j_bc, ends_bc = j_f.unsqueeze(2).to_broadcast(full), ends.unsqueeze(1).to_broadcast(full)
            own.link(v.tensor_tensor(past, ends_bc, j_bc, ALU.is_gt))
            own.link(v.tensor_reduce(expert_f, past, AX.X, ALU.add))
            own.mark(v.tensor_scalar(used, expert_f, 1.0, None, ALU.is_ge))
            own.link(v.tensor_scalar(expert_f, expert_f, 1.0, 0.0, ALU.subtract, ALU.max))
            own.mark(v.tensor_copy(table[:, 0], expert_f))
            own.mark(v.tensor_scalar(table[:, 2], expert_f, -1.0, float(NE), ALU.mult, ALU.add))
            own.link(v.tensor_tensor(past, ends_bc, j_bc, ALU.is_le))
            own.link(v.tensor_tensor(past, past, ends_bc, ALU.mult))
            own.link(v.tensor_reduce(first_f, past, AX.X, ALU.max))
            own.link(v.tensor_tensor(first_f, j_f, first_f, ALU.subtract))
            own.mark(v.tensor_scalar(first_f, first_f, float(RT), None, ALU.mult))
            own.link(v.tensor_scalar(expert_f, expert_f, float(REG), None, ALU.mult))
            own.link(v.tensor_tensor(first_f, first_f, expert_f, ALU.add))
            own.link(v.tensor_tensor(first_f, first_f, used, ALU.mult))
            v.tensor_copy(table[:, 1], first_f).then_inc(table_ready, 1)

            def x_lo(j, par):
                dve.wait_ge(x_hi_out, j + 1)
                v.tensor_tensor(x16[:, par, :, LO], PS[:, 7 * par].rearrange("p (k n) -> p k n", k=KC), x16[:, par, :, HI], ALU.subtract
                                ).then_inc(x_lo_out, 1)

            def y(j, i, par):
                dve.wait_ge(y_ps, j + 1)
                dve.wait_ge(b2_in[par], i * 16 + 16)
                if not (isinstance(j, int) and j < 2):
                    dve.wait_ge(y_sent[par], i * 16)
                v.scalar_tensor_tensor(yS[:, par], PS[:, 5 + par].rearrange("p (u d) -> p u d", u=2), 1 / WS,
                                       b2t[:, par].unsqueeze(1).to_broadcast([P, 2, D]), ALU.mult, ALU.add).then_inc(y_out, 1)

            def step(j, i, par):
                if not last_tile(j):
                    x_lo(j + 1, 1 - par)
                for half in range(2):
                    f = slice(FC // 2 * half, FC // 2 * (half + 1))
                    dve.wait_ge(g_hi, j * 2 + (half + 1))
                    v.tensor_tensor(hid16[:, par, f, LO], gel[:, f], hid16[:, par, f, HI], ALU.subtract).then_inc(g_lo, 1)
                if not (isinstance(j, int) and j == 0):
                    y(j - 1, i + (par - 1), 1 - par)

            x_lo(0, 0)
            full = [P, NT, NE]
            own.mark(v.scalar_tensor_tensor(both[:, 0], rank, 0.0, gate, ALU.is_equal, ALU.mult))
            own.link(v.scalar_tensor_tensor(both[:, 1], rank, 1.0, gate, ALU.is_equal, ALU.mult))
            own.link(v.tensor_reduce(weight, both, AX.X, ALU.add))
            own.link(v.scalar_tensor_tensor(starts, starts, float(RT), rc[:, R_BASE:R_BASE + NE], ALU.mult, ALU.subtract))
            own.link(v.tensor_tensor(row_of, row_of, starts.unsqueeze(1).to_broadcast(full), ALU.add))
            own.mark(v.scalar_tensor_tensor(both[:, 0], rank, 0.0, row_of, ALU.is_equal, ALU.mult))
            own.link(v.scalar_tensor_tensor(both[:, 1], rank, 1.0, row_of, ALU.is_equal, ALU.mult))
            own.link(v.tensor_reduce(back_f, both, AX.X, ALU.add))
            v.tensor_copy(back_u, back_f).then_inc(back_ready, 1)
            expert_tiles(dve, step)
            y(NTILE - 1, NTILE // 2, 0)
            for c in range(NC):
                dve.wait_ge(gather_in[c], 2 * CT * 16)
                for n in range(2):
                    for t in range(CT * c, CT * (c + 1)):
                        ins = v.scalar_tensor_tensor(x_all[:, t], gathered[:, n, t], weight[:, n, t:t + 1], x_all[:, t], ALU.mult, ALU.add)
                        if n == 0 and t == CT * (c + 1) - 1:
                            own.link(ins)
                ins.then_inc(added, 1)

        def moe_tensor(pe):
            te = nc.tensor
            pe.wait_ge(table_ready, 1)

            def transposes(j, i, par):
                pe.wait_ge(xg_in[par], i * 16 + 16)
                for k in range(KC):
                    for u in range(2):
                        ins = te.transpose(PS[:, 7 * par, RT * k + P * u:RT * k + P * (u + 1)], xg[:, par, u, P * k:P * (k + 1)], ident)
                ins.then_inc(t_ps, 1)

            def weights(e, part, at_col, n):
                return experts[:, bass.ds(e, 1), at_col:at_col + n].rearrange("p e n -> p (e n)")

            def outputs(j, par):
                e = pe.value_load(table[0:1, 0, bass.ds(j, 1)], min_val=0, max_val=NE - 1)
                ready = pe.value_load(table[0:1, 2, bass.ds(j, 1)], min_val=1, max_val=NE)
                pe.wait_ge(g_lo, j * 2 + 2)
                pe.wait_ge(w2_ready, ready)
                if not (isinstance(j, int) and j < 2):
                    pe.wait_ge(y_out, j - 1)
                for u in range(2):
                    for m in range(3 * FC):
                        f, (a, b) = m // 3, PASSES[m % 3]
                        ins = te.matmul(PS[:, 5 + par, D * u:D * (u + 1)], hid16[:, par, f, a, P * u:P * (u + 1)],
                                        weights(e, b, W2_AT + (2 * f + b) * D, D), start=m == 0, stop=m == 3 * FC - 1)
                ins.then_inc(y_ps, 1)

            def step(j, i, par):
                if not last_tile(j):
                    transposes(j + 1, i + par, 1 - par)
                e = pe.value_load(table[0:1, 0, bass.ds(j, 1)], min_val=0, max_val=NE - 1)
                ready = pe.value_load(table[0:1, 2, bass.ds(j, 1)], min_val=1, max_val=NE)
                pe.wait_ge(x_lo_out, j + 1)
                pe.wait_ge(w1_ready, ready)
                for f in range(FC):
                    if f % 2 == 0 and not (isinstance(j, int) and j == 0):
                        pe.wait_ge(gel_out, j * FC + (f + 2 - FC))
                    for m in range(3 * KC):
                        k, (a, b) = m // 3, PASSES[m % 3]
                        ins = te.matmul(PS[:, 1 + f // 2, RT * (f % 2):RT * (f % 2 + 1)], weights(e, a, (2 * k + a) * FF + P * f, P),
                                        x16[:, par, k, b], start=m == 0, stop=m == 3 * KC - 1)
                    ins.then_inc(hid_ps, 1)
                if not (isinstance(j, int) and j == 0):
                    outputs(j - 1, 1 - par)

            transposes(0, 0, 0)
            expert_tiles(pe, step)
            outputs(NTILE - 1, (NTILE - 1) % 2)

        def after_attention_sync(sp):
            sp.wait_ge(lg_out, NC)
            sp.dma_start(b1s, b1).then_inc(b1_in, 16)
            moe_sync(sp)

        def after_attention_pool(pool, own):
            moe_pool(pool, own, *rwkv_pool(pool, own))

        def after_attention_scalar(act):
            rwkv_scalar(act)
            moe_scalar(act)

        def after_attention_vector(dve, own):
            dve.wait_ge(xbo_ready, 8)
            dve.wait_ge(ao_split, NT)
            dve.wait_ge(rc_in, 16)
            rwkv_vector(dve, own)
            moe_vector(dve, own)

        def after_attention_tensor(pe):
            rwkv_tensor(pe)
            moe_tensor(pe)

        block = stack.enter_context(nc.Block())

        def attention_tiles(eng, step, trail=None, per=0):
            step(0, True, False)
            with eng.Fori(1, NT - 1) as t:
                if trail:
                    trail.enter(t - 1, per)
                step(t, False, False)
            if trail:
                trail.leave(NT - 2)
            step(NT - 1, False, True)

        UNITS = [(b, j) for b in range(BT) for j in range(2)]

        @block.sync
        def _(sp):
            x_v = x.rearrange("(t p) d -> p t d", p=P)
            ctx_v = ctx_t.rearrange("(k p) n -> p k n", p=P)
            w_v = w_all.rearrange("(k p) n -> p k n", p=P)
            sp.dma_start(vec, vecs).then_inc(vecs_in, 16)
            sp.dma_start(stage[:, :, 0:NWA], w_v[:, :, 0:NWA]).then_inc(wa_in, 16)
            for c in range(NC):
                sp.dma_start(x_all[:, CT * c:CT * (c + 1), :], x_v[:, CT * c:CT * (c + 1), :]).then_inc(x_in[c], 16)
                if c == 0:
                    sp.dma_start(clf, ctx_last).then_inc(cl_in, 16)
            for b in range(BT):
                sp.dma_start(ctxf[:, b], ctx_v[:, :, SK * b:SK * (b + 1)]).then_inc(ctx_in[b], 16)
            sp.dma_start(rc, route_consts.partition_broadcast(P)).then_inc(rc_in, 16)
            sp.dma_start(bo_bc, bo.partition_broadcast(P)).then_inc(bo_in, 16)
            sp.dma_start(stage[:, :, NWA:NW], w_v[:, :, NWA:NW]).then_inc(wb_in, 16)
            sp.dma_start(stage2, w_value2.rearrange("(k p) n -> p k n", p=P)).then_inc(wb_in, 16)
            with sp.Fori(1, NT) as t:
                for b in range(BT):
                    sp.wait_ge(ctx_split, t * BT + (b - BT + 1))
                    sp.dma_start(ctxf[:, b], ctx_v[:, :, bass.ds(t * (BT * SK) + SK * b, SK)]).then_inc(ctx_in[b], 16)
            after_attention_sync(sp)

        @block.gpsimd
        def _(pool):
            g = nc.gpsimd
            own = Trail(pool, pool_step, wait_apart)

            def keep(m, base, cm, pattern, op=ALU.is_ge, fill=0.0):
                own.link(g.affine_select(out=m, in_=m, compare_op=op, fill=fill, base=base, channel_multiplier=cm, pattern=pattern))

            g.memset(neghalf, -0.5).then_inc(consts, 1)
            own.mark(g.memset(ident, 0.0))
            own.mark(g.memset(mask8, 1.0))
            own.mark(g.memset(maskO, 1.0))
            own.mark(g.memset(maskV, 1.0))
            own.mark(g.memset(sel16, 0.0))
            own.link(g.memset(plast, 0.0))
            keep(ident, 0, 1, [[-1, P]], ALU.not_equal, 1.0)
            keep(mask8, 0, 1, [[-HD, 8]])
            keep(mask8, HD - 1, -1, [[HD, 8]])
            keep(maskO, 0, 1, [[-SQ, 4], [0, HD]])
            keep(maskO, SQ - 1, -1, [[SQ, 4], [0, HD]])
            keep(maskV, 0, 1, [[0, 2], [-4, 2], [0, 64]])
            keep(maskV, 3, -1, [[0, 2], [4, 2], [0, 64]])
            for h in range(4):
                keep(sel16, -SQ * h, 1, [[-1, SQ]], ALU.not_equal, 1.0)
            own.mark(g.memset(ones16, 1.0))
            own.link(g.memset(earlier, 1.0))
            keep(earlier, 0, -1, [[1, P]], ALU.is_gt)
            g.tensor_copy(ident16, ident).then_inc(consts, 1)

            pool.wait_ge(cl_in, 16)
            for k in range(KC):
                own.link(g.tensor_scalar(cl16[:, k, HI], clf[:, k], 1.0, 0.0, ALU.mult, ALU.add))
                g.tensor_tensor(cl16[:, k, LO], clf[:, k], cl16[:, k, HI], ALU.subtract).then_inc(cl_split, 1)

            def split_ctx_hi(slot, par, arrivals):
                wait_apart(pool, ctx_in[slot], arrivals * 16)
                own.link(g.tensor_scalar(ctx16[:, par, :, HI, 0:SK], ctxf[:, slot], 1.0, 0.0, ALU.mult, ALU.add))

            def split_ctx_lo(slot, par):
                g.tensor_tensor(ctx16[:, par, :, LO, 0:SK], ctxf[:, slot], ctx16[:, par, :, HI, 0:SK], ALU.subtract).then_inc(ctx_split, 1)

            split_ctx_hi(0, 0, 1)
            split_ctx_lo(0, 0)
            pool.wait_ge(var_ready, 1)
            g.tensor_tensor(rs0, ve0, neghalf, ALU.pow).then_inc(rstd_ready, 1)
            split_ctx_hi(1, 1, 1)
            split_ctx_lo(1, 1)
            for i in range(NT // 2):
                pool.wait_ge(vl_evac, i + 1)
                own.link(g.tensor_scalar(vlast[:8, 2 * i:2 * i + 2, HI], vlf[:8, i % 2], 1.0, 0.0, ALU.mult, ALU.add))
                g.tensor_tensor(vlast[:8, 2 * i:2 * i + 2, LO], vlf[:8, i % 2], vlast[:8, 2 * i:2 * i + 2, HI], ALU.subtract).then_inc(vl_split, 1)

            def plast_of(U, b, j):
                wait_apart(pool, probs, U + 1)
                g.tensor_copy(plast[:, j, b, :, b], Pr[:, j, :, SK - 1]).then_inc(p_last, 1)

            def split_o(Up, b, j):
                wait_apart(pool, o_masked, Up + 1)
                s = (2 * b + j) % 4
                own.link(g.tensor_scalar(Om16[:, s, HI], Om[:, j], 1.0, 0.0, ALU.mult, ALU.add))
                g.tensor_tensor(Om16[:, s, LO], Om[:, j], Om16[:, s, HI], ALU.subtract).then_inc(o_split, 1)

            def step(t, first, last):
                for n, (b, j) in enumerate(UNITS):
                    U = t * 8 + n
                    ahead = b + 2
                    load = j == 0 and not (last and ahead >= BT)
                    if load:
                        wait_apart(pool, v_ps, t * 8 + (2 * b + 2))
                        split_ctx_hi(ahead % BT, b % 2, t + (1 + ahead // BT))
                    plast_of(U, b, j)
                    if load:
                        split_ctx_lo(ahead % BT, b % 2)
                    if not (first and n == 0):
                        split_o(t * 8 + (n - 1), *UNITS[n - 1])
                    if first:
                        rest_of_weights(n)

            def rest_of_weights(n):
                if n == 0:
                    pool.wait_ge(wb_in, 32)
                    pool.wait_ge(bo_in, 16)
                    pool.wait_ge(xn_ready, NC)
                cols = slice(NWA + (NW - NWA) // 8 * n, NWA + (NW - NWA) // 8 * (n + 1))
                own.mark(g.tensor_scalar(stage[:, :, cols], stage[:, :, cols], WS, 0.0, ALU.mult, ALU.add))
                own.link(g.tensor_scalar(stage2[:, n], stage2[:, n], WS, 0.0, ALU.mult, ALU.add))
                own.mark(g.tensor_scalar(W16[:, :, HI, cols], stage[:, :, cols], 1.0, 0.0, ALU.mult, ALU.add))
                own.link(g.tensor_scalar(WV2[:, n, HI], stage2[:, n], 1.0, 0.0, ALU.mult, ALU.add))
                g.tensor_tensor(W16[:, :, LO, cols], stage[:, :, cols], W16[:, :, HI, cols], ALU.subtract)
                g.tensor_tensor(WV2[:, n, LO], stage2[:, n], WV2[:, n, HI], ALU.subtract).then_inc(wb_ready, 1)
                rows = x_all[:, 2 * n:2 * n + 2]
                g.tensor_tensor(rows, rows, bo_bc.unsqueeze(1).to_broadcast([P, 2, D]), ALU.add).then_inc(xbo_ready, 1)

            attention_tiles(pool, step, own, 4 + 8)
            split_o(8 * NT - 1, BT - 1, 1)
            after_attention_pool(pool, own)

        @block.scalar
        def _(act):
            s = nc.scalar

            def x_hi(c):
                act.wait_ge(xt_ps, c + 1)
                for k in range(KC):
                    ins = s.activation(xT[:, c % 2, k, HI], PS[:, 2 * (c % 2) + k], ACT.Copy)
                ins.then_inc(xt_hi, 1)

            def q_parts(c):
                act.wait_ge(q_ps, c + 1)
                for j in range(KC):
                    ins = s.activation(qT[:, j, HI, CN * c:CN * (c + 1)], PS[:, 4 + 2 * (c % 2) + j], ACT.Identity,
                                       bias=vec64[:, BQ, j:j + 1])
                ins.then_inc(q_hi, 1)

            for c in range(NC + 1):
                if c < NC:
                    x_hi(c)
                if c > 0:
                    q_parts(c - 1)

            def kv_hi(n, bpar, b4, j):
                act.wait_ge(k_ps, n + 1)
                s.activation(Kt[:, bpar, j, HI, 0:SK], PS[:, 4, 0:SK], ACT.Identity, bias=vec64[:, BK, j:j + 1]).then_inc(k_hi, 1)
                act.wait_ge(v_ps, n + 1)
                s.activation(Vt[:, b4, j, HI], PS[:, 5, 0:D], ACT.Copy).then_inc(v_hi, 1)

            def pt_high(Up):
                act.wait_ge(pt_ps, Up + 1)
                s.activation(PT[:, HI], PS[:, 6], ACT.Copy)
                s.activation(PTl[:8, HI], PS[:8, 7, P:2 * P], ACT.Copy).then_inc(pt_hi, 1)

            def tile_out(t):
                act.wait_ge(selected, t * 8)
                s.activation(aoF, PS[:, 5, D:2 * D].rearrange("p (k n) -> p k n", k=KC), ACT.Copy, scale=1 / WS).then_inc(ao_evac, 1)

            for j in range(2):
                kv_hi(j, 0, 0, j)

            def step(t, first, last):
                for n, (b, j) in enumerate(UNITS):
                    U = t * 8 + n
                    if not (first and n == 0):
                        pt_high(U - 1)
                    if n == 1 and not first:
                        tile_out(t)
                    act.wait_ge(negmax, U + 1)
                    for h in range(2):
                        ins = s.activation(Pr[:, j, h], PS[:, 2 * j + h, 0:SK], ACT.Exp, bias=nb[:, j, h:h + 1], scale=SM,
                                           accum_out=den[:, j, h:h + 1])
                    ins.then_inc(probs, 1)
                    if not (last and b == BT - 1):
                        kv_hi(U + 2, (b + 1) % 2, (b + 1) % BT, j)

            attention_tiles(act, step)
            pt_high(8 * NT - 1)
            tile_out(NT)
            after_attention_scalar(act)

        @block.vector
        def _(dve):
            v = nc.vector
            own = Trail(dve, dve_step)
            dve.wait_ge(vecs_in, 16)
            own.mark(v.tensor_scalar(vec64, vec, WS, None, ALU.mult))
            dve.wait_ge(wa_in, 16)
            own.link(v.tensor_scalar(W16[:, :, HI, 0:NWA], stage[:, :, 0:NWA], WS, None, ALU.mult))
            v.scalar_tensor_tensor(W16[:, :, LO, 0:NWA], stage[:, :, 0:NWA], WS, W16[:, :, HI, 0:NWA],
                                   ALU.mult, ALU.subtract).then_inc(wa_ready, 1)
            for t in range(NT):
                if t % CT == 0:
                    dve.wait_ge(x_in[t // CT], 16)
                n = own.mark(v.bn_stats(st0[:, t], x_all[:, t]))
            dve.wait_ge(dve_step, n)
            for t in range(NT):
                n = own.mark(v.bn_aggr(mv0[:, t], st0[:, t]))
            dve.wait_ge(dve_step, n)
            v.tensor_scalar(ve0, mv0[:, :, 1], 1e-5, None, ALU.add).then_inc(var_ready, 1)

            def last_values(i):
                dve.wait_ge(vl_ps, i + 1)
                need(dve, vl_split, i - 1)
                v.tensor_tensor(vlf[:8, i % 2], PS[:8, i].rearrange("p (t n) -> p t n", t=2),
                                maskV8, ALU.mult).then_inc(vl_evac, 1)

            dve.wait_ge(rstd_ready, 1)
            maskV8 = maskV[:8].rearrange("p a b n -> p (a b n)").unsqueeze(1).to_broadcast([8, 2, D])
            for c in range(NC + 2):
                if c < NC:
                    need(dve, xt_ps, c - 1)
                    for i in range(CT):
                        t = CT * c + i
                        ins = v.tensor_scalar(xn[:, c % 2, i], x_all[:, t], mv0[:, t, 0:1], rs0[:, t:t + 1], ALU.subtract, ALU.mult)
                    ins.then_inc(xn_ready, 1)
                if c == 0:
                    for i in range(NT // 2):
                        last_values(i)
                if 0 < c <= NC:
                    dve.wait_ge(xt_hi, c)
                    for k in range(KC):
                        ins = v.tensor_tensor(xT[:, (c - 1) % 2, k, LO], PS[:, 2 * ((c - 1) % 2) + k], xT[:, (c - 1) % 2, k, HI], ALU.subtract)
                    ins.then_inc(xt_split, 1)
                if c > 1:
                    dve.wait_ge(q_hi, c - 1)
                    for j in range(KC):
                        cols = slice(CN * (c - 2), CN * (c - 1))
                        ins = v.scalar_tensor_tensor(qT[:, j, LO, cols], PS[:, 4 + 2 * (c % 2) + j], vec64[:, BQ, j:j + 1],
                                                     qT[:, j, HI, cols], ALU.add, ALU.subtract)
                    ins.then_inc(q_split, 1)

            def kv_lo(n, bpar, b4, j):
                dve.wait_ge(k_hi, n + 1)
                v.scalar_tensor_tensor(Kt[:, bpar, j, LO, 0:SK], PS[:, 4, 0:SK], vec64[:, BK, j:j + 1], Kt[:, bpar, j, HI, 0:SK],
                                       ALU.add, ALU.subtract).then_inc(k_split, 1)
                dve.wait_ge(v_hi, n + 1)
                v.tensor_tensor(Vt[:, b4, j, LO], PS[:, 5, 0:D], Vt[:, b4, j, HI], ALU.subtract).then_inc(v_split, 1)

            qT4 = qT.rearrange("p j c n -> p (j c) n")

            def spread_queries(pair, half, heads):
                src = qT4[:, :, bass.ds(pair * (2 * SQ), 2 * SQ)].rearrange("p c (b q) -> p c b q", b=2)
                for h in heads:
                    ins = v.tensor_scalar(Qbd[:, half, :, :, SQ * h:SQ * (h + 1)], src, mask8[:, h:h + 1], None, ALU.mult)
                if heads[-1] == 7:
                    ins.then_inc(qbd, 1)

            def last_values_now(tile, half):
                v.tensor_copy(vlc[:8, half].rearrange("p c n -> p (c n)"),
                              vlast[:8].rearrange("p t c n -> p t (c n)")[:, bass.ds(tile, 1)].squeeze(1) if not isinstance(tile, int)
                              else vlast[:8, tile].rearrange("p c n -> p (c n)")).then_inc(vl_now, 1)

            dve.wait_ge(q_split, NC)
            dve.wait_ge(vl_split, NT // 2)
            spread_queries(0, 0, range(8))
            last_values_now(0, 0)
            for j in range(2):
                kv_lo(j, 0, 0, j)

            def pt_low(Up):
                dve.wait_ge(pt_hi, Up + 1)
                v.tensor_tensor(PT[:, LO], PS[:, 6], PT[:, HI], ALU.subtract)
                v.tensor_tensor(PTl[:8, LO], PS[:8, 7, P:2 * P], PTl[:8, HI], ALU.subtract).then_inc(pt_split, 1)

            def mask_out(Up, j):
                dve.wait_ge(pv, Up + 1)
                own.link(v.reciprocal(rec[:, j], den[:, j]))
                for h in range(2):
                    ins = v.scalar_tensor_tensor(Om[:, j, 64 * h:64 * (h + 1)], PS[:, 7, 64 * h:64 * (h + 1)], rec[:, j, h:h + 1],
                                                 maskO.rearrange("p a b -> p (a b)"), ALU.mult, ALU.mult)
                ins.then_inc(o_masked, 1)

            def split_tile_out(t):
                dve.wait_ge(ao_evac, t)
                cols = bass.ds(t * P - P, P)
                for k in range(KC):
                    own.link(v.tensor_scalar(aoT[:, k, HI, cols], aoF[:, k], vec[:, BV, k:k + 1], None, ALU.add))
                    ins = v.scalar_tensor_tensor(aoT[:, k, LO, cols], aoF[:, k], vec[:, BV, k:k + 1], aoT[:, k, HI, cols],
                                                 ALU.add, ALU.subtract)
                ins.then_inc(ao_split, 1)

            def step(t, first, last):
                for n, (b, j) in enumerate(UNITS):
                    U = t * 8 + n
                    half = b // 2
                    dve.wait_ge(scores, U + 1)
                    own.link(v.tensor_reduce(nm[:, j], PS[:, 2 * j:2 * j + 2, 0:SK], AX.X, ALU.max, negate=True))
                    v.tensor_scalar(nb[:, j], nm[:, j], SM, PS_LN, ALU.mult, ALU.add).then_inc(negmax, 1)
                    if not (first and n == 0):
                        pt_low(U - 1)
                    if not (last and b == BT - 1):
                        kv_lo(U + 2, (b + 1) % 2, (b + 1) % BT, j)
                    if not (last and half == 1):
                        if n % 4 < 3:
                            spread_queries(t * 2 + (half + 1), 1 - half, (range(0, 3), range(3, 6), range(6, 8))[n % 4])
                        if n % 4 == 1:
                            need(dve, pv, t * 8 + 4 * half)
                            last_values_now(t + half, 1 - half)
                    if n == 2 and not first:
                        split_tile_out(t)
                    if not (first and n == 0):
                        mask_out(U - 1, UNITS[n - 1][1])

            attention_tiles(dve, step, own, 8 * 2 + 2)
            pt_low(8 * NT - 1)
            mask_out(8 * NT - 1, 1)
            split_tile_out(NT)
            after_attention_vector(dve, own)

        @block.tensor
        def _(pe):
            te = nc.tensor
            pe.wait_ge(cl_split, KC)
            pe.wait_ge(wa_ready, 1)
            for t in range(NT):
                n = 0
                for k in range(KC):
                    for a, b in PASSES:
                        ins = te.matmul(PS[:8, t // 2, D * (t % 2):D * (t % 2 + 1)], cl16[:, k, a, t], W16[:, k, b, WV:WV + D],
                                        start=n == 0, stop=n == 2 * len(PASSES) - 1)
                        n += 1
                if t % 2:
                    ins.then_inc(vl_ps, 1)
            pe.wait_ge(consts, 2)
            pe.wait_ge(vl_evac, NT // 2)
            for c in range(NC + 1):
                if c < NC:
                    pe.wait_ge(xn_ready, c + 1)
                    need(pe, xt_split, c - 1)
                    for k in range(KC):
                        for i in range(CT):
                            ins = te.transpose(PS[:, 2 * (c % 2) + k, P * i:P * (i + 1)], xn[:, c % 2, i, P * k:P * (k + 1)], ident)
                    ins.then_inc(xt_ps, 1)
                if c > 0:
                    pe.wait_ge(xt_split, c)
                    need(pe, q_split, c - 2)
                    for j in range(KC):
                        n = 0
                        for k in range(KC):
                            for a, b in PASSES:
                                ins = te.matmul(PS[:, 4 + 2 * ((c - 1) % 2) + j], W16[:, k, a, WQ + P * j:WQ + P * (j + 1)],
                                                xT[:, (c - 1) % 2, k, b], start=n == 0, stop=n == 5)
                                n += 1
                    ins.then_inc(q_ps, 1)

            def project_keys(n, par, j):
                need(pe, k_split, n)
                m = 0
                for k in range(KC):
                    for a, b in PASSES:
                        ins = te.matmul(PS[:, 4, 0:SK], W16[:, k, a, WK + P * j:WK + P * (j + 1)], ctx16[:, par, k, b, 0:SK],
                                        start=m == 0, stop=m == 5)
                        m += 1
                ins.then_inc(k_ps, 1)

            def project_values(n, par, j):
                need(pe, v_split, n)
                m = 0
                for k in range(KC):
                    for a, b in PASSES:
                        ins = te.matmul(PS[:, 5, 0:D], ctx16[:, par, k, a, P * j:P * (j + 1)], W16[:, k, b, WV:WV + D],
                                        start=m == 0, stop=m == 5)
                        m += 1
                ins.then_inc(v_ps, 1)

            pe.wait_ge(q_split, NC)
            pe.wait_ge(ctx_split, 1)
            for j in range(2):
                project_keys(j, 0, j)
                project_values(j, 0, j)

            def select_heads(Up, b, j):
                pe.wait_ge(o_split, Up + 1)
                for m, a in enumerate((HI, LO)):
                    ins = te.matmul(PS[:, 5, D + P * j + SQ * b:D + P * j + SQ * (b + 1)], Om16[:, (2 * b + j) % 4, a], sel16,
                                    start=m == 0, stop=m == 1)
                ins.then_inc(selected, 1)

            def transpose_probs(Up, b, j):
                pe.wait_ge(probs, Up + 1)
                pe.wait_ge(p_last, Up + 1)
                need(pe, o_masked, Up)
                for h in range(2):
                    for k in range(2):
                        te.transpose(PS[:, 6, P * (2 * h + k):P * (2 * h + k + 1)], Pr[:, j, h, P * k:P * (k + 1)], ident)
                te.transpose(PS[:8, 7, P:2 * P], plast[:, j, b].rearrange("p g c -> p (g c)"), ident).then_inc(pt_ps, 1)

            def outputs(Up, b, j):
                pe.wait_ge(pt_split, Up + 1)
                half = b // 2
                for h in range(2):
                    cols = slice(P * j + 64 * h, P * j + 64 * (h + 1))
                    terms = [(PT[:, a, P * (2 * h + k):P * (2 * h + k + 1)], Vt[:, b, k, c, cols]) for k in range(2) for a, c in PASSES]
                    terms += [(PTl[:8, a], vlc[:8, half, c, cols]) for a, c in PASSES]
                    for m, (lhs, rhs) in enumerate(terms):
                        ins = te.matmul(PS[:, 7, 64 * h:64 * (h + 1)], lhs, rhs, start=m == 0, stop=m == len(terms) - 1)
                ins.then_inc(pv, 1)

            def step(t, first, last):
                for n, (b, j) in enumerate(UNITS):
                    U = t * 8 + n
                    half = b // 2
                    if n % 4 == 0:
                        pe.wait_ge(qbd, t * 2 + (half + 1))
                        pe.wait_ge(vl_now, t * 2 + (half + 1))
                    pe.wait_ge(k_split, U + 1)
                    need(pe, probs, U - 1)
                    for h in range(2):
                        for m, (a, c) in enumerate(PASSES):
                            ins = te.matmul(PS[:, 2 * j + h, 0:SK], Qbd[:, half, 2 * j + a, b % 2, P * h:P * (h + 1)],
                                            Kt[:, b % 2, j, c, 0:SK], start=m == 0, stop=m == 2)
                    ins.then_inc(scores, 1)
                    if not (first and n == 0):
                        transpose_probs(U - 1, *UNITS[n - 1])
                    more = not (last and b == BT - 1)
                    if n == 1 and not first:
                        pe.wait_ge(v_split, U + 2)
                        select_heads(U - 2, *UNITS[n - 2])
                    if more:
                        if n % 2 == 0:
                            pe.wait_ge(ctx_split, t * 4 + (b + 2))
                        project_keys(U + 2, (b + 1) % 2, j)
                    if n == 1 and not first:
                        pe.wait_ge(ao_evac, t)
                    elif not (first and n < 2):
                        if more:
                            pe.wait_ge(v_split, U + 2)
                        select_heads(U - 2, *UNITS[n - 2])
                    if more:
                        project_values(U + 2, (b + 1) % 2, j)
                    if not (first and n == 0):
                        pe.wait_ge(v_split, (t * 8 + (n - 1) // 2 * 2 + 2) if n else t * 8)
                        outputs(U - 1, *UNITS[n - 1])

            attention_tiles(pe, step)
            U = 8 * NT
            transpose_probs(U - 1, BT - 1, 1)
            select_heads(U - 2, BT - 1, 0)
            outputs(U - 1, BT - 1, 1)
            select_heads(U - 1, BT - 1, 1)
            after_attention_tensor(pe)


def kernel(**inputs):
    import numpy as np
    import concourse.bacc as bacc
    from concourse.bass_utils import run_bass_kernel_spmd

    def a(name):
        return np.asarray(inputs[name])

    def layer(name):
        return a("L0_" + name)

    ctx = a("ctx_1024")
    last = ctx[:, SK - 1, :].reshape(NT, BT, KC, P).transpose(3, 2, 0, 1)
    w_all = np.concatenate(
        [layer("xattn_" + n).T for n in ("Wq", "Wk", "Wv", "Wo")]
        + [layer("attn_" + n) for n in ("W_key", "W_value", "W_recept", "W_out", "W_recept2", "W_key2")]
        + [layer("ffn_w_gate").T], axis=1)
    vecs = np.stack([layer(n) for n in (
        "xattn_bq", "xattn_bk", "xattn_bv", "attn_ln1_w", "attn_ln2_w", "attn_time_decay", "attn_time_first",
        "attn_time_mix_k", "attn_time_mix_v", "attn_time_mix_r", "attn_time_mix_k2", "attn_time_mix_r2")])
    e = np.arange(NE)
    route_consts = np.concatenate([e * REG, np.arange(TPE) * RT, (e[:, None] > e[None, :]).ravel(), np.arange(NTILE)]).astype(np.float32)
    host = {
        "x": a("x").reshape(TOK, D),
        "ctx_t": ctx.reshape(NB * SK, D).T,
        "ctx_last": np.concatenate([last, last], axis=3),
        "w_all": w_all,
        "w_value2": layer("attn_W_value2"),
        "vecs": vecs.reshape(NV, KC, P).transpose(2, 0, 1),
        "bo": layer("xattn_bo"),
        "route_consts": route_consts,
        "w1": layer("ffn_W1"),
        "b1": layer("ffn_b1").reshape(NE, FC, P).transpose(2, 0, 1),
        "w2": layer("ffn_W2"),
        "b2": layer("ffn_b2"),
    }
    nc = bacc.Bacc("TRN2", target_bir_lowering=False, num_devices=1)
    arrays, args = {}, []
    for name, value in host.items():
        value = np.ascontiguousarray(value)
        arrays[f"in_{name}"] = value
        args.append(nc.dram_tensor(f"in_{name}", value.shape, mybir.dt.from_np(value.dtype), kind="ExternalInput").ap())
    args.append(nc.dram_tensor("out", (TOK, D), F32, kind="ExternalOutput").ap())
    perceiver_layer(nc, *args)
    r = run_bass_kernel_spmd(nc, [arrays], core_ids=[0])
    return r.results[0]["out"].reshape(NB, SQ, D)
```

```python
import concourse.bass as bass
from concourse import mybir
from contextlib import ExitStack

F32 = mybir.dt.float32
F16 = mybir.dt.float16
U32, I32 = mybir.dt.uint32, mybir.dt.int32
ALU = mybir.AluOpType
ACT = mybir.ActivationFunctionType
AX = mybir.AxisListType

NB, SQ, SK, D = 64, 32, 257, 256
NH, HD = 16, 16
P = 128
TOK = NB * SQ
NT = TOK // P
BT = P // SQ
KC = D // P
FF, NE = 1024, 8
FC = FF // P
CT = 4
CN = CT * P
NC = NT // CT
CB = CN // SQ
HI, LO = 0, 1
PASSES = ((HI, HI), (HI, LO), (LO, HI))

WS = 64.0
PS_LN = 8.317766166719343
SM = HD ** -0.5 / (WS * WS)

WQ, WK, WV, WO, WTK, WTV, WTR, WTO, WR2, WK2, WG = (0, 256, 512, 768, 1024, 1280, 1536, 1792, 2048, 2304, 3328)
NW = WG + NE
NWA = WTK
BQ, BK, BV, LN1, LN2, TD, TF, MK, MV, MR, MK2, MR2 = range(12)
NV = 12
RT = 2 * P
REG = TOK + RT
TPE = TOK // RT
NTILE = (2 * TOK + NE * (RT - 1)) // RT
R_BASE, R_TILE, R_AFTER, R_J = 0, NE, NE + TPE, NE + TPE + NE * NE
NRC = R_J + NTILE


class Trail:

    def __init__(self, eng, sem, wait=None):
        self.eng, self.sem, self.base, self.k = eng, sem, 0, 0
        self.wait = wait or (lambda eng, sem, n: eng.wait_ge(sem, n))

    def mark(self, ins):
        ins.then_inc(self.sem, 1)
        self.k += 1
        return self.base + self.k

    def link(self, ins):
        self.wait(self.eng, self.sem, self.mark(ins))

    def enter(self, i, per):
        self.outer, self.per = self.base + self.k, per
        self.base, self.k = self.outer + i * per, 0

    def leave(self, times):
        assert self.k == self.per, f"{self.k} steps of {self.sem}, not {self.per}"
        self.base, self.k = self.outer + times * self.per, 0

ARENA = 212800 // 4


def need(eng, sem, n):
    if not (isinstance(n, int) and n <= 0):
        eng.wait_ge(sem, n)


def perceiver_layer(nc, x, ctx_t, ctx_last, w_all, w_value2, vecs, bo, route_consts, w1, b1, w2, b2, out):
    stack = ExitStack()
    with stack:
        def sem(name):
            return stack.enter_context(nc.semaphore(name))

        routed = nc.dram_tensor("routed", (NE * REG, D), F32).ap()
        returned = nc.dram_tensor("returned", (NTILE * RT, D), F32).ap()

        arena = stack.enter_context(nc.sbuf_tensor("arena", [P, ARENA], F32))
        PS = stack.enter_context(nc.psum_tensor("PS", [P, 8, 512], F32))
        at = {}

        def place(name, off, shape, dt=F32):
            n = 1
            for s in shape:
                n *= s
            size = n * (2 if dt == F16 else 4)
            size = (size + 31) // 32 * 32
            assert off % 4 == 0 and off + size <= ARENA * 4, (name, off, size)
            flat = arena[:, off // 4:(off + size) // 4]
            if dt != F32:
                flat = flat.bitcast(dt)
            flat = flat[:, 0:n]
            at[name] = off + size
            if len(shape) == 1:
                return flat
            names = " ".join(f"d{i}" for i in range(len(shape)))
            return flat.rearrange(f"p ({names}) -> p {names}", **{f"d{i}": s for i, s in enumerate(shape)})

        W16 = place("W16", 0, [KC, 2, NW], F16)
        WV2 = place("WV2", at["W16"], [FC, 2, D], F16)
        x_all = place("x_all", at["WV2"], [NT, D])
        vec = place("vec", at["x_all"], [NV, KC])
        vec64 = place("vec64", at["vec"], [NV, KC])
        ident = place("ident", at["vec64"], [P])
        neghalf = place("neghalf", at["ident"], [NT])
        logits = place("logits", at["neghalf"], [NT, NE])
        gate = place("gate", at["logits"], [NT, NE])
        rank = place("rank", at["gate"], [NT, NE])
        row_of = place("row_of", at["rank"], [NT, NE])
        taken = place("taken", at["row_of"], [NT, NE], F16)
        before = place("before", at["taken"], [NT + 1, NE], F16)
        picked = place("picked", at["before"], [2, CT, NE])
        rows_f = place("rows_f", at["picked"], [2, CT])
        rows_u = place("rows_u", at["rows_f"], [2, CT], U32)
        mx = place("mx", at["rows_u"], [CT])
        rc = place("rc", at["mx"], [NRC])
        earlier = place("earlier", at["rc"], [P], F16)
        ones16 = place("ones16", at["earlier"], [P], F16)
        aoT = place("aoT", at["ones16"], [KC, 2, TOK], F16)
        A0 = at["aoT"]
        qT = place("qT", A0, [KC, 2, TOK], F16)
        vlast = place("vlast", at["qT"], [NT, 2, D], F16)
        ctxf = place("ctxf", at["vlast"], [BT, KC, SK])
        ctx16 = place("ctx16", at["ctxf"], [2, KC, 2, SK + 1], F16)
        Kt = place("Kt", at["ctx16"], [2, 2, 2, SK + 1], F16)
        Vt = place("Vt", at["Kt"], [BT, 2, 2, D], F16)
        Pr = place("Pr", at["Vt"], [2, 2, SK])
        PT = place("PT", at["Pr"], [2, 4 * P], F16)
        PTl = place("PTl", at["PT"], [2, P], F16)
        plast = place("plast", at["PTl"], [2, BT, 2, BT])
        Qbd = place("Qbd", at["plast"], [2, 4, 2, 8 * SQ], F16)
        vlc = place("vlc", at["Qbd"], [2, 2, D], F16)
        Om = place("Om", at["vlc"], [2, P])
        Om16 = place("Om16", at["Om"], [4, 2, P], F16)
        aoF = place("aoF", at["Om16"], [KC, P])
        nm = place("nm", at["aoF"], [2, 2])
        nb = place("nb", at["nm"], [2, 2])
        den = place("den", at["nb"], [2, 2])
        rec = place("rec", at["den"], [2, 2])
        mask8 = place("mask8", at["rec"], [8])
        maskO = place("maskO", at["mask8"], [4, HD])
        maskV = place("maskV", at["maskO"], [2, 2, 64])
        sel16 = place("sel16", at["maskV"], [SQ], F16)
        S0 = at["sel16"]
        stage = place("stage", S0, [KC, NW])
        stage2 = place("stage2", at["stage"], [FC, D])
        xn = place("xn", at["stage2"], [2, CT, D])
        xT = place("xT", at["xn"], [2, KC, 2, CN], F16)
        clf = place("clf", at["xT"], [KC, NT, 8])
        cl16 = place("cl16", at["clf"], [KC, 2, NT, 8], F16)
        vlf = place("vlf", at["cl16"], [2, 2, D])
        bo_bc = place("bo_bc", at["vlf"], [D])
        st0 = place("st0", at["bo_bc"], [NT, 6])
        mv0 = place("mv0", at["st0"], [NT, 2])
        ve0 = place("ve0", at["mv0"], [NT])
        rs0 = place("rs0", at["ve0"], [NT])

        vecs_in, wa_in, wb_in, bo_in, rc_in, cl_in = sem("vecs_in"), sem("wa_in"), sem("wb_in"), sem("bo_in"), sem("rc_in"), sem("cl_in")
        x_in = [sem(f"x_in{c}") for c in range(NC)]
        ctx_in = [sem(f"ctx_in{b}") for b in range(BT)]
        consts, wa_ready, wb_ready = sem("consts"), sem("wa_ready"), sem("wb_ready")
        var_ready, rstd_ready, xn_ready = sem("var_ready"), sem("rstd_ready"), sem("xn_ready")
        xt_ps, xt_hi, xt_split = sem("xt_ps"), sem("xt_hi"), sem("xt_split")
        q_ps, q_hi, q_split = sem("q_ps"), sem("q_hi"), sem("q_split")
        cl_split, vl_ps, vl_evac, vl_split = sem("cl_split"), sem("vl_ps"), sem("vl_evac"), sem("vl_split")
        ctx_split = sem("ctx_split")
        k_ps, k_hi, k_split = sem("k_ps"), sem("k_hi"), sem("k_split")
        v_ps, v_hi, v_split = sem("v_ps"), sem("v_hi"), sem("v_split")
        qbd, vl_now, scores, negmax, probs, p_last = sem("qbd"), sem("vl_now"), sem("scores"), sem("negmax"), sem("probs"), sem("p_last")
        pt_ps, pt_hi, pt_split, pv = sem("pt_ps"), sem("pt_hi"), sem("pt_split"), sem("pv")
        o_masked, o_split, selected, ao_evac, ao_split = sem("o_masked"), sem("o_split"), sem("selected"), sem("ao_evac"), sem("ao_split")
        xbo_ready = sem("xbo_ready")
        ptl_ps, ptl_hi = sem("ptl_ps"), sem("ptl_hi")
        dve_step, pool_step = sem("dve_step"), sem("pool_step")

        wait_value = {}

        def wait_apart(eng, sem, n):
            if not isinstance(n, int):
                if eng not in wait_value:
                    wait_value[eng] = eng.alloc_register("wait_value")
                eng.reg_mov(wait_value[eng], n)
                n = wait_value[eng]
                eng.wait_ge(consts, 1)
            eng.wait_ge(sem, n)


        NR = 3
        h2T = place("h2T", A0, [KC, CB, SQ + 1])
        d2T = place("d2T", at["h2T"], [KC, CN])
        h2N = place("h2N", at["d2T"], [CT, D])
        mix2f = place("mix2f", at["h2N"], [2, CN])
        mix216 = place("mix216", at["mix2f"], [2, KC, 2, CN], F16)
        r2N = place("r2N", at["mix216"], [CT, D])
        reluf = place("reluf", at["r2N"], [NR, CN])
        xn3 = place("xn3", at["reluf"], [CT, D])
        k216 = place("k216", at["xn3"], [FC, 2, CN], F16)
        st3 = place("st3", at["k216"], [CT, 6])
        mv3 = place("mv3", at["st3"], [CT, 2])
        ve3 = place("ve3", at["mv3"], [CT])
        rs3 = place("rs3", at["ve3"], [CT])
        ew = place("ew", at["rs3"], [2, KC])
        st1 = place("st1", at["ew"], [CT, 6])
        mv1 = place("mv1", at["st1"], [CT, 2])
        ve1 = place("ve1", at["mv1"], [2, CT])
        rs1 = place("rs1", at["ve1"], [2, CT])
        shift1 = place("shift1", at["rs1"], [CT])
        st2 = place("st2", at["shift1"], [CT, 6])
        mv2 = place("mv2", at["st2"], [CT, 2])
        ve2 = place("ve2", at["mv2"], [CT])
        rs2 = place("rs2", at["ve2"], [CT])
        xl = place("xl", at["rs2"], [CT, D])
        hN = place("hN", at["xl"], [CT, D])
        hT = place("hT", at["hN"], [KC, CB, SQ + 1])
        dT = place("dT", at["hT"], [KC, CN])
        mixf = place("mixf", at["dT"], [2, CN])
        mix16 = place("mix16", at["mixf"], [3, KC, 2, CN], F16)
        ek = place("ek", at["mix16"], [KC, CN])
        eu = place("eu", at["ek"], [KC, CN])
        vS = place("vS", at["eu"], [KC, CN])
        rS = place("rS", at["vS"], [KC, CN])
        ekp = place("ekp", at["rS"], [KC, CB, SQ + 1])
        ekvp = place("ekvp", at["ekp"], [KC, CB, SQ + 1])
        num = place("num", at["ekvp"], [2, CB, SQ + 1])
        dnm = place("dnm", at["num"], [2, CB, SQ + 1])
        top = place("top", at["dnm"], [2, CN])
        bot = place("bot", at["top"], [2, CN])
        rw16 = place("rw16", at["bot"], [KC, 2, CN], F16)
        decay = place("decay", at["rw16"], [KC, CB, SQ + 1])
        euv = dT
        flat_hN = hN.rearrange("p t n -> p (t n)")
        x3T = flat_hN.bitcast(F16).rearrange("p (k a n) -> p k a n", k=KC, a=2)
        cmp1, cmp2 = (flat_hN[:, i * CT * NE * NE:(i + 1) * CT * NE * NE].rearrange("p (t e j) -> p t e j", e=NE, j=NE) for i in range(2))
        yN = bot.rearrange("p k n -> p (k n)").rearrange("p (t n) -> p t n", t=CT)
        W2_AT = KC * 2 * FF
        experts = place("experts", ARENA * 4 - NE * 2 * W2_AT * 2, [NE, 2 * W2_AT], F16)
        w1f = place("w1f", at["ones16"], [KC, FF])
        w2f = place("w2f", at["w1f"], [FC, D])

        (sm_in, sm_exp, before_ready, count_ps, total_ps, rows_ready, routed_sent, w1_in, w2_in, w1_ready, w2_ready) = [sem(n) for n in (
            "sm_in sm_exp before_ready count_ps total_ps rows_ready routed_sent w1_in w2_in w1_ready w2_ready").split()]
        (c_ew, wo_ps, tm_var, tm_rs, tm_norm, h_ps, h_t, d_t, mixed, mix_hi, mix_lo, kvr_ps, kvr_out, eu_v, rwf, rw_hi, rw_lo,
         wout_ps, y_var, y_rs, h2_n, h2_ps, h2_t, d2_t, mixed2, mix2_hi, mix2_lo, key_ps, relu_out, sq_out, k2_hi, k2_lo, r2_ps, r2_out,
         val_ps, x2_var, x2_rs, xn3_done, x3_ps, x3_hi, x3_lo, lg_ps, lg_out) = [sem(n) for n in (
            "c_ew wo_ps tm_var tm_rs tm_norm h_ps h_t d_t mixed mix_hi mix_lo kvr_ps kvr_out eu_v rwf rw_hi rw_lo "
            "wout_ps y_var y_rs h2_n h2_ps h2_t d2_t mixed2 mix2_hi mix2_lo key_ps relu_out sq_out k2_hi k2_lo r2_ps r2_out "
            "val_ps x2_var x2_rs xn3_done x3_ps x3_hi x3_lo lg_ps lg_out").split()]

        top_ready, hn_done = sem("top_ready"), sem("hn_done")
        E20, EM20 = 485165195.4097903, 2.061153622438558e-09
        H2_BANKS = (4, 7)
        fold = lambda ap: ap.rearrange("p (b q) -> p b q", q=SQ)

        def chunk_steps(step):
            for s in range(NC + 2):
                step(s, s < NC, 1 <= s <= NC, s >= 2, s + 1 < NC)

        def tiles_of(c, i, n):
            return x_all[:, c * CT + i:c * CT + i + n]

        def rwkv_pool(pool, own):
            g = nc.gpsimd

            def minus(out, a, b):
                return g.tensor_tensor(out, a, b, ALU.subtract)

            def difference(dst, src):
                for k in range(KC):
                    ins = minus(fold(dst[:, k]), src[:, k, :, 1:], src[:, k, :, 0:SQ])
                return ins

            def first_rs(a):
                pool.wait_ge(tm_var, a + 1)
                g.tensor_tensor(rs1, ve1, neghalf[:, 0:2 * CT].rearrange("p (a b) -> p a b", a=2), ALU.pow).then_inc(tm_rs, 1)

            def first_difference(a):
                pool.wait_ge(h_t, a + 1)
                difference(dT, hT).then_inc(d_t, 1)

            def load_w1(e):
                g.dma_start(w1f, w1[e].rearrange("(k p) f -> p k f", p=P)).then_inc(w1_in, 16)

            def load_w2(e):
                g.dma_start(w2f, w2[e].rearrange("(f p) d -> p f d", p=P)).then_inc(w2_in, 16)

            def split(f32, hi, lo, ready):
                own.link(g.tensor_scalar(f32, f32, WS, 0.0, ALU.mult, ALU.add))
                own.link(g.tensor_scalar(hi, f32, 1.0, 0.0, ALU.mult, ALU.add))
                g.tensor_tensor(lo, f32, hi, ALU.subtract).then_inc(ready, 1)

            def split_w1(e):
                pool.wait_ge(w1_in, 16 * (NE - e))
                w = experts[:, e, 0:W2_AT].rearrange("p (k a f) -> p k a f", k=KC, a=2)
                split(w1f, w[:, :, HI], w[:, :, LO], w1_ready)
                if e:
                    pool.wait_ge(w1_ready, NE - e)
                    load_w1(e - 1)

            def split_w2(e):
                pool.wait_ge(w2_in, 16 * (NE - e))
                w = experts[:, e, W2_AT:].rearrange("p (f a d) -> p f a d", f=FC, a=2)
                split(w2f, w[:, :, HI], w[:, :, LO], w2_ready)
                if e:
                    pool.wait_ge(w2_ready, NE - e)
                    load_w2(e - 1)

            def scatter(c):
                if c == NC - 1:
                    g.memset(zeros, 0.0).then_inc(zeros_ready, 1)
                pool.wait_ge(rows_ready, c + 1)
                for n in range(2):
                    for i in range(CT):
                        g.indirect_dma_start(routed, bass.IndirectOffsetOnAxis(ap=rows_u[:, n, i:i + 1], axis=0), xn3[:, i], None
                                             ).then_inc(routed_sent, 16)

            def step(s, tm, cm, rt, nx):
                c = s - 1

                def mixed2_lo(m):
                    for k in range(KC):
                        pool.wait_ge(mix2_hi, c * 4 + 2 * m + k + 1)
                        minus(mix216[:, m, k, LO], mix2f[:, k], mix216[:, m, k, HI]).then_inc(mix2_lo, 1)

                def euv_of(o):
                    pool.wait_ge(eu_v, s * 2 + o + 1)
                    g.tensor_tensor(euv[:, o], eu[:, o], vS[:, o], ALU.mult).then_inc(rwf, 1)

                def rw_lo_of(o):
                    pool.wait_ge(rw_hi, s * 2 + o + 1)
                    minus(rw16[:, o, LO], top[:, o], rw16[:, o, HI]).then_inc(rw_lo, 1)

                def k2_lo_of(fs):
                    for f in fs:
                        pool.wait_ge(k2_hi, c * 8 + f + 1)
                        minus(k216[:, f, LO], reluf[:, f % NR], k216[:, f, HI]).then_inc(k2_lo, 1)

                if s == NC - 1:
                    pool.wait_ge(wo_ps, 2 * NC)
                    load_w1(NE - 1)
                    load_w2(NE - 1)
                if tm:
                    for m in range(3):
                        for k in range(KC):
                            pool.wait_ge(mix_hi, s * 6 + 2 * m + k + 1)
                            minus(mix16[:, m, k, LO], mixf[:, k], mix16[:, m, k, HI]).then_inc(mix_lo, 1)
                if cm:
                    mixed2_lo(0)
                    mixed2_lo(1)
                if s == NC:
                    split_w1(NE - 1)
                if tm:
                    euv_of(0)
                if cm:
                    k2_lo_of(range(1))
                if tm:
                    rw_lo_of(0)
                    euv_of(1)
                if cm:
                    k2_lo_of(range(1, 4))
                if tm:
                    rw_lo_of(1)
                if cm:
                    k2_lo_of(range(4, 6))
                if nx:
                    first_rs(s + 1)
                if cm:
                    k2_lo_of(range(6, 8))
                if tm:
                    pool.wait_ge(y_var, s + 1)
                    g.tensor_tensor(rs2, ve2, neghalf[:, 0:CT], ALU.pow).then_inc(y_rs, 1)
                if nx:
                    first_difference(s + 1)
                if rt:
                    scatter(s - 2)
                if tm:
                    pool.wait_ge(h2_t, s + 1)
                    difference(d2T, h2T).then_inc(d2_t, 1)
                if cm:
                    pool.wait_ge(x2_var, s)
                    g.tensor_tensor(rs3, ve3, neghalf[:, 0:CT], ALU.pow).then_inc(x2_rs, 1)
                if s == NC:
                    split_w2(NE - 1)

            first_rs(0)
            first_difference(0)
            chunk_steps(step)
            pool.wait_ge(routed_sent, NC * (2 * CT * 16))
            return split_w1, split_w2

        def rwkv_scalar(act):
            a = nc.scalar
            pad = lambda t, k: t[:, k, :, 1:]
            a.activation(ew[:, 0], vec[:, TD], ACT.Exp).then_inc(c_ew, 1)
            act.wait_ge(c_ew, 2)
            a.activation(ew[:, 1], ew[:, 0], ACT.Exp).then_inc(c_ew, 1)

            def front_rows(c):
                act.wait_ge(tm_norm, c + 1)
                for i in range(CT):
                    ins = a.activation(hN[:, i], tiles_of(c, i, 1).squeeze(1), ACT.Identity, bias=shift1[:, i:i + 1], scale=rs1[:, 1, i:i + 1])
                ins.then_inc(hn_done, 1)

            def front_transposed(c):
                act.wait_ge(h_ps, c + 1)
                for k in range(KC):
                    ins = a.activation(pad(hT, k), fold(PS[:, k]), ACT.Copy, scale=vec[:, LN1, k:k + 1])
                ins.then_inc(h_t, 1)

            def step(s, tm, cm, rt, nx):
                c = s - 1
                if tm:
                    for m in range(3):
                        for k in range(KC):
                            act.wait_ge(mixed, s * 6 + 2 * m + k + 1)
                            a.activation(mix16[:, m, k, HI], mixf[:, k], ACT.Copy).then_inc(mix_hi, 1)
                        if m == 1:
                            for o in range(KC):
                                act.wait_ge(kvr_ps, s * 6 + o + 1)
                                need(act, top_ready, s * 2)
                                a.activation(ek[:, o], PS[:, o], ACT.Exp, scale=1 / WS)
                                a.activation(eu[:, o], PS[:, o], ACT.Exp, scale=1 / WS, bias=vec[:, TF, o:o + 1]).then_inc(kvr_out, 1)
                if cm:
                    for m in range(2):
                        for k in range(KC):
                            act.wait_ge(mixed2, c * 4 + 2 * m + k + 1)
                            a.activation(mix216[:, m, k, HI], mix2f[:, k], ACT.Copy).then_inc(mix2_hi, 1)
                if rt:
                    act.wait_ge(x3_ps, c)
                    for k in range(KC):
                        ins = a.activation(x3T[:, k, HI], PS[:, 6 + k], ACT.Copy)
                    ins.then_inc(x3_hi, 1)
                if tm:
                    for o in range(KC):
                        act.wait_ge(kvr_ps, s * 6 + o + 3)
                        a.activation(vS[:, o], PS[:, 2 + o], ACT.Copy, scale=1 / WS).then_inc(kvr_out, 1)
                    for o in range(KC):
                        act.wait_ge(kvr_ps, s * 6 + o + 5)
                        a.activation(rS[:, o], PS[:, o], ACT.Tanh, scale=0.5 / WS).then_inc(kvr_out, 1)
                if rt:
                    act.wait_ge(lg_ps, c)
                    a.activation(logits[:, (s - 2) * CT:(s - 1) * CT], PS[:, 4, 0:CT * NE].rearrange("p (t e) -> p t e", e=NE),
                                 ACT.Copy, scale=1 / WS).then_inc(lg_out, 1)
                    act.wait_ge(sm_in, c)
                    chunk = gate[:, (s - 2) * CT:(s - 1) * CT]
                    a.activation(chunk, chunk, ACT.Exp).then_inc(sm_exp, 1)
                if cm:
                    for p in range(2):
                        act.wait_ge(r2_ps, c * 2 + p + 1)
                        a.activation(r2N[:, 2 * p:2 * p + 2], PS[:, 6 + p].rearrange("p (a n) -> p a n", a=2), ACT.Tanh,
                                     scale=0.5 / WS).then_inc(r2_out, 1)

                def relu(f):
                    act.wait_ge(key_ps, c * 8 + f + 1)
                    if f >= NR:
                        act.wait_ge(k2_lo, c * 8 + f - NR + 1)
                    a.activation(reluf[:, f % NR], PS[:, 5 + f % 3], ACT.Relu, scale=1 / WS).then_inc(relu_out, 1)

                def square(f):
                    act.wait_ge(relu_out, c * 8 + f + 1)
                    a.activation(reluf[:, f % NR], reluf[:, f % NR], ACT.Square).then_inc(sq_out, 1)

                def square_hi(f):
                    act.wait_ge(sq_out, c * 8 + f + 1)
                    a.activation(k216[:, f, HI], reluf[:, f % NR], ACT.Copy).then_inc(k2_hi, 1)

                def rw_high(o):
                    if tm:
                        act.wait_ge(top_ready, s * 2 + o + 1)
                        a.activation(rw16[:, o, HI], top[:, o], ACT.Copy).then_inc(rw_hi, 1)

                if cm:
                    relu(0)
                    for f in range(1, FC + 1):
                        square(f - 1)
                        if f < FC:
                            relu(f)
                        square_hi(f - 1)
                        if f == 1:
                            rw_high(0)
                        if f == 4:
                            rw_high(1)
                        if f == 6 and nx:
                            front_rows(s + 1)
                elif tm:
                    rw_high(0)
                    rw_high(1)
                    front_rows(s + 1)
                if nx:
                    front_transposed(s + 1)
                if tm:
                    act.wait_ge(y_rs, s + 1)
                    for i in range(CT):
                        ins = a.activation(h2N[:, i], yN[:, i], ACT.Copy, scale=rs2[:, i:i + 1])
                    ins.then_inc(h2_n, 1)
                    act.wait_ge(h2_ps, s + 1)
                    for k in range(KC):
                        ins = a.activation(pad(h2T, k), fold(PS[:, H2_BANKS[k]]), ACT.Copy, scale=vec[:, LN2, k:k + 1])
                    ins.then_inc(h2_t, 1)

            front_rows(0)
            front_transposed(0)
            chunk_steps(step)

        def rwkv_vector(dve, own):
            v = nc.vector
            for t in (hT, h2T, ekp, ekvp):
                v.memset(t[:, :, :, 0:1], 0.0)
            own.mark(v.memset(before[:, 0:1], 0.0))
            own.link(v.memset(decay, 0.0))
            dve.wait_ge(c_ew, 1)
            v.tensor_scalar(ew[:, 0], ew[:, 0], -1.0, -20.0, ALU.mult, ALU.max).then_inc(c_ew, 1)
            dve.wait_ge(c_ew, 3)
            own.link(v.tensor_copy(decay[:, :, :, 1:], ew[:, 1].unsqueeze(2).unsqueeze(3).to_broadcast([P, KC, CB, SQ])))
            lower = rc[:, R_AFTER:R_AFTER + NE * NE].rearrange("p (e j) -> p e j", j=NE)

            def stats(st, mv, src):
                for i in range(CT):
                    n = own.mark(v.bn_stats(st[:, i], src(i)))
                wait_apart(dve, dve_step, n)
                for i in range(CT):
                    n = own.mark(v.bn_aggr(mv[:, i], st[:, i]))
                dve.wait_ge(dve_step, n)

            def front(c):
                for p in range(2):
                    dve.wait_ge(wo_ps, c * 2 + p + 1)
                    rows = tiles_of(c, 2 * p, 2)
                    n = own.mark(v.scalar_tensor_tensor(rows, PS[:, p].rearrange("p (a n) -> p a n", a=2), 1 / WS, rows, ALU.mult, ALU.add))
                wait_apart(dve, dve_step, n)
                stats(st1, mv1, lambda i: tiles_of(c, i, 1).squeeze(1))
                own.mark(v.tensor_scalar(ve1[:, 0], mv1[:, :, 1], 1e-5, None, ALU.add))
                v.tensor_scalar(ve1[:, 1], mv1[:, :, 1], 1.0 + 1e-6, 1e-11, ALU.mult, ALU.add).then_inc(tm_var, 1)
                dve.wait_ge(tm_rs, c + 1)
                v.scalar_tensor_tensor(shift1, mv1[:, :, 0], -1.0, rs1[:, 1], ALU.mult, ALU.mult).then_inc(tm_norm, 1)

            def first_norm(c):
                for i in range(CT):
                    own.mark(v.tensor_scalar(xl[:, i], tiles_of(c, i, 1).squeeze(1), mv1[:, i, 0:1], rs1[:, 0, i:i + 1], ALU.subtract, ALU.mult))

            def gates(c):
                tiles = slice(c * CT, (c + 1) * CT)
                bc_e = lambda t: t.unsqueeze(2).to_broadcast([P, CT, NE])
                full = [P, CT, NE, NE]
                dve.wait_ge(lg_out, c + 1)
                own.link(v.tensor_reduce(mx, logits[:, tiles], AX.X, ALU.max))
                v.tensor_tensor(gate[:, tiles], logits[:, tiles], bc_e(mx), ALU.subtract).then_inc(sm_in, 1)
                dve.wait_ge(sm_exp, c + 1)
                own.link(v.tensor_reduce(mx, gate[:, tiles], AX.X, ALU.add))
                own.link(v.reciprocal(mx, mx))
                own.link(v.tensor_tensor(gate[:, tiles], gate[:, tiles], bc_e(mx), ALU.mult))
                of_j, of_e = gate[:, tiles].unsqueeze(2).to_broadcast(full), gate[:, tiles].unsqueeze(3).to_broadcast(full)
                own.mark(v.tensor_tensor(cmp1, of_j, of_e, ALU.is_gt))
                own.link(v.tensor_tensor(cmp2, of_j, of_e, ALU.is_equal))
                own.link(v.tensor_tensor(cmp2, cmp2, lower.unsqueeze(1).to_broadcast(full), ALU.mult))
                own.link(v.tensor_tensor(cmp1, cmp1, cmp2, ALU.add))
                own.link(v.tensor_reduce(rank[:, tiles], cmp1, AX.X, ALU.add))
                own.link(v.tensor_scalar(taken[:, tiles], rank[:, tiles], 2.0, None, ALU.is_lt))
                for t in range(c * CT, (c + 1) * CT):
                    ins = v.tensor_tensor(before[:, t + 1], before[:, t], taken[:, t], ALU.add)
                    if t < (c + 1) * CT - 1:
                        own.link(ins)
                ins.then_inc(before_ready, 1)

            def places(c):
                tiles = slice(c * CT, (c + 1) * CT)
                dve.wait_ge(count_ps, c + 1)
                counts = PS[:, 4, 64:64 + CT * NE].rearrange("p (t e) -> p t e", e=NE)
                own.link(v.tensor_tensor(row_of[:, tiles], counts, rc[:, R_BASE:R_BASE + NE].unsqueeze(1).to_broadcast([P, CT, NE]), ALU.add))
                own.mark(v.scalar_tensor_tensor(picked[:, 0], rank[:, tiles], 0.0, row_of[:, tiles], ALU.is_equal, ALU.mult))
                own.link(v.scalar_tensor_tensor(picked[:, 1], rank[:, tiles], 1.0, row_of[:, tiles], ALU.is_equal, ALU.mult))
                own.link(v.tensor_reduce(rows_f, picked, AX.X, ALU.add))
                need(dve, routed_sent, c * (2 * CT * 16))
                v.tensor_copy(rows_u, rows_f).then_inc(rows_ready, 1)

            def wkv(s, o):
                dve.wait_ge(kvr_out, s * 6 + o + 1)
                own.mark(v.tensor_scalar(ekp[:, o, :, 1:], fold(ek[:, o]), EM20, E20, ALU.max, ALU.min))
                own.link(v.tensor_scalar(eu[:, o], eu[:, o], EM20, E20, ALU.max, ALU.min))
                dve.wait_ge(kvr_out, s * 6 + o + 3)
                own.mark(v.tensor_tensor(ekvp[:, o, :, 1:], ekp[:, o, :, 1:], fold(vS[:, o]), ALU.mult))
                v.tensor_tensor_scan(dnm[:, o].rearrange("p b q -> p (b q)"), decay[:, o].rearrange("p b q -> p (b q)"),
                                     ekp[:, o].rearrange("p b q -> p (b q)"), 0.0, ALU.mult, ALU.add).then_inc(eu_v, 1)
                dve.wait_ge(eu_v, s * 2 + o + 1)
                own.mark(v.scalar_tensor_tensor(fold(bot[:, o]), dnm[:, o, :, 0:SQ], 1e-8, fold(eu[:, o]), ALU.add, ALU.add))
                own.link(v.tensor_tensor_scan(num[:, o].rearrange("p b q -> p (b q)"), decay[:, o].rearrange("p b q -> p (b q)"),
                                              ekvp[:, o].rearrange("p b q -> p (b q)"), 0.0, ALU.mult, ALU.add))
                own.mark(v.reciprocal(bot[:, o], bot[:, o]))
                dve.wait_ge(rwf, s * 2 + o + 1)
                own.link(v.tensor_tensor(fold(top[:, o]), num[:, o, :, 0:SQ], fold(euv[:, o]), ALU.add))
                own.link(v.tensor_tensor(top[:, o], top[:, o], bot[:, o], ALU.mult))
                dve.wait_ge(kvr_out, s * 6 + o + 5)
                v.scalar_tensor_tensor(top[:, o], rS[:, o], 1.0, top[:, o], ALU.add, ALU.mult).then_inc(top_ready, 1)

            def mix(s, m):
                if m == 0:
                    dve.wait_ge(d_t, s + 1)
                for k in range(KC):
                    need(dve, mix_lo, s * 6 + 2 * m + k - 1)
                    v.scalar_tensor_tensor(fold(mixf[:, k]), fold(dT[:, k]), vec[:, MK + m, k:k + 1], hT[:, k, :, 0:SQ],
                                           ALU.mult, ALU.add).then_inc(mixed, 1)

            def step(s, tm, cm, rt, nx):
                c = s - 1
                if tm:
                    mix(s, 1)
                    mix(s, 2)
                if cm:
                    dve.wait_ge(d2_t, s)

                    for m, col in ((0, MK2), (1, MR2)):
                        for k in range(KC):
                            need(dve, mix2_lo, c * 4 + 2 * m + k - 1)
                            v.scalar_tensor_tensor(fold(mix2f[:, k]), fold(d2T[:, k]), vec[:, col, k:k + 1], h2T[:, k, :, 0:SQ],
                                                   ALU.mult, ALU.add).then_inc(mixed2, 1)
                if rt:
                    dve.wait_ge(x3_hi, c)
                    for k in range(KC):
                        ins = v.tensor_tensor(x3T[:, k, LO], PS[:, 6 + k], x3T[:, k, HI], ALU.subtract)
                    ins.then_inc(x3_lo, 1)
                if tm:
                    wkv(s, 0)
                if rt:
                    gates(s - 2)
                if tm:
                    wkv(s, 1)
                if rt:
                    places(s - 2)
                if nx:
                    front(s + 1)
                if tm:
                    for p in range(2):
                        dve.wait_ge(wout_ps, s * 2 + p + 1)
                        pair = slice(2 * p, 2 * p + 2)
                        n = own.mark(v.scalar_tensor_tensor(yN[:, pair], PS[:, 2 + p].rearrange("p (a n) -> p a n", a=2), 0.5 / WS, xl[:, pair],
                                                            ALU.mult, ALU.add))
                    wait_apart(dve, dve_step, n)
                    stats(st2, mv2, lambda i: yN[:, i])
                    own.link(v.tensor_tensor(ve2, mv2[:, :, 0], mv2[:, :, 0], ALU.mult))
                    v.scalar_tensor_tensor(ve2, ve2, 1e-6, mv2[:, :, 1], ALU.add, ALU.add).then_inc(y_var, 1)
                    rows = tiles_of(s, 0, CT)
                    own.mark(v.tensor_tensor(rows, rows, yN, ALU.add))
                if nx:
                    first_norm(s + 1)
                if cm:
                    dve.wait_ge(r2_out, s * 2)
                    for p in range(2):
                        dve.wait_ge(val_ps, c * 2 + p + 1)
                        n = own.mark(v.scalar_tensor_tensor(r2N[:, 2 * p:2 * p + 2], r2N[:, 2 * p:2 * p + 2], 1.0,
                                                            PS[:, 5 + p].rearrange("p (a n) -> p a n", a=2), ALU.add, ALU.mult))
                    dve.wait_ge(dve_step, n)
                    rows = tiles_of(c, 0, CT)
                    n = own.mark(v.scalar_tensor_tensor(rows, r2N, 0.5 / WS, rows, ALU.mult, ALU.add))
                    dve.wait_ge(dve_step, n)
                    stats(st3, mv3, lambda i: tiles_of(c, i, 1).squeeze(1))
                    v.tensor_scalar(ve3, mv3[:, :, 1], 1e-5, None, ALU.add).then_inc(x2_var, 1)
                if nx:
                    mix(s + 1, 0)
                if cm:
                    dve.wait_ge(x2_rs, s)
                    need(dve, routed_sent, c * (2 * CT * 16))
                    for i in range(CT):
                        ins = v.tensor_scalar(xn3[:, i], tiles_of(c, i, 1).squeeze(1), mv3[:, i, 0:1], rs3[:, i:i + 1], ALU.subtract, ALU.mult)
                    ins.then_inc(xn3_done, 1)

            front(0)
            first_norm(0)
            mix(0, 0)
            chunk_steps(step)

        def rwkv_tensor(pe):
            te = nc.tensor

            def product(out, pairs):
                n, last = 0, 3 * len(pairs) - 1
                for lhs, rhs in pairs:
                    for a, b in PASSES:
                        ins = te.matmul(out, lhs(a), rhs(b), start=n == 0, stop=n == last)
                        n += 1
                return ins

            def w(k, col, n=P):
                return lambda part: W16[:, k, part, col:col + n]

            def rows_out(bank, pairs_of, done, tiles=range(CT)):
                for i in tiles:
                    ins = product(PS[:, bank + i // 2, D * (i % 2):D * (i % 2 + 1)], pairs_of(i))
                    if i % 2:
                        ins.then_inc(done, 1)

            def transposed(banks, rows, done):
                for k in range(KC):
                    for i in range(CT):
                        ins = te.transpose(PS[:, banks[k], P * i:P * (i + 1)], rows[:, i, P * k:P * (k + 1)], ident)
                ins.then_inc(done, 1)

            def wo(c):
                pe.wait_ge(ao_split, c * CT + CT)
                rows_out(0, lambda i: [((lambda part, k=k: aoT[:, k, part, c * CN + i * P:c * CN + (i + 1) * P]), w(k, WO, D)) for k in range(KC)],
                         wo_ps)

            def first_rows(c):
                pe.wait_ge(hn_done, c + 1)
                transposed((0, 1), hN, h_ps)

            def step(s, tm, cm, rt, nx):
                c, r = s - 1, s - 2

                def kvr(m, col):
                    pe.wait_ge(mix_lo, s * 6 + 2 * m + 2)
                    for o in range(KC):
                        if m == 2:
                            pe.wait_ge(kvr_out, s * 6 + o + 1)
                        product(PS[:, (2 * m + o) % 4], [(w(k, col + P * o), lambda part, k=k: mix16[:, m, k, part]) for k in range(KC)]
                                ).then_inc(kvr_ps, 1)

                if tm:
                    pe.wait_ge(h_t, s + 1)
                    kvr(0, WTK)
                if rt:
                    pe.wait_ge(xn3_done, c)
                    need(pe, h2_t, min(s, NC))
                    transposed((6, 7), xn3, x3_ps)
                if tm:
                    need(pe, y_var, s)
                    kvr(1, WTV)
                    kvr(2, WTR)
                if rt:
                    pe.wait_ge(x3_lo, c)
                    for i in range(CT):
                        ins = product(PS[:, 4, NE * i:NE * (i + 1)],
                                      [(lambda part, k=k: x3T[:, k, part, P * i:P * (i + 1)], w(k, WG, NE)) for k in range(KC)])
                    ins.then_inc(lg_ps, 1)
                if nx:
                    pe.wait_ge(kvr_out, s * 6 + 6)
                    wo(s + 1)
                if cm:
                    pe.wait_ge(mix2_lo, c * 4 + 4)
                    pe.wait_ge(h2_t, s)
                    rows_out(6, lambda i: [(lambda part, k=k: mix216[:, 1, k, part, P * i:P * (i + 1)], w(k, WR2, D)) for k in range(KC)], r2_ps)

                def key(f):
                    if 1 <= f < 3:
                        pe.wait_ge(r2_out, c * 2 + f)
                    if f >= 3:
                        pe.wait_ge(relu_out, c * 8 + f - 2)
                    product(PS[:, 5 + f % 3], [(w(k, WK2 + P * f), lambda part, k=k: mix216[:, 0, k, part]) for k in range(KC)]
                            ).then_inc(key_ps, 1)

                def takers():
                    pe.wait_ge(before_ready, c)
                    for i in range(CT):
                        out = PS[:, 4, 64 + NE * i:64 + NE * (i + 1)]
                        te.matmul(out, earlier, taken[:, r * CT + i], start=True, stop=False)
                        ins = te.matmul(out, ones16, before[:, r * CT + i], start=False, stop=True)
                    ins.then_inc(count_ps, 1)
                    if r == NC - 1:
                        te.matmul(PS[:, 5, 0:NE], ones16, before[:, NT], start=True, stop=True).then_inc(total_ps, 1)

                if cm:
                    for f in range(6):
                        key(f)
                if rt:
                    takers()
                if tm:
                    pe.wait_ge(rw_lo, s * 2 + 2)
                    pe.wait_ge(kvr_out, s * 6 + 4)
                    rows_out(2, lambda i: [(lambda part, k=k: rw16[:, k, part, P * i:P * (i + 1)], w(k, WTO, D)) for k in range(KC)], wout_ps)

                def val(tiles):
                    rows_out(5, lambda i: [(lambda part, f=f: k216[:, f, part, P * i:P * (i + 1)], lambda part, f=f: WV2[:, f, part])
                                           for f in range(FC)], val_ps, tiles)

                if cm:
                    for f in range(6, FC):
                        key(f)
                if nx:
                    first_rows(s + 1)
                if cm:
                    pe.wait_ge(k2_lo, s * 8)
                    val(range(CT))
                if tm:
                    pe.wait_ge(h2_n, s + 1)
                    need(pe, rows_ready, c)
                    transposed(H2_BANKS, h2N, h2_ps)

            pe.wait_ge(wb_ready, 8)
            wo(0)
            first_rows(0)
            chunk_steps(step)

        xg = place("xg", 0, [2, 2, D])
        x16 = place("x16", at["xg"], [2, KC, 2, RT], F16)
        gel = place("gel", at["x16"], [FC, RT])
        hid16 = place("hid16", at["gel"], [2, FC, 2, RT], F16)
        zeros = place("zeros", at["hid16"], [D])
        both = place("both", at["zeros"], [2, NT, NE])
        assert at["both"] <= at["WV2"], "over RWKV's weights"
        b1s = place("b1s", A0, [NE, FC])
        tiles_of_e = place("tiles_of_e", at["b1s"], [NE])
        ends = place("ends", at["tiles_of_e"], [NE])
        starts = place("starts", at["ends"], [NE])
        more = place("more", at["starts"], [NE, NE])
        past = place("past", at["more"], [NTILE, NE])
        expert_f = place("expert_f", at["past"], [NTILE])
        used = place("used", at["expert_f"], [NTILE])
        first_f = place("first_f", at["used"], [NTILE])
        table = place("table", at["first_f"], [3, NTILE], I32)
        pad_at = place("pad_at", at["table"], [NE], I32)
        early_f = place("early_f", at["pad_at"], [NTILE + 1])
        early = place("early", at["early_f"], [2], I32)
        weight = place("weight", at["early"], [2, NT])
        back_f = place("back_f", at["weight"], [2, NT])
        back_u = place("back_u", at["back_f"], [2, NT], U32)
        b2t = place("b2t", at["back_u"], [2, D])
        yS = place("yS", at["b2t"], [2, 2, D])
        gathered = place("gathered", ARENA * 4 - 2 * 2 * W2_AT * 2, [2, NT, D])
        assert at["yS"] <= ARENA * 4 - NE * 2 * W2_AT * 2

        (table_ready, pad_sent, zeros_ready, b1_in, t_ps, x_hi_out, x_lo_out, hid_ps, gel_out, g_hi, g_lo, y_ps, y_out, back_ready, added, stored, rows_filled, pad_ready) = [
            sem(n) for n in ("table_ready pad_sent zeros_ready b1_in t_ps x_hi_out x_lo_out hid_ps gel_out g_hi g_lo y_ps y_out "
                             "back_ready added stored rows_filled pad_ready").split()]
        xg_in = [sem("xg_in0"), sem("xg_in1")]
        b2_in = [sem("b2_in0"), sem("b2_in1")]
        y_sent = [sem("y_sent0"), sem("y_sent1")]
        gather_in = [[sem(f"gather_in{n}_{c}") for c in range(NC)] for n in range(2)]
        returned_v = returned.rearrange("(j u p) d -> p j u d", p=P, u=2)

        later = rc[:, R_AFTER:R_AFTER + NE * NE].rearrange("p (e j) -> p j e", j=NE)

        def expert_tiles(eng, step, trail=None, per=0):
            step(0, 0, 0)
            step(1, 0, 1)
            with eng.Fori(1, NTILE // 2) as i:
                if trail:
                    trail.enter(i - 1, per)
                for par in range(2):
                    step(i * 2 + par, i, par)
            if trail:
                trail.leave(NTILE // 2 - 1)
            step(NTILE - 1, NTILE // 2, 0)

        def last_tile(j):
            return isinstance(j, int) and j == NTILE - 1

        def moe_sync(sp):
            sp.wait_ge(zeros_ready, 1)
            sp.wait_ge(pad_ready, 1)
            for e in range(NE):
                at_row = sp.value_load(pad_at[0:1, e:e + 1], min_val=e * REG, max_val=e * REG + TOK)
                sp.dma_start(routed[bass.ds(at_row, RT)].rearrange("(u p) d -> p u d", p=P), zeros.unsqueeze(1).to_broadcast([P, 2, D])).then_inc(pad_sent, 16)
            sp.wait_ge(routed_sent, NC * 2 * CT * 16)
            sp.wait_ge(pad_sent, NE * 16)
            sp.wait_ge(table_ready, 1)

            def load(j, i, par):
                row = sp.value_load(table[0:1, 1, bass.ds(j, 1)], min_val=0, max_val=NE * REG - RT)
                sp.dma_start(xg[:, par], routed[bass.ds(row, RT)].rearrange("(u p) d -> p u d", p=P)).then_inc(xg_in[par], 16)

            def store(j, par):
                sp.wait_ge(y_out, j + 1)
                sp.dma_start(returned_v[:, bass.ds(j, 1)].squeeze(1), yS[:, par]).then_inc(y_sent[par], 16)

            def load_b2(j, par):
                e = sp.value_load(table[0:1, 0, bass.ds(j, 1)], min_val=0, max_val=NE - 1)
                sp.dma_start(b2t[:, par], b2[bass.ds(e, 1)].rearrange("e d -> (e d)").partition_broadcast(P)).then_inc(b2_in[par], 16)

            def step(j, i, par):
                if not (isinstance(j, int) and j + 2 >= NTILE):
                    sp.wait_ge(t_ps, j + 1)
                    load(j + 2, i + 1, par)
                if not (isinstance(j, int) and j == 0):
                    store(j - 1, 1 - par)
                if not last_tile(j):
                    load_b2(j + 1, 1 - par)

            load(0, 0, 0)
            load(1, 0, 1)
            load_b2(0, 0)
            step(0, 0, 0)
            step(1, 0, 1)
            with sp.Fori(1, NTILE // 2 - 1) as i:
                for par in range(2):
                    step(i * 2 + par, i, par)
            for j in range(NTILE - 3, NTILE):
                step(j, j // 2, j % 2)
            store(NTILE - 1, (NTILE - 1) % 2)
            for c in range(NC):
                sp.wait_ge(added, c + 1)
                sp.dma_start(out.rearrange("(t p) d -> p t d", p=P)[:, CT * c:CT * (c + 1)], x_all[:, CT * c:CT * (c + 1)]).then_inc(stored, 16)
            sp.wait_ge(stored, 16 * NC)

        def moe_pool(pool, own, split_w1, split_w2):
            g = nc.gpsimd
            for e in range(NE - 2, -1, -1):
                split_w1(e)
                split_w2(e)
            pool.wait_ge(back_ready, 1)

            def gather(n):
                for c in range(NC):
                    for t in range(CT * c, CT * (c + 1)):
                        g.indirect_dma_start(gathered[:, n, t], None, returned, bass.IndirectOffsetOnAxis(ap=back_u[:, n, t:t + 1], axis=0)
                                             ).then_inc(gather_in[n][c], 16)

            for par in range(2):
                stores = pool.value_load(early[0:1, par:par + 1], min_val=16, max_val=16 * NTILE)
                wait_apart(pool, y_sent[par], stores)
            gather(0)
            for par in range(2):
                pool.wait_ge(y_sent[par], 16 * ((NTILE + 1 - par) // 2))
            gather(1)

        def moe_scalar(act):
            a = nc.scalar
            act.wait_ge(table_ready, 1)
            act.wait_ge(b1_in, 16)

            def x_hi(j, par):
                act.wait_ge(t_ps, j + 1)
                if not (isinstance(j, int) and j < 2):
                    act.wait_ge(hid_ps, (j - 1) * FC)
                a.activation(x16[:, par, :, HI], PS[:, 7 * par].rearrange("p (k n) -> p k n", k=KC), ACT.Copy).then_inc(x_hi_out, 1)

            def step(j, i, par):
                if not last_tile(j):
                    x_hi(j + 1, 1 - par)
                e = act.value_load(table[0:1, 0, bass.ds(j, 1)], min_val=0, max_val=NE - 1)

                def hi(half):
                    f = slice(FC // 2 * half, FC // 2 * (half + 1))
                    act.wait_ge(gel_out, j * FC + FC // 2 * (half + 1))
                    if not (isinstance(j, int) and j < 2):
                        act.wait_ge(y_ps, j - 1)
                    a.activation(hid16[:, par, f, HI], gel[:, f], ACT.Copy).then_inc(g_hi, 1)

                for f in range(FC):
                    if f % 2 == 0:
                        act.wait_ge(hid_ps, j * FC + (f + 2))
                    if f % (FC // 2) == 0 and not (isinstance(j, int) and j == 0):
                        act.wait_ge(g_lo, j * 2 + (f // (FC // 2) - 1))
                    a.activation(gel[:, f], PS[:, 1 + f // 2, RT * (f % 2):RT * (f % 2 + 1)], ACT.Gelu,
                                 bias=b1s[:, bass.ds(e, 1), f:f + 1].squeeze(1), scale=1 / WS).then_inc(gel_out, 1)
                    if f == FC // 2:
                        hi(0)
                hi(1)

            x_hi(0, 0)
            expert_tiles(act, step)

        def moe_vector(dve, own):
            v = nc.vector
            dve.wait_ge(total_ps, 1)
            dve.wait_ge(rows_ready, NC)
            total = PS[:, 5, 0:NE]
            own.mark(v.tensor_tensor(ends, total, rc[:, R_BASE:R_BASE + NE], ALU.add))
            bc8 = [P, NE, TPE]
            own.link(v.tensor_tensor(more, total.unsqueeze(2).to_broadcast(bc8), rc[:, R_TILE:R_TILE + TPE].unsqueeze(1).to_broadcast(bc8), ALU.is_gt))
            v.tensor_copy(pad_at, ends).then_inc(pad_ready, 1)
            dve.wait_ge(pad_ready, 1)
            own.link(v.tensor_reduce(tiles_of_e, more, AX.X, ALU.add))
            own.link(v.tensor_tensor(more, tiles_of_e.unsqueeze(1).to_broadcast([P, NE, NE]), later, ALU.mult))
            own.link(v.tensor_reduce(starts, more, AX.X, ALU.add))
            own.link(v.tensor_tensor(ends, starts, tiles_of_e, ALU.add))
            full = [P, NTILE, NE]
            j_f = rc[:, R_J:R_J + NTILE]
            j_bc, ends_bc = j_f.unsqueeze(2).to_broadcast(full), ends.unsqueeze(1).to_broadcast(full)
            own.link(v.tensor_tensor(past, ends_bc, j_bc, ALU.is_gt))
            own.link(v.tensor_reduce(expert_f, past, AX.X, ALU.add))
            own.mark(v.tensor_scalar(used, expert_f, 1.0, None, ALU.is_ge))
            own.link(v.tensor_scalar(expert_f, expert_f, 1.0, 0.0, ALU.subtract, ALU.max))
            own.mark(v.tensor_copy(table[:, 0], expert_f))
            own.mark(v.tensor_scalar(table[:, 2], expert_f, -1.0, float(NE), ALU.mult, ALU.add))
            own.link(v.tensor_tensor(past, ends_bc, j_bc, ALU.is_le))
            own.link(v.tensor_tensor(past, past, ends_bc, ALU.mult))
            own.link(v.tensor_reduce(first_f, past, AX.X, ALU.max))
            own.link(v.tensor_tensor(first_f, j_f, first_f, ALU.subtract))
            own.mark(v.tensor_scalar(first_f, first_f, float(RT), None, ALU.mult))
            own.link(v.tensor_scalar(expert_f, expert_f, float(REG), None, ALU.mult))
            own.link(v.tensor_tensor(first_f, first_f, expert_f, ALU.add))
            own.link(v.tensor_tensor(first_f, first_f, used, ALU.mult))
            v.tensor_copy(table[:, 1], first_f).then_inc(table_ready, 1)

            def x_lo(j, par):
                dve.wait_ge(x_hi_out, j + 1)
                v.tensor_tensor(x16[:, par, :, LO], PS[:, 7 * par].rearrange("p (k n) -> p k n", k=KC), x16[:, par, :, HI], ALU.subtract
                                ).then_inc(x_lo_out, 1)

            def y(j, i, par):
                dve.wait_ge(y_ps, j + 1)
                dve.wait_ge(b2_in[par], i * 16 + 16)
                if not (isinstance(j, int) and j < 2):
                    dve.wait_ge(y_sent[par], i * 16)
                v.scalar_tensor_tensor(yS[:, par], PS[:, 5 + par].rearrange("p (u d) -> p u d", u=2), 1 / WS,
                                       b2t[:, par].unsqueeze(1).to_broadcast([P, 2, D]), ALU.mult, ALU.add).then_inc(y_out, 1)

            def step(j, i, par):
                if not last_tile(j):
                    x_lo(j + 1, 1 - par)
                for half in range(2):
                    f = slice(FC // 2 * half, FC // 2 * (half + 1))
                    dve.wait_ge(g_hi, j * 2 + (half + 1))
                    v.tensor_tensor(hid16[:, par, f, LO], gel[:, f], hid16[:, par, f, HI], ALU.subtract).then_inc(g_lo, 1)
                if not (isinstance(j, int) and j == 0):
                    y(j - 1, i + (par - 1), 1 - par)

            x_lo(0, 0)
            full = [P, CT, NE, NE]
            takers = both.rearrange("p n t e -> p (n t e)").rearrange("p (t e j) -> p t e j", e=NE, j=NE)
            for c in range(NC):
                tiles = slice(CT * c, CT * (c + 1))
                own.link(v.tensor_tensor(takers, taken[:, tiles].unsqueeze(2).to_broadcast(full), later.unsqueeze(1).to_broadcast(full), ALU.mult))
                own.link(v.tensor_reduce(rank[:, tiles], takers, AX.X, ALU.add))
            own.link(v.scalar_tensor_tensor(rank, taken, -8.0, rank, ALU.mult, ALU.add))
            full = [P, NT, NE]
            own.mark(v.scalar_tensor_tensor(both[:, 0], rank, -8.0, gate, ALU.is_equal, ALU.mult))
            own.link(v.scalar_tensor_tensor(both[:, 1], rank, -7.0, gate, ALU.is_equal, ALU.mult))
            own.link(v.tensor_reduce(weight, both, AX.X, ALU.add))
            own.mark(v.memset(early_f[:, NTILE:], 0.0))
            own.link(v.tensor_scalar(early_f[:, 0:NTILE], j_f, starts[:, 0:1], 16.0, ALU.is_lt, ALU.mult))
            own.link(v.tensor_reduce(back_f[:, 0, 0:2], early_f.rearrange("p (i n) -> p n i", n=2), AX.X, ALU.add))
            own.link(v.tensor_copy(early, back_f[:, 0, 0:2]))
            own.link(v.scalar_tensor_tensor(starts, starts, float(RT), rc[:, R_BASE:R_BASE + NE], ALU.mult, ALU.subtract))
            own.link(v.tensor_tensor(row_of, row_of, starts.unsqueeze(1).to_broadcast(full), ALU.add))
            own.mark(v.scalar_tensor_tensor(both[:, 0], rank, -8.0, row_of, ALU.is_equal, ALU.mult))
            own.link(v.scalar_tensor_tensor(both[:, 1], rank, -7.0, row_of, ALU.is_equal, ALU.mult))
            own.link(v.tensor_reduce(back_f, both, AX.X, ALU.add))
            v.tensor_copy(back_u, back_f).then_inc(back_ready, 1)
            expert_tiles(dve, step)
            y(NTILE - 1, NTILE // 2, 0)
            for n in range(2):
                for c in range(NC):
                    dve.wait_ge(gather_in[n][c], CT * 16)
                    for t in range(CT * c, CT * (c + 1)):
                        ins = v.scalar_tensor_tensor(x_all[:, t], gathered[:, n, t], weight[:, n, t:t + 1], x_all[:, t], ALU.mult, ALU.add)
                    if n == 0:
                        done = own.mark(ins)
                    else:
                        ins.then_inc(added, 1)
                if n == 0:
                    dve.wait_ge(dve_step, done)

        def moe_tensor(pe):
            te = nc.tensor
            pe.wait_ge(table_ready, 1)

            def transposes(j, i, par):
                pe.wait_ge(xg_in[par], i * 16 + 16)
                for k in range(KC):
                    for u in range(2):
                        ins = te.transpose(PS[:, 7 * par, RT * k + P * u:RT * k + P * (u + 1)], xg[:, par, u, P * k:P * (k + 1)], ident)
                ins.then_inc(t_ps, 1)

            def weights(e, part, at_col, n):
                return experts[:, bass.ds(e, 1), at_col:at_col + n].rearrange("p e n -> p (e n)")

            def outputs(j, par):
                e = pe.value_load(table[0:1, 0, bass.ds(j, 1)], min_val=0, max_val=NE - 1)
                ready = pe.value_load(table[0:1, 2, bass.ds(j, 1)], min_val=1, max_val=NE)
                pe.wait_ge(g_lo, j * 2 + 2)
                pe.wait_ge(w2_ready, ready)
                if not (isinstance(j, int) and j < 2):
                    pe.wait_ge(y_out, j - 1)
                for u in range(2):
                    for m in range(3 * FC):
                        f, (a, b) = m // 3, PASSES[m % 3]
                        ins = te.matmul(PS[:, 5 + par, D * u:D * (u + 1)], hid16[:, par, f, a, P * u:P * (u + 1)],
                                        weights(e, b, W2_AT + (2 * f + b) * D, D), start=m == 0, stop=m == 3 * FC - 1)
                ins.then_inc(y_ps, 1)

            def step(j, i, par):
                if not last_tile(j):
                    transposes(j + 1, i + par, 1 - par)
                e = pe.value_load(table[0:1, 0, bass.ds(j, 1)], min_val=0, max_val=NE - 1)
                ready = pe.value_load(table[0:1, 2, bass.ds(j, 1)], min_val=1, max_val=NE)
                pe.wait_ge(x_lo_out, j + 1)
                pe.wait_ge(w1_ready, ready)
                for f in range(FC):
                    if f % 2 == 0 and not (isinstance(j, int) and j == 0):
                        pe.wait_ge(gel_out, j * FC + (f + 2 - FC))
                    for m in range(3 * KC):
                        k, (a, b) = m // 3, PASSES[m % 3]
                        ins = te.matmul(PS[:, 1 + f // 2, RT * (f % 2):RT * (f % 2 + 1)], weights(e, a, (2 * k + a) * FF + P * f, P),
                                        x16[:, par, k, b], start=m == 0, stop=m == 3 * KC - 1)
                    ins.then_inc(hid_ps, 1)
                if not (isinstance(j, int) and j == 0):
                    outputs(j - 1, 1 - par)

            transposes(0, 0, 0)
            expert_tiles(pe, step)
            outputs(NTILE - 1, (NTILE - 1) % 2)

        def after_attention_sync(sp):
            sp.dma_start(returned.rearrange("(p n) d -> p (n d)", p=P).rearrange("p (n d) -> p n d", d=P), ident.unsqueeze(1).to_broadcast([P, 4 * NTILE, P])
                         ).then_inc(rows_filled, 16)
            sp.wait_ge(rows_filled, 16)
            sp.wait_ge(lg_out, NC)
            sp.dma_start(b1s, b1).then_inc(b1_in, 16)
            moe_sync(sp)

        def after_attention_pool(pool, own):
            moe_pool(pool, own, *rwkv_pool(pool, own))

        def after_attention_scalar(act):
            rwkv_scalar(act)
            moe_scalar(act)

        def after_attention_vector(dve, own):
            dve.wait_ge(xbo_ready, 8)
            dve.wait_ge(ao_split, NT)
            dve.wait_ge(rc_in, 16)
            rwkv_vector(dve, own)
            moe_vector(dve, own)

        def after_attention_tensor(pe):
            rwkv_tensor(pe)
            moe_tensor(pe)

        block = stack.enter_context(nc.Block())

        def attention_tiles(eng, step, trail=None, per=0):
            step(0, True, False)
            with eng.Fori(1, NT - 1) as t:
                if trail:
                    trail.enter(t - 1, per)
                step(t, False, False)
            if trail:
                trail.leave(NT - 2)
            step(NT - 1, False, True)

        UNITS = [(b, j) for b in range(BT) for j in range(2)]

        @block.sync
        def _(sp):
            x_v = x.rearrange("(t p) d -> p t d", p=P)
            ctx_v = ctx_t.rearrange("(k p) n -> p k n", p=P)
            w_v = w_all.rearrange("(k p) n -> p k n", p=P)
            sp.dma_start(vec, vecs).then_inc(vecs_in, 16)
            sp.dma_start(stage[:, :, 0:NWA], w_v[:, :, 0:NWA]).then_inc(wa_in, 16)
            for c in range(NC):
                sp.dma_start(x_all[:, CT * c:CT * (c + 1), :], x_v[:, CT * c:CT * (c + 1), :]).then_inc(x_in[c], 16)
                if c == 0:
                    sp.dma_start(clf, ctx_last).then_inc(cl_in, 16)
            for b in range(BT):
                sp.dma_start(ctxf[:, b], ctx_v[:, :, SK * b:SK * (b + 1)]).then_inc(ctx_in[b], 16)
            sp.dma_start(rc, route_consts.partition_broadcast(P)).then_inc(rc_in, 16)
            sp.dma_start(bo_bc, bo.partition_broadcast(P)).then_inc(bo_in, 16)
            sp.dma_start(stage[:, :, NWA:NW], w_v[:, :, NWA:NW]).then_inc(wb_in, 16)
            sp.dma_start(stage2, w_value2.rearrange("(k p) n -> p k n", p=P)).then_inc(wb_in, 16)
            with sp.Fori(1, NT) as t:
                for b in range(BT):
                    sp.wait_ge(ctx_split, t * BT + (b - BT + 1))
                    sp.dma_start(ctxf[:, b], ctx_v[:, :, bass.ds(t * (BT * SK) + SK * b, SK)]).then_inc(ctx_in[b], 16)
            after_attention_sync(sp)

        @block.gpsimd
        def _(pool):
            g = nc.gpsimd
            own = Trail(pool, pool_step, wait_apart)

            def keep(m, base, cm, pattern, op=ALU.is_ge, fill=0.0):
                own.link(g.affine_select(out=m, in_=m, compare_op=op, fill=fill, base=base, channel_multiplier=cm, pattern=pattern))

            g.memset(neghalf, -0.5).then_inc(consts, 1)
            own.mark(g.memset(ident, 0.0))
            own.mark(g.memset(mask8, 1.0))
            own.mark(g.memset(maskO, 1.0))
            own.mark(g.memset(maskV, 1.0))
            own.mark(g.memset(sel16, 0.0))
            own.link(g.memset(plast, 0.0))
            keep(ident, 0, 1, [[-1, P]], ALU.not_equal, 1.0)
            keep(mask8, 0, 1, [[-HD, 8]])
            keep(mask8, HD - 1, -1, [[HD, 8]])
            keep(maskO, 0, 1, [[-SQ, 4], [0, HD]])
            keep(maskO, SQ - 1, -1, [[SQ, 4], [0, HD]])
            keep(maskV, 0, 1, [[0, 2], [-4, 2], [0, 64]])
            keep(maskV, 3, -1, [[0, 2], [4, 2], [0, 64]])
            for h in range(4):
                keep(sel16, -SQ * h, 1, [[-1, SQ]], ALU.not_equal, 1.0)
            own.mark(g.memset(ones16, 1.0))
            own.link(g.memset(earlier, 1.0))
            g.affine_select(out=earlier, in_=earlier, compare_op=ALU.is_gt, fill=0.0, base=0, channel_multiplier=-1, pattern=[[1, P]]
                            ).then_inc(consts, 1)

            pool.wait_ge(cl_in, 16)
            for k in range(KC):
                own.link(g.tensor_scalar(cl16[:, k, HI], clf[:, k], 1.0, 0.0, ALU.mult, ALU.add))
                g.tensor_tensor(cl16[:, k, LO], clf[:, k], cl16[:, k, HI], ALU.subtract).then_inc(cl_split, 1)

            def split_ctx_hi(slot, par, arrivals):
                wait_apart(pool, ctx_in[slot], arrivals * 16)
                own.link(g.tensor_scalar(ctx16[:, par, :, HI, 0:SK], ctxf[:, slot], 1.0, 0.0, ALU.mult, ALU.add))

            def split_ctx_lo(slot, par):
                g.tensor_tensor(ctx16[:, par, :, LO, 0:SK], ctxf[:, slot], ctx16[:, par, :, HI, 0:SK], ALU.subtract).then_inc(ctx_split, 1)

            split_ctx_hi(0, 0, 1)
            split_ctx_lo(0, 0)
            pool.wait_ge(var_ready, 1)
            g.tensor_tensor(rs0, ve0, neghalf, ALU.pow).then_inc(rstd_ready, 1)
            split_ctx_hi(1, 1, 1)
            split_ctx_lo(1, 1)
            for i in range(NT // 2):
                pool.wait_ge(vl_evac, i + 1)
                own.link(g.tensor_scalar(vlast[:8, 2 * i:2 * i + 2, HI], vlf[:8, i % 2], 1.0, 0.0, ALU.mult, ALU.add))
                g.tensor_tensor(vlast[:8, 2 * i:2 * i + 2, LO], vlf[:8, i % 2], vlast[:8, 2 * i:2 * i + 2, HI], ALU.subtract).then_inc(vl_split, 1)

            def plast_of(U, b, j):
                wait_apart(pool, probs, U + 1)
                g.tensor_copy(plast[:, j, b, :, b], Pr[:, j, :, SK - 1]).then_inc(p_last, 1)

            def split_o(Up, b, j):
                wait_apart(pool, o_masked, Up + 1)
                s = (2 * b + j) % 4
                own.link(g.tensor_scalar(Om16[:, s, HI], Om[:, j], 1.0, 0.0, ALU.mult, ALU.add))
                g.tensor_tensor(Om16[:, s, LO], Om[:, j], Om16[:, s, HI], ALU.subtract).then_inc(o_split, 1)

            def step(t, first, last):
                for n, (b, j) in enumerate(UNITS):
                    U = t * 8 + n
                    ahead = b + 2
                    load = j == 0 and not (last and ahead >= BT)
                    if load:
                        wait_apart(pool, v_ps, t * 8 + (2 * b + 2))
                        split_ctx_hi(ahead % BT, b % 2, t + (1 + ahead // BT))
                    if not (first and n < 2):
                        split_o(U - 2, *UNITS[n - 2])
                    plast_of(U, b, j)
                    if load:
                        split_ctx_lo(ahead % BT, b % 2)
                    if first:
                        rest_of_weights(n)

            def rest_of_weights(n):
                if n == 0:
                    pool.wait_ge(wb_in, 32)
                    pool.wait_ge(bo_in, 16)
                    pool.wait_ge(xn_ready, NC)
                cols = slice(NWA + (NW - NWA) // 8 * n, NWA + (NW - NWA) // 8 * (n + 1))
                own.mark(g.tensor_scalar(stage[:, :, cols], stage[:, :, cols], WS, 0.0, ALU.mult, ALU.add))
                own.link(g.tensor_scalar(stage2[:, n], stage2[:, n], WS, 0.0, ALU.mult, ALU.add))
                own.mark(g.tensor_scalar(W16[:, :, HI, cols], stage[:, :, cols], 1.0, 0.0, ALU.mult, ALU.add))
                own.link(g.tensor_scalar(WV2[:, n, HI], stage2[:, n], 1.0, 0.0, ALU.mult, ALU.add))
                g.tensor_tensor(W16[:, :, LO, cols], stage[:, :, cols], W16[:, :, HI, cols], ALU.subtract)
                g.tensor_tensor(WV2[:, n, LO], stage2[:, n], WV2[:, n, HI], ALU.subtract).then_inc(wb_ready, 1)
                rows = x_all[:, 2 * n:2 * n + 2]
                g.tensor_tensor(rows, rows, bo_bc.unsqueeze(1).to_broadcast([P, 2, D]), ALU.add).then_inc(xbo_ready, 1)

            attention_tiles(pool, step, own, 4 + 8)
            split_o(8 * NT - 2, BT - 1, 0)
            split_o(8 * NT - 1, BT - 1, 1)
            after_attention_pool(pool, own)

        @block.scalar
        def _(act):
            s = nc.scalar

            def x_hi(c):
                act.wait_ge(xt_ps, c + 1)
                for k in range(KC):
                    ins = s.activation(xT[:, c % 2, k, HI], PS[:, 2 * (c % 2) + k], ACT.Copy)
                ins.then_inc(xt_hi, 1)

            def q_parts(c):
                act.wait_ge(q_ps, c + 1)
                for j in range(KC):
                    ins = s.activation(qT[:, j, HI, CN * c:CN * (c + 1)], PS[:, 4 + 2 * (c % 2) + j], ACT.Identity,
                                       bias=vec64[:, BQ, j:j + 1])
                ins.then_inc(q_hi, 1)

            for c in range(NC + 1):
                if c < NC:
                    x_hi(c)
                if c > 0:
                    q_parts(c - 1)

            def kv_hi(n, bpar, b4, j):
                act.wait_ge(k_ps, n + 1)
                s.activation(Kt[:, bpar, j, HI, 0:SK], PS[:, 4, 0:SK], ACT.Identity, bias=vec64[:, BK, j:j + 1]).then_inc(k_hi, 1)
                act.wait_ge(v_ps, n + 1)
                s.activation(Vt[:, b4, j, HI], PS[:, 5, 0:D], ACT.Copy).then_inc(v_hi, 1)

            def pt_high(Up):
                act.wait_ge(pt_ps, Up + 1)
                s.activation(PT[:, HI], PS[:, 6], ACT.Copy).then_inc(pt_hi, 1)
                act.wait_ge(ptl_ps, Up + 1)
                s.activation(PTl[:8, HI], PS[:8, 7, P:2 * P], ACT.Copy).then_inc(ptl_hi, 1)

            def tile_out(t):
                act.wait_ge(selected, t * 8)
                s.activation(aoF, PS[:, 5, D:2 * D].rearrange("p (k n) -> p k n", k=KC), ACT.Copy, scale=1 / WS).then_inc(ao_evac, 1)

            for j in range(2):
                kv_hi(j, 0, 0, j)

            def step(t, first, last):
                for n, (b, j) in enumerate(UNITS):
                    U = t * 8 + n
                    if not (first and n == 0):
                        pt_high(U - 1)
                    act.wait_ge(negmax, U + 1)
                    for h in range(2):
                        ins = s.activation(Pr[:, j, h], PS[:, 2 * j + h, 0:SK], ACT.Exp, bias=nb[:, j, h:h + 1], scale=SM,
                                           accum_out=den[:, j, h:h + 1])
                    ins.then_inc(probs, 1)
                    if n == 2 and not first:
                        tile_out(t)
                    if not (last and b == BT - 1):
                        kv_hi(U + 2, (b + 1) % 2, (b + 1) % BT, j)

            attention_tiles(act, step)
            pt_high(8 * NT - 1)
            tile_out(NT)
            after_attention_scalar(act)

        @block.vector
        def _(dve):
            v = nc.vector
            own = Trail(dve, dve_step)
            dve.wait_ge(vecs_in, 16)
            own.mark(v.tensor_scalar(vec64, vec, WS, None, ALU.mult))
            dve.wait_ge(wa_in, 16)
            own.link(v.tensor_scalar(W16[:, :, HI, 0:NWA], stage[:, :, 0:NWA], WS, None, ALU.mult))
            v.scalar_tensor_tensor(W16[:, :, LO, 0:NWA], stage[:, :, 0:NWA], WS, W16[:, :, HI, 0:NWA],
                                   ALU.mult, ALU.subtract).then_inc(wa_ready, 1)
            for t in range(NT):
                if t % CT == 0:
                    dve.wait_ge(x_in[t // CT], 16)
                n = own.mark(v.bn_stats(st0[:, t], x_all[:, t]))
            dve.wait_ge(dve_step, n)
            for t in range(NT):
                n = own.mark(v.bn_aggr(mv0[:, t], st0[:, t]))
            dve.wait_ge(dve_step, n)
            v.tensor_scalar(ve0, mv0[:, :, 1], 1e-5, None, ALU.add).then_inc(var_ready, 1)

            def last_values(i):
                dve.wait_ge(vl_ps, i + 1)
                need(dve, vl_split, i - 1)
                v.tensor_tensor(vlf[:8, i % 2], PS[:8, i].rearrange("p (t n) -> p t n", t=2),
                                maskV8, ALU.mult).then_inc(vl_evac, 1)

            dve.wait_ge(rstd_ready, 1)
            maskV8 = maskV[:8].rearrange("p a b n -> p (a b n)").unsqueeze(1).to_broadcast([8, 2, D])
            for c in range(NC + 2):
                if c < NC:
                    need(dve, xt_ps, c - 1)
                    for i in range(CT):
                        t = CT * c + i
                        ins = v.tensor_scalar(xn[:, c % 2, i], x_all[:, t], mv0[:, t, 0:1], rs0[:, t:t + 1], ALU.subtract, ALU.mult)
                    ins.then_inc(xn_ready, 1)
                if c == 0:
                    for i in range(NT // 2):
                        last_values(i)
                if 0 < c <= NC:
                    dve.wait_ge(xt_hi, c)
                    for k in range(KC):
                        ins = v.tensor_tensor(xT[:, (c - 1) % 2, k, LO], PS[:, 2 * ((c - 1) % 2) + k], xT[:, (c - 1) % 2, k, HI], ALU.subtract)
                    ins.then_inc(xt_split, 1)
                if c > 1:
                    dve.wait_ge(q_hi, c - 1)
                    for j in range(KC):
                        cols = slice(CN * (c - 2), CN * (c - 1))
                        ins = v.scalar_tensor_tensor(qT[:, j, LO, cols], PS[:, 4 + 2 * (c % 2) + j], vec64[:, BQ, j:j + 1],
                                                     qT[:, j, HI, cols], ALU.add, ALU.subtract)
                    ins.then_inc(q_split, 1)

            def kv_lo(n, bpar, b4, j):
                dve.wait_ge(k_hi, n + 1)
                v.scalar_tensor_tensor(Kt[:, bpar, j, LO, 0:SK], PS[:, 4, 0:SK], vec64[:, BK, j:j + 1], Kt[:, bpar, j, HI, 0:SK],
                                       ALU.add, ALU.subtract).then_inc(k_split, 1)
                dve.wait_ge(v_hi, n + 1)
                v.tensor_tensor(Vt[:, b4, j, LO], PS[:, 5, 0:D], Vt[:, b4, j, HI], ALU.subtract).then_inc(v_split, 1)

            qT4 = qT.rearrange("p j c n -> p (j c) n")

            def spread_queries(pair, half, heads):
                src = qT4[:, :, bass.ds(pair * (2 * SQ), 2 * SQ)].rearrange("p c (b q) -> p c b q", b=2)
                for h in heads:
                    ins = v.tensor_scalar(Qbd[:, half, :, :, SQ * h:SQ * (h + 1)], src, mask8[:, h:h + 1], None, ALU.mult)
                if heads[-1] == 7:
                    ins.then_inc(qbd, 1)

            def last_values_now(tile, half):
                v.tensor_copy(vlc[:8, half].rearrange("p c n -> p (c n)"),
                              vlast[:8].rearrange("p t c n -> p t (c n)")[:, bass.ds(tile, 1)].squeeze(1) if not isinstance(tile, int)
                              else vlast[:8, tile].rearrange("p c n -> p (c n)")).then_inc(vl_now, 1)

            dve.wait_ge(q_split, NC)
            dve.wait_ge(vl_split, NT // 2)
            spread_queries(0, 0, range(8))
            last_values_now(0, 0)
            for j in range(2):
                kv_lo(j, 0, 0, j)

            def pt_low(Up, j):
                dve.wait_ge(pt_hi, Up + 1)
                v.tensor_tensor(PT[:, LO], PS[:, 6], PT[:, HI], ALU.subtract)
                dve.wait_ge(ptl_hi, Up + 1)
                v.tensor_tensor(PTl[:8, LO], PS[:8, 7, P:2 * P], PTl[:8, HI], ALU.subtract).then_inc(pt_split, 1)
                own.link(v.reciprocal(rec[:, j], den[:, j]))

            def mask_out(Up, j):
                dve.wait_ge(pv, Up + 1)
                for h in range(2):
                    ins = v.scalar_tensor_tensor(Om[:, j, 64 * h:64 * (h + 1)], PS[:, 7, 64 * h:64 * (h + 1)], rec[:, j, h:h + 1],
                                                 maskO.rearrange("p a b -> p (a b)"), ALU.mult, ALU.mult)
                ins.then_inc(o_masked, 1)

            def split_tile_out(t):
                dve.wait_ge(ao_evac, t)
                cols = bass.ds(t * P - P, P)
                for k in range(KC):
                    own.link(v.tensor_scalar(aoT[:, k, HI, cols], aoF[:, k], vec[:, BV, k:k + 1], None, ALU.add))
                    ins = v.scalar_tensor_tensor(aoT[:, k, LO, cols], aoF[:, k], vec[:, BV, k:k + 1], aoT[:, k, HI, cols],
                                                 ALU.add, ALU.subtract)
                ins.then_inc(ao_split, 1)

            def step(t, first, last):
                for n, (b, j) in enumerate(UNITS):
                    U = t * 8 + n
                    half = b // 2
                    if not (first and n < 2):
                        mask_out(U - 2, j)
                    dve.wait_ge(scores, U + 1)
                    own.link(v.tensor_reduce(nm[:, j], PS[:, 2 * j:2 * j + 2, 0:SK], AX.X, ALU.max, negate=True))
                    v.tensor_scalar(nb[:, j], nm[:, j], SM, PS_LN, ALU.mult, ALU.add).then_inc(negmax, 1)
                    if not (first and n == 0):
                        pt_low(U - 1, 1 - j)
                    if not (last and b == BT - 1):
                        kv_lo(U + 2, (b + 1) % 2, (b + 1) % BT, j)
                    if not (last and half == 1):
                        if n % 4 < 3:
                            spread_queries(t * 2 + (half + 1), 1 - half, (range(0, 3), range(3, 6), range(6, 8))[n % 4])
                        if n % 4 == 1:
                            need(dve, pv, t * 8 + 4 * half)
                            last_values_now(t + half, 1 - half)
                    if n == 3 and not first:
                        split_tile_out(t)

            attention_tiles(dve, step, own, 8 * 2 + 2)
            mask_out(8 * NT - 2, 0)
            pt_low(8 * NT - 1, 1)
            mask_out(8 * NT - 1, 1)
            split_tile_out(NT)
            after_attention_vector(dve, own)

        @block.tensor
        def _(pe):
            te = nc.tensor
            pe.wait_ge(cl_split, KC)
            pe.wait_ge(wa_ready, 1)
            for t in range(NT):
                n = 0
                for k in range(KC):
                    for a, b in PASSES:
                        ins = te.matmul(PS[:8, t // 2, D * (t % 2):D * (t % 2 + 1)], cl16[:, k, a, t], W16[:, k, b, WV:WV + D],
                                        start=n == 0, stop=n == 2 * len(PASSES) - 1)
                        n += 1
                if t % 2:
                    ins.then_inc(vl_ps, 1)
            pe.wait_ge(consts, 2)
            pe.wait_ge(vl_evac, NT // 2)
            for c in range(NC + 1):
                if c < NC:
                    pe.wait_ge(xn_ready, c + 1)
                    need(pe, xt_split, c - 1)
                    for k in range(KC):
                        for i in range(CT):
                            ins = te.transpose(PS[:, 2 * (c % 2) + k, P * i:P * (i + 1)], xn[:, c % 2, i, P * k:P * (k + 1)], ident)
                    ins.then_inc(xt_ps, 1)
                if c > 0:
                    pe.wait_ge(xt_split, c)
                    need(pe, q_split, c - 2)
                    for j in range(KC):
                        n = 0
                        for k in range(KC):
                            for a, b in PASSES:
                                ins = te.matmul(PS[:, 4 + 2 * ((c - 1) % 2) + j], W16[:, k, a, WQ + P * j:WQ + P * (j + 1)],
                                                xT[:, (c - 1) % 2, k, b], start=n == 0, stop=n == 5)
                                n += 1
                    ins.then_inc(q_ps, 1)

            def project_keys(n, par, j):
                need(pe, k_split, n)
                m = 0
                for k in range(KC):
                    for a, b in PASSES:
                        ins = te.matmul(PS[:, 4, 0:SK], W16[:, k, a, WK + P * j:WK + P * (j + 1)], ctx16[:, par, k, b, 0:SK],
                                        start=m == 0, stop=m == 5)
                        m += 1
                ins.then_inc(k_ps, 1)

            def project_values(n, par, j):
                need(pe, v_split, n)
                m = 0
                for k in range(KC):
                    for a, b in PASSES:
                        ins = te.matmul(PS[:, 5, 0:D], ctx16[:, par, k, a, P * j:P * (j + 1)], W16[:, k, b, WV:WV + D],
                                        start=m == 0, stop=m == 5)
                        m += 1
                ins.then_inc(v_ps, 1)

            pe.wait_ge(q_split, NC)
            pe.wait_ge(ctx_split, 1)
            for j in range(2):
                project_keys(j, 0, j)
                project_values(j, 0, j)

            def select_heads(Up, b, j):
                pe.wait_ge(o_split, Up + 1)
                for m, a in enumerate((HI, LO)):
                    ins = te.matmul(PS[:, 5, D + P * j + SQ * b:D + P * j + SQ * (b + 1)], Om16[:, (2 * b + j) % 4, a], sel16,
                                    start=m == 0, stop=m == 1)
                ins.then_inc(selected, 1)

            def transpose_probs(Up, j):
                pe.wait_ge(probs, Up + 1)
                for h in range(2):
                    for k in range(2):
                        ins = te.transpose(PS[:, 6, P * (2 * h + k):P * (2 * h + k + 1)], Pr[:, j, h, P * k:P * (k + 1)], ident)
                ins.then_inc(pt_ps, 1)

            def transpose_last(Up, b, j):
                pe.wait_ge(p_last, Up + 1)
                need(pe, o_masked, Up)
                te.transpose(PS[:8, 7, P:2 * P], plast[:, j, b].rearrange("p g c -> p (g c)"), ident).then_inc(ptl_ps, 1)

            def outputs(Up, b, j, values):
                pe.wait_ge(v_split, values)
                pe.wait_ge(pt_split, Up + 1)
                half = b // 2
                for h in range(2):
                    cols = slice(P * j + 64 * h, P * j + 64 * (h + 1))
                    terms = [(PT[:, a, P * (2 * h + k):P * (2 * h + k + 1)], Vt[:, b, k, c, cols]) for k in range(2) for a, c in PASSES]
                    terms += [(PTl[:8, a], vlc[:8, half, c, cols]) for a, c in PASSES]
                    for m, (lhs, rhs) in enumerate(terms):
                        ins = te.matmul(PS[:, 7, 64 * h:64 * (h + 1)], lhs, rhs, start=m == 0, stop=m == len(terms) - 1)
                ins.then_inc(pv, 1)

            def step(t, first, last):
                for n, (b, j) in enumerate(UNITS):
                    U = t * 8 + n
                    half = b // 2
                    if not (first and n < 2):
                        outputs(U - 2, *UNITS[n - 2], t * 8 + n // 2 * 2)
                    if n % 4 == 0:
                        pe.wait_ge(qbd, t * 2 + (half + 1))
                        pe.wait_ge(vl_now, t * 2 + (half + 1))
                    pe.wait_ge(k_split, U + 1)
                    need(pe, probs, U - 1)
                    for h in range(2):
                        for m, (a, c) in enumerate(PASSES):
                            ins = te.matmul(PS[:, 2 * j + h, 0:SK], Qbd[:, half, 2 * j + a, b % 2, P * h:P * (h + 1)],
                                            Kt[:, b % 2, j, c, 0:SK], start=m == 0, stop=m == 2)
                    ins.then_inc(scores, 1)
                    if not (first and n == 0):
                        transpose_probs(U - 1, UNITS[n - 1][1])
                    more = not (last and b == BT - 1)
                    if n == 2 and not first:
                        pe.wait_ge(v_split, U + 2)
                        select_heads(U - 3, *UNITS[n - 3])
                    if more:
                        if n % 2 == 0:
                            pe.wait_ge(ctx_split, t * 4 + (b + 2))
                        project_keys(U + 2, (b + 1) % 2, j)
                    if not (first and n == 0):
                        transpose_last(U - 1, *UNITS[n - 1])
                    if n == 2 and not first:
                        pe.wait_ge(ao_evac, t)
                    elif not (first and n < 3):
                        if more:
                            pe.wait_ge(v_split, U + 2)
                        select_heads(U - 3, *UNITS[n - 3])
                    if more:
                        project_values(U + 2, (b + 1) % 2, j)

            attention_tiles(pe, step)
            U = 8 * NT
            outputs(U - 2, BT - 1, 0, U)
            transpose_probs(U - 1, 1)
            transpose_last(U - 1, BT - 1, 1)
            select_heads(U - 3, BT - 2, 1)
            select_heads(U - 2, BT - 1, 0)
            outputs(U - 1, BT - 1, 1, U)
            select_heads(U - 1, BT - 1, 1)
            after_attention_tensor(pe)


def kernel(**inputs):
    import numpy as np
    import concourse.bacc as bacc
    from concourse.bass_utils import run_bass_kernel_spmd

    def a(name):
        return np.asarray(inputs[name])

    def layer(name):
        return a("L0_" + name)

    ctx = a("ctx_1024")
    last = ctx[:, SK - 1, :].reshape(NT, BT, KC, P).transpose(3, 2, 0, 1)
    w_all = np.concatenate(
        [layer("xattn_" + n).T for n in ("Wq", "Wk", "Wv", "Wo")]
        + [layer("attn_" + n) for n in ("W_key", "W_value", "W_recept", "W_out", "W_recept2", "W_key2")]
        + [layer("ffn_w_gate").T], axis=1)
    vecs = np.stack([layer(n) for n in (
        "xattn_bq", "xattn_bk", "xattn_bv", "attn_ln1_w", "attn_ln2_w", "attn_time_decay", "attn_time_first",
        "attn_time_mix_k", "attn_time_mix_v", "attn_time_mix_r", "attn_time_mix_k2", "attn_time_mix_r2")])
    e = np.arange(NE)
    route_consts = np.concatenate([e * REG, np.arange(TPE) * RT, (e[:, None] > e[None, :]).ravel(), np.arange(NTILE)]).astype(np.float32)
    host = {
        "x": a("x").reshape(TOK, D),
        "ctx_t": ctx.reshape(NB * SK, D).T,
        "ctx_last": np.concatenate([last, last], axis=3),
        "w_all": w_all,
        "w_value2": layer("attn_W_value2"),
        "vecs": vecs.reshape(NV, KC, P).transpose(2, 0, 1),
        "bo": layer("xattn_bo"),
        "route_consts": route_consts,
        "w1": layer("ffn_W1"),
        "b1": layer("ffn_b1").reshape(NE, FC, P).transpose(2, 0, 1),
        "w2": layer("ffn_W2"),
        "b2": layer("ffn_b2"),
    }
    nc = bacc.Bacc("TRN2", target_bir_lowering=False, num_devices=1)
    arrays, args = {}, []
    for name, value in host.items():
        value = np.ascontiguousarray(value)
        arrays[f"in_{name}"] = value
        args.append(nc.dram_tensor(f"in_{name}", value.shape, mybir.dt.from_np(value.dtype), kind="ExternalInput").ap())
    args.append(nc.dram_tensor("out", (TOK, D), F32, kind="ExternalOutput").ap())
    perceiver_layer(nc, *args)
    r = run_bass_kernel_spmd(nc, [arrays], core_ids=[0])
    return r.results[0]["out"].reshape(NB, SQ, D)
```
